# Optimizing a Trainium2 kernel written in Bass

```python
import numpy as np
import jax
import jax.numpy as jnp

def _softmax(x, axis=-1):
    return jax.nn.softmax(x, axis=axis)

def _gelu(x):
    return jax.nn.gelu(x, approximate=True)

def _silu(x):
    return jax.nn.silu(x)

def _sigmoid(x):
    return jax.nn.sigmoid(x)

def _layernorm(x, axis=-1, eps=1e-05):
    m = jnp.mean(x, axis=axis, keepdims=True)
    v = jnp.var(x, axis=axis, keepdims=True)
    return (x - m) / jnp.sqrt(v + eps)

def _scatter_add(tgt, idx, src, axis=0):
    return tgt.at[idx].add(src)

def _segment_sum(src, seg, n):
    return jax.ops.segment_sum(src, seg, n)
kernel_name = 'mk_vit_tower_postln_d1_tok_img256_r4_67c5bc'

def setup_inputs(seed: int=0):
    np.random.seed(seed)
    _w = jnp.asarray

    def _rec_inputs():
        import jax
        import jax.numpy as jnp
        _rk = jax.random.key(seed)
        x = -0.000125008 + 0.999885 * jax.random.normal(jax.random.fold_in(_rk, 1), (64, 64, 64, 64), jnp.float32)
        return x
    x = _rec_inputs()

    def _L0_tok_setup():
        import jax, jax.numpy as jnp
        import numpy as np
        B, C, H, W = (32, 64, 64, 64)
        STRIDE, HEADS = (4, 8)

        def _ln(x, w, b):
            mu = x.mean(-1, keepdims=True)
            var = ((x - mu) ** 2).mean(-1, keepdims=True)
            return (x - mu) * jax.lax.rsqrt(var + 1e-05) * w + b
        key = jax.random.key(seed)
        ks = jax.random.split(key, 4)
        return {'features': jax.random.normal(ks[0], (B, C, H, W), dtype=jnp.float32), 'ln_q_w': jnp.ones((C,), jnp.float32), 'ln_q_b': jnp.zeros((C,), jnp.float32), 'Wq': jax.random.normal(ks[1], (C, C), dtype=jnp.float32) * 0.02, 'ln_kv_w': jnp.ones((C,), jnp.float32), 'ln_kv_b': jnp.zeros((C,), jnp.float32), 'Wkv': jax.random.normal(ks[2], (2 * C, C), dtype=jnp.float32) * 0.02, 'proj_w': jax.random.normal(ks[3], (C, C), dtype=jnp.float32) * 0.02, 'proj_b': jnp.zeros((C,), jnp.float32), 'conv_stride': STRIDE, 'num_heads': HEADS}
    _L0_tok_all = _L0_tok_setup()
    _L0_tok_in = {k: v for k, v in _L0_tok_all.items() if k in ('ln_q_w', 'ln_q_b', 'Wq', 'ln_kv_w', 'ln_kv_b', 'Wkv', 'proj_w', 'proj_b')}
    del _L0_tok_all

    def _L0_attn_setup():
        import jax, jax.numpy as jnp
        import numpy as np
        from jax import lax

        def _solve_im(u, a, W_B, b_B, dt):
            s = 1.0 / (1.0 + dt * dt * a)
            Bu = jnp.einsum('bnq,pq->bnp', u, W_B) + b_B
            f_x = dt * s * Bu
            f_z = dt * dt * s * Bu
            dsa = dt * s * a
            ds = dt * s

            def step(carry, f):
                x, z = carry
                fx, fz = f
                x_new = s * x - dsa * z + fx
                z_new = ds * x + s * z + fz
                return ((x_new, z_new), z_new)
            Bsz, _, q = u.shape
            init = (jnp.zeros((Bsz, q), u.dtype), jnp.zeros((Bsz, q), u.dtype))
            _, z_t = lax.scan(step, init, (jnp.moveaxis(f_x, 1, 0), jnp.moveaxis(f_z, 1, 0)))
            return jnp.moveaxis(z_t, 0, 1)

        def _reference_tuple_inner(u, a, W_B, b_B, W_C, b_C, W_D, b_D):
            N = u.shape[1]
            dt = 1.0 / N
            y = _solve_im(u, a, W_B, b_B, dt)
            x = jnp.einsum('bnq,pq->bnp', y, W_C) + b_C + (jnp.einsum('bnq,pq->bnp', u, W_D) + b_D)
            x = jax.nn.gelu(x, approximate=False)
            out = x * jax.nn.sigmoid(x) + u
            return (out, y)
        key = jax.random.key(seed)
        ks = jax.random.split(key, 8)
        B, N, q = (16, 1024, 64)
        sc = float(1.0 / np.sqrt(q))
        return {'u': jax.random.normal(ks[0], (B, N, q), jnp.float32), 'a': jax.random.normal(ks[1], (q,), jnp.float32), 'W_B': jax.random.normal(ks[2], (q, q), jnp.float32) * sc, 'b_B': jax.random.normal(ks[3], (q,), jnp.float32) * sc, 'W_C': jax.random.normal(ks[4], (q, q), jnp.float32) * sc, 'b_C': jax.random.normal(ks[5], (q,), jnp.float32) * sc, 'W_D': jax.random.normal(ks[6], (q, q), jnp.float32) * sc, 'b_D': jax.random.normal(ks[7], (q,), jnp.float32) * sc}
    _L0_attn_all = _L0_attn_setup()
    _L0_attn_in = {k: v for k, v in _L0_attn_all.items() if k in ('a', 'W_B', 'b_B', 'W_C', 'b_C', 'W_D', 'b_D')}
    del _L0_attn_all

    def _L0_ffn_setup():
        import jax, jax.numpy as jnp
        import numpy as np
        B, A = (1024, 8)
        IN, OUT = (64, 64)
        SH1, SH2 = (64, 128)
        EH1, EH2 = (128, 64)
        E, TOPK = (4, 2)

        def _shared_mlp(x, W1, b1, W2, b2, W3, b3):
            h = jax.nn.relu(x @ W1 + b1)
            h = jax.nn.relu(h @ W2 + b2)
            return h @ W3 + b3

        def _experts_mlp(x, eW1, eb1, eW2, eb2, eW3, eb3):
            h = jax.nn.relu(jnp.einsum('baf,efh->ebah', x, eW1) + eb1[:, None, None, :])
            h = jax.nn.relu(jnp.einsum('ebah,ehg->ebag', h, eW2) + eb2[:, None, None, :])
            o = jnp.einsum('ebag,ego->ebao', h, eW3) + eb3[:, None, None, :]
            return jnp.moveaxis(o, 0, -1)
        key = jax.random.key(seed)
        ks = jax.random.split(key, 16)
        s = 0.05
        return {'x': jax.random.normal(ks[0], (B, A, IN), jnp.float32), 'sW1': jax.random.normal(ks[1], (IN, SH1), jnp.float32) * s, 'sb1': jnp.zeros((SH1,), jnp.float32), 'sW2': jax.random.normal(ks[2], (SH1, SH2), jnp.float32) * s, 'sb2': jnp.zeros((SH2,), jnp.float32), 'sW3': jax.random.normal(ks[3], (SH2, OUT), jnp.float32) * s, 'sb3': jnp.zeros((OUT,), jnp.float32), 'eW1': jax.random.normal(ks[4], (E, IN, EH1), jnp.float32) * s, 'eb1': jnp.zeros((E, EH1), jnp.float32), 'eW2': jax.random.normal(ks[5], (E, EH1, EH2), jnp.float32) * s, 'eb2': jnp.zeros((E, EH2), jnp.float32), 'eW3': jax.random.normal(ks[6], (E, EH2, OUT), jnp.float32) * s, 'eb3': jnp.zeros((E, OUT), jnp.float32), 'gW': jax.random.normal(ks[7], (IN, E), jnp.float32) * s, 'gb': jnp.zeros((E,), jnp.float32)}
    _L0_ffn_all = _L0_ffn_setup()
    _L0_ffn_in = {k: v for k, v in _L0_ffn_all.items() if k in ('sW1', 'sb1', 'sW2', 'sb2', 'sW3', 'sb3', 'eW1', 'eb1', 'eW2', 'eb2', 'eW3', 'eb3', 'gW', 'gb')}
    del _L0_ffn_all
    return {'x': x, 'L0_tok_ln_q_w': _L0_tok_in['ln_q_w'], 'L0_tok_ln_q_b': _L0_tok_in['ln_q_b'], 'L0_tok_Wq': _L0_tok_in['Wq'], 'L0_tok_ln_kv_w': _L0_tok_in['ln_kv_w'], 'L0_tok_ln_kv_b': _L0_tok_in['ln_kv_b'], 'L0_tok_Wkv': _L0_tok_in['Wkv'], 'L0_tok_proj_w': _L0_tok_in['proj_w'], 'L0_tok_proj_b': _L0_tok_in['proj_b'], 'L0_attn_a': _L0_attn_in['a'], 'L0_attn_W_B': _L0_attn_in['W_B'], 'L0_attn_b_B': _L0_attn_in['b_B'], 'L0_attn_W_C': _L0_attn_in['W_C'], 'L0_attn_b_C': _L0_attn_in['b_C'], 'L0_attn_W_D': _L0_attn_in['W_D'], 'L0_attn_b_D': _L0_attn_in['b_D'], 'L0_ffn_sW1': _L0_ffn_in['sW1'], 'L0_ffn_sb1': _L0_ffn_in['sb1'], 'L0_ffn_sW2': _L0_ffn_in['sW2'], 'L0_ffn_sb2': _L0_ffn_in['sb2'], 'L0_ffn_sW3': _L0_ffn_in['sW3'], 'L0_ffn_sb3': _L0_ffn_in['sb3'], 'L0_ffn_eW1': _L0_ffn_in['eW1'], 'L0_ffn_eb1': _L0_ffn_in['eb1'], 'L0_ffn_eW2': _L0_ffn_in['eW2'], 'L0_ffn_eb2': _L0_ffn_in['eb2'], 'L0_ffn_eW3': _L0_ffn_in['eW3'], 'L0_ffn_eb3': _L0_ffn_in['eb3'], 'L0_ffn_gW': _L0_ffn_in['gW'], 'L0_ffn_gb': _L0_ffn_in['gb']}

def reference(x, L0_tok_ln_q_w, L0_tok_ln_q_b, L0_tok_Wq, L0_tok_ln_kv_w, L0_tok_ln_kv_b, L0_tok_Wkv, L0_tok_proj_w, L0_tok_proj_b, L0_attn_a, L0_attn_W_B, L0_attn_b_B, L0_attn_W_C, L0_attn_b_C, L0_attn_W_D, L0_attn_b_D, L0_ffn_sW1, L0_ffn_sb1, L0_ffn_sW2, L0_ffn_sb2, L0_ffn_sW3, L0_ffn_sb3, L0_ffn_eW1, L0_ffn_eb1, L0_ffn_eW2, L0_ffn_eb2, L0_ffn_eW3, L0_ffn_eb3, L0_ffn_gW, L0_ffn_gb):
    import jax
    import jax.numpy as jnp

    def _L0_tok_ref(features, ln_q_w, ln_q_b, Wq, ln_kv_w, ln_kv_b, Wkv, proj_w, proj_b, conv_stride, num_heads):
        import jax, jax.numpy as jnp
        import numpy as np
        B, C, H, W = (32, 64, 64, 64)
        STRIDE, HEADS = (4, 8)

        def _ln(x, w, b):
            mu = x.mean(-1, keepdims=True)
            var = ((x - mu) ** 2).mean(-1, keepdims=True)
            return (x - mu) * jax.lax.rsqrt(var + 1e-05) * w + b
        s = conv_stride
        b, c, hh, ww = features.shape
        h, w = (hh // s, ww // s)
        hw, n, d = (h * w, s * s, c // num_heads)
        scale = c ** (-0.5)
        x = features.reshape(b, c, h, s, w, s)
        reduce_feats = x.mean((3, 5)).reshape(b, c, hw).transpose(0, 2, 1)
        unf = x.transpose(0, 1, 2, 4, 3, 5).reshape(b, c, hw, n).transpose(0, 2, 3, 1)
        q = _ln(reduce_feats, ln_q_w, ln_q_b) @ Wq.T
        q = q.reshape(b, hw, num_heads, d).transpose(0, 2, 1, 3)
        kv = _ln(unf, ln_kv_w, ln_kv_b) @ Wkv.T
        kv = kv.reshape(b, hw, n, 2, num_heads, d).transpose(3, 0, 4, 1, 2, 5)
        k, v = (kv[0], kv[1])
        attn = jax.nn.softmax(jnp.einsum('bhpd,bhpnd->bhpn', q * scale, k), axis=-1)
        aggre = jnp.einsum('bhpn,bhpnd->bhpd', attn, v)
        aggre = aggre.transpose(0, 2, 1, 3).reshape(b, hw, c)
        return reduce_feats + aggre @ proj_w.T + proj_b

    def _L0_attn_ref(u, a, W_B, b_B, W_C, b_C, W_D, b_D):
        import jax, jax.numpy as jnp
        import numpy as np
        from jax import lax

        def _solve_im(u, a, W_B, b_B, dt):
            s = 1.0 / (1.0 + dt * dt * a)
            Bu = jnp.einsum('bnq,pq->bnp', u, W_B) + b_B
            f_x = dt * s * Bu
            f_z = dt * dt * s * Bu
            dsa = dt * s * a
            ds = dt * s

            def step(carry, f):
                x, z = carry
                fx, fz = f
                x_new = s * x - dsa * z + fx
                z_new = ds * x + s * z + fz
                return ((x_new, z_new), z_new)
            Bsz, _, q = u.shape
            init = (jnp.zeros((Bsz, q), u.dtype), jnp.zeros((Bsz, q), u.dtype))
            _, z_t = lax.scan(step, init, (jnp.moveaxis(f_x, 1, 0), jnp.moveaxis(f_z, 1, 0)))
            return jnp.moveaxis(z_t, 0, 1)

        def _reference_tuple_inner(u, a, W_B, b_B, W_C, b_C, W_D, b_D):
            N = u.shape[1]
            dt = 1.0 / N
            y = _solve_im(u, a, W_B, b_B, dt)
            x = jnp.einsum('bnq,pq->bnp', y, W_C) + b_C + (jnp.einsum('bnq,pq->bnp', u, W_D) + b_D)
            x = jax.nn.gelu(x, approximate=False)
            out = x * jax.nn.sigmoid(x) + u
            return (out, y)
        return _reference_tuple_inner(u, a, W_B, b_B, W_C, b_C, W_D, b_D)[0]

    def _L0_ffn_ref(x, sW1, sb1, sW2, sb2, sW3, sb3, eW1, eb1, eW2, eb2, eW3, eb3, gW, gb):
        import jax, jax.numpy as jnp
        import numpy as np
        B, A = (1024, 8)
        IN, OUT = (64, 64)
        SH1, SH2 = (64, 128)
        EH1, EH2 = (128, 64)
        E, TOPK = (4, 2)

        def _shared_mlp(x, W1, b1, W2, b2, W3, b3):
            h = jax.nn.relu(x @ W1 + b1)
            h = jax.nn.relu(h @ W2 + b2)
            return h @ W3 + b3

        def _experts_mlp(x, eW1, eb1, eW2, eb2, eW3, eb3):
            h = jax.nn.relu(jnp.einsum('baf,efh->ebah', x, eW1) + eb1[:, None, None, :])
            h = jax.nn.relu(jnp.einsum('ebah,ehg->ebag', h, eW2) + eb2[:, None, None, :])
            o = jnp.einsum('ebag,ego->ebao', h, eW3) + eb3[:, None, None, :]
            return jnp.moveaxis(o, 0, -1)
        all_out = _experts_mlp(x, eW1, eb1, eW2, eb2, eW3, eb3)
        shared = _shared_mlp(x, sW1, sb1, sW2, sb2, sW3, sb3)
        gates = jax.nn.softmax(x @ gW + gb, axis=-1)
        topv, topi = jax.lax.top_k(gates, TOPK)
        topw = jax.nn.softmax(topv, axis=-1)
        sel = jnp.take_along_axis(all_out, topi[:, :, None, :], axis=-1)
        gated = jnp.sum(sel * topw[:, :, None, :], axis=-1)
        return shared + gated
    h = _L0_tok_ref(x, L0_tok_ln_q_w, L0_tok_ln_q_b, L0_tok_Wq, L0_tok_ln_kv_w, L0_tok_ln_kv_b, L0_tok_Wkv, L0_tok_proj_w, L0_tok_proj_b, 4, 8)
    h = _layernorm(h + _L0_attn_ref(h, L0_attn_a, L0_attn_W_B, L0_attn_b_B, L0_attn_W_C, L0_attn_b_C, L0_attn_W_D, L0_attn_b_D), axis=-1)
    h = _layernorm(h + _L0_ffn_ref(h, L0_ffn_sW1, L0_ffn_sb1, L0_ffn_sW2, L0_ffn_sb2, L0_ffn_sW3, L0_ffn_sb3, L0_ffn_eW1, L0_ffn_eb1, L0_ffn_eW2, L0_ffn_eb2, L0_ffn_eW3, L0_ffn_eb3, L0_ffn_gW, L0_ffn_gb), axis=-1)
    return h

_drawn_inputs = setup_inputs


def setup_inputs(seed=0):
    import zlib

    import numpy as np

    out = dict(_drawn_inputs(seed))
    spreads = {'L0_tok_ln_q_w': (1.0, 0.6),
     'L0_tok_ln_q_b': (0.0, 2.0),
     'L0_tok_ln_kv_w': (1.0, 0.6),
     'L0_tok_ln_kv_b': (0.0, 0.661),
     'L0_tok_proj_b': (0.0, 0.1),
     'L0_ffn_sb1': (0.0, 0.722),
     'L0_ffn_sb2': (0.0, 0.1),
     'L0_ffn_sb3': (0.0, 0.1),
     'L0_ffn_eb1': (0.0, 0.8),
     'L0_ffn_eb2': (0.0, 0.545),
     'L0_ffn_eb3': (0.0, 0.1),
     'L0_ffn_gb': (0.0, 0.306)}
    factors = {'L0_tok_Wq': 45.527, 'L0_attn_a': 8.0, 'L0_attn_W_B': 3.605, 'L0_ffn_eW1': 2.771}
    for name, (base, spread) in spreads.items():
        noise = np.random.default_rng([zlib.crc32(name.encode()), seed]).standard_normal(out[name].shape)
        drawn = base * np.exp(spread * noise) if base else spread * noise
        out[name] = jnp.asarray(drawn.astype(out[name].dtype))
    for name, factor in factors.items():
        out[name] = (out[name] * factor).astype(out[name].dtype)
    return out
```

```python
from contextlib import ExitStack

import numpy as np

import concourse.bass as bass
from concourse import mybir

ALU = mybir.AluOpType
ACT = mybir.ActivationFunctionType
AX = mybir.AxisListType
F32 = mybir.dt.float32

P = 128
B, C, H, W = 64, 64, 64, 64
S = 4
N_PIX = S * S
HEADS = 8
D = C // HEADS
HW = (H // S) * (W // S)
PAIRS = B // 2
UNITS = PAIRS
PX = H * W // 2
PT = HW // 2
CH = 512
NJ = PX // CH
E = 4
NF = 4
DT = 1.0 / HW
L = 16
NCK = HW // L
EPS = 1e-5
ITERS = PAIRS // 2
G = 2 * HW // P

K_ONES, K_CEN, K_EYE, K_IND, K_AVG, K_PATCH, K_UP, K_EPS, K_END = 0, 128, 256, 384, 448, 512, 576, 592, 593
V_LNQW, V_LNQB, V_LNKW, V_LNKB, V_PROJB, V_A, V_BB, V_BC, V_BD, N_VEC = range(10)
T_RAW, T_PROJ, T_VEC, T_END = 0, 384, 512, 512 + N_VEC
R_SSM, R_EW1, R_SW1, R_SW2, R_SW3, R_EW2, R_EW3, R_GW, R_B3, R_GB, R_EB, R_END = (
    0, 384, 1408, 1536, 1792, 1856, 2112, 2368, 2376, 2888, 2892, 2900)
SV_A, SV_S, SV_NM, SV_F, SV_FB, SV_CD = range(6)
N_COEFS = 11 + 3 * L
N_CHUNKS = PAIRS * HW // CH
STORE = 4 * 16
N_RES = 8


def shape_constants():
    k = np.zeros((P, K_END), np.float32)
    blocks = np.kron(np.eye(2), np.ones((C, C))) / C
    k[:, K_ONES:K_CEN] = blocks
    k[:, K_CEN:K_EYE] = np.eye(P) - blocks
    k[:, K_EYE:K_IND] = np.eye(P)
    for b in range(2):
        for p in range(P):
            k[p, K_IND + 32 * b + 16 * b + p // D] = 1.0
            at = K_AVG + 32 * b + 16 * b + HEADS * (p // C)
            k[p, at:at + HEADS] = 1.0 / C
    for p in range(P):
        for b in range(2):
            k[p, K_PATCH + 32 * b + 16 * b + (p % W) // S] = 1.0
    for e in range(E):
        for f in range(E):
            k[:, K_UP + E * e + f] = float(f >= e)
    k[:, K_EPS] = EPS
    return k


def build(nc, t):
    ctx = ExitStack()
    with ctx:
        def sb(name, *shape):
            return ctx.enter_context(nc.sbuf_tensor("sb_" + name, list(shape), F32))

        def sem(name):
            return ctx.enter_context(nc.semaphore(name))

        banks = [ctx.enter_context(nc.psum_tensor(f"bank{i}", [P, CH], F32)) for i in range(8)]

        arena = sb("arena", P, NF * 2 * PX)
        hT = sb("hT", P, PAIRS * HW)
        const = sb("const", P, K_END)
        xsq = sb("xsq", P, 2, PX)
        prodk = sb("prodk", P, 2, PX)
        prodv = sb("prodv", P, 8, CH)
        rows2 = sb("rows2", P, 2, 1024)
        sum16 = sb("sum16", P, 2 * PT)
        means = sb("means", P, NF, 2, 2 * PT)
        qbuf = sb("qbuf", P, 2, 2, PT, S)
        qstat = sb("qstat", P, 2 * PT)
        qrstd = sb("qrstd", P, 2 * PT)
        qraw = sb("qraw", P, 2 * PT)
        vstat = sb("vstat", P, CH)
        rstd = sb("rstd", P, CH)
        score = sb("score", P, CH)
        wgt = sb("wgt", P, CH)
        smx = sb("smx", P, 32)
        smxs = sb("smxs", P, 32 * S)
        ssm = sb("ssm", P, 32)
        srz = sb("srz", P, 32 * S)
        cbias = sb("cbias", P, 32 * S)
        wT = sb("wT", P, 2, CH)
        aggr_t = sb("aggr_t", P, 2 * PT)
        aggr = sb("aggr", P, 2 * PT)
        tok_w = sb("tok_w", P, T_END)
        scaled = prodk[:, 0, 0:3 * P]
        wqkv = sb("wqkv", P, 3, P)
        bqkv = sb("bqkv", P, 4)
        indbk = sb("indbk", P, 64)
        rest_w = sb("rest_w", P, R_END)
        sv = sb("sv", P, 6)
        cz = sb("cz", P, L + 1, 2)
        cv = sb("cv", P, L + 1, 2)
        cacc = sb("cacc", P, 2)
        wmT = sb("wmT", P, 2, P)

        raw = tok_w[:, T_RAW:T_PROJ]
        projw = tok_w[:, T_PROJ:T_VEC]
        vecs = tok_w[:, T_VEC:T_END]
        wssm = rest_w[:, R_SSM:R_EW1].rearrange("p (a n) -> p a n", a=3)
        ew1 = rest_w[:, R_EW1:R_SW1].rearrange("p (m e n) -> p m e n", m=2, e=E)
        sw1 = rest_w[:, R_SW1:R_SW2]
        sw2 = rest_w[:, R_SW2:R_SW3].rearrange("p (m n) -> p m n", m=2)
        sw3 = rest_w[:, R_SW3:R_EW2]
        ew2 = rest_w[:, R_EW2:R_EW3].rearrange("p (e n) -> p e n", e=E)
        ew3 = rest_w[:, R_EW3:R_GW].rearrange("p (q n) -> p q n", q=2)
        gw = rest_w[:, R_GW:R_B3]
        b3 = rest_w[:, R_B3:R_GB].rearrange("p (g n) -> p g n", g=G)
        gbias = rest_w[:, R_GB:R_EB]
        ebias = rest_w[:, R_EB:R_END]

        def vec(n):
            return vecs[:, n:n + 1]

        ones64 = const[:, K_ONES:K_CEN]
        centre = const[:, K_CEN:K_EYE]
        eye = const[:, K_EYE:K_IND]
        eps = const[:, K_EPS:K_EPS + 1]

        def ind(b):
            return const[:, K_IND + 32 * b:K_IND + 32 * b + 32]

        def patch(b):
            return const[:, K_PATCH + 32 * b:K_PATCH + 32 * b + 32]

        def avg(b):
            return const[:, K_AVG + 32 * b:K_AVG + 32 * b + 32]

        x = arena[:, :].rearrange("p (m b n) -> p m b n", m=NF, b=2)

        const_in = sem("const_in")
        tok_in = sem("tok_in")
        rest_in = sem("rest_in")
        coefs = sem("coefs")
        ones_row = sem("ones_row")
        x_in = [sem(f"x_in{m}") for m in range(NF)]
        weights_scaled = sem("weights_scaled")
        setup_mm = sem("setup_mm")
        weights_centred = sem("weights_centred")
        biases_ready = sem("biases_ready")
        row_pairs_added = sem("row_pairs_added")
        rows_added = sem("rows_added")
        half_rows_added = sem("half_rows_added")
        patch_summed = sem("patch_summed")
        mean_taken = sem("mean_taken")
        q_moments_mm = sem("q_moments_mm")
        q_raw_mm = sem("q_raw_mm")
        q_mean_squared = sem("q_mean_squared")
        q_variance_ready = sem("q_variance_ready")
        q_log_ready = sem("q_log_ready")
        q_rstd_ready = sem("q_rstd_ready")
        q_scaled = sem("q_scaled")
        q_ready = sem("q_ready")
        pixels_squared = sem("pixels_squared")
        pixel_mean_mm = sem("pixel_mean_mm")
        pixel_square_mm = sem("pixel_square_mm")
        mean_squared = sem("mean_squared")
        variance_ready = sem("variance_ready")
        log_ready = sem("log_ready")
        rstd_ready = sem("rstd_ready")
        bias_term_mm = sem("bias_term_mm")
        bias_term_ready = sem("bias_term_ready")
        keys_mm = sem("keys_mm")
        keys_times_q = sem("keys_times_q")
        scores_mm = sem("scores_mm")
        scores_scaled = sem("scores_scaled")
        scores_biased = sem("scores_biased")
        score_max_ready = sem("score_max_ready")
        score_max_spread = sem("score_max_spread")
        scores_shifted = sem("scores_shifted")
        scores_exp = sem("scores_exp")
        exp_summed = sem("exp_summed")
        sum_inverted = sem("sum_inverted")
        inverse_sum_ready = sem("inverse_sum_ready")
        weights_raw = sem("weights_raw")
        weights_ready = sem("weights_ready")
        weights_turned = sem("weights_turned")
        weights_copied = sem("weights_copied")
        values_mm = sem("values_mm")
        values_weighted = sem("values_weighted")
        aggregate_mm = sem("aggregate_mm")
        aggregate_copied = sem("aggregate_copied")
        aggregate_turned = sem("aggregate_turned")
        aggregate_ready = sem("aggregate_ready")
        projected_mm = sem("projected_mm")
        tokens_ready = sem("tokens_ready")
        drive_mm = sem("drive_mm")
        force_ready = sem("force_ready")
        scan_step = sem("scan_step")
        carry_step = sem("carry_step")
        chunk_fixed = sem("chunk_fixed")
        mixed_mm = sem("mixed_mm")
        gelu_ready = sem("gelu_ready")
        silu_ready = sem("silu_ready")
        residual_ready = sem("residual_ready")
        centred_mm = sem("centred_mm")
        centred_squared = sem("centred_squared")
        norm_variance_mm = sem("norm_variance_mm")
        norm_log_ready = sem("norm_log_ready")
        norm_rstd_ready = sem("norm_rstd_ready")
        normed_ready = sem("normed_ready")
        logits_mm = sem("logits_mm")
        logits_biased = sem("logits_biased")
        logits_max = sem("logits_max")
        logits_shifted = sem("logits_shifted")
        logits_exp = sem("logits_exp")
        logits_sum = sem("logits_sum")
        logits_inverse = sem("logits_inverse")
        gates_ready = sem("gates_ready")
        gates_compared = sem("gates_compared")
        ties_found = sem("ties_found")
        ties_counted = sem("ties_counted")
        wins_ready = sem("wins_ready")
        rank_ready = sem("rank_ready")
        gate_max = sem("gate_max")
        gates_shifted = sem("gates_shifted")
        gates_exp = sem("gates_exp")
        picked = sem("picked")
        picked_sum = sem("picked_sum")
        picked_inverse = sem("picked_inverse")
        routing_ready = sem("routing_ready")
        routing_turned = sem("routing_turned")
        routing_copied = sem("routing_copied")
        hidden_mm = sem("hidden_mm")
        hidden_ready = sem("hidden_ready")
        experts_mm = sem("experts_mm")
        experts_weighted = sem("experts_weighted")
        half_summed = sem("half_summed")
        gated_summed = sem("gated_summed")
        base_done = sem("base_done")
        sum_ready = sem("sum_ready")
        sum_added = sem("sum_added")
        mean_ready = sem("mean_ready")
        out_centred = sem("out_centred")
        out_squared = sem("out_squared")
        out_square_sum = sem("out_square_sum")
        out_log_ready = sem("out_log_ready")
        out_rstd_ready = sem("out_rstd_ready")
        out_ready = sem("out_ready")
        stored = [sem(f"stored{i}") for i in range(2)]

        def count(value):
            return max(value, 0) if isinstance(value, int) else value

        def pipeline(eng, step, total):
            lead, tail = NF, NF
            for n in range(lead):
                step(n, n % NF)
            with eng.Fori(1, (total - tail) // NF) as k:
                for m in range(NF):
                    step(k * NF + m, m)
            for n in range(total - tail, total):
                step(n, n % NF)

        ring = banks[0:3]
        bank_s, bank_sq, bank_mu, bank_ag, bank_t = banks[3:8]
        RING_K, RING_P, RING_V = 1, 9, 10

        mix = arena[:, :]
        pos = [0]

        def cut(n):
            a = mix[:, pos[0]:pos[0] + n]
            pos[0] += n
            return a

        h2 = cut(2 * CH).rearrange("p (i n) -> p i n", i=2)
        sq3 = cut(CH)
        ln3 = cut(CH)
        h1s = cut(CH)
        h1e = cut(8 * CH).rearrange("p (m e n) -> p m e n", m=2, e=E)
        h2s = cut(2 * CH).rearrange("p (m n) -> p m n", m=2)
        h2e = cut(4 * CH).rearrange("p (m q n) -> p m q n", m=2, q=2)
        eprod = cut(2 * CH).rearrange("p (r n) -> p r n", r=2)
        esum2 = cut(CH).rearrange("p (r m e c) -> p r m e c", r=2, m=2, e=2)
        gsum = cut(CH)
        ysb = cut(CH)
        ycen = cut(CH)
        ysq = cut(CH)
        out_t = cut(2 * CH).rearrange("p (i a n) -> p i a n", i=2, a=2)
        lg = cut(32)
        lgx = cut(32)
        gat = cut(32)
        pick = cut(32)
        wmoe = cut(32)
        l8 = cut(8 * 8).rearrange("p (a n) -> p a n", a=8)
        y8 = cut(8 * 4).rearrange("p (a n) -> p a n", a=4)
        beat = cut(P)
        tie = cut(P)
        assert pos[0] <= NF * 2 * PX
        force = arena[:, 0:PAIRS * HW]
        z = arena[:, PAIRS * HW:2 * PAIRS * HW]
        vel = xsq[:, 0, 0:CH]
        acc = xsq[:, 0, CH:2 * CH]
        zin = xsq[:, 0, 2 * CH:3 * CH]
        vin = xsq[:, 0, 3 * CH:4 * CH]
        ctmp = xsq[:, 1, 0:2 * PAIRS]

        def chunk(a, n):
            return a.rearrange("p (n k) -> p n k", k=CH)[:, n, :]

        def tokens_of(g):
            return slice((g // 2) * HW + g % 2, (g // 2 + 1) * HW, 2)

        bank_cen, bank_var, bank_base = banks[3], banks[4], banks[5]
        bank_o = banks[6:8]

        def mixture(eng, step):
            for i in range(2):
                step(i, i)
            with eng.Fori(1, ITERS // 2 - 1) as k:
                for p in range(2):
                    step(2 * k + p, p)
            for i in range(ITERS - 2, ITERS):
                step(i, i % 2)

        def by_chunk(eng, step, lead=2):
            for n in range(lead):
                step(n, n % 2)
            with eng.Fori(lead // 2, N_CHUNKS // 2) as k:
                for r in range(2):
                    step(2 * k + r, r)

        block = ctx.enter_context(nc.Block())


        @block.sync
        def _(sp):
            def load(u, m):
                sp.wait_ge(values_mm, count((u - NF) * 8 + 8))
                half = m % 2
                for b in range(2):
                    src = t["x"][(u - half) + b]
                    sp.dma_start(x[:, m, b, :], src[:, half * PX:(half + 1) * PX]).then_inc(x_in[m], 16)

            sp.dma_start(tok_w[:, :], t["tok_w"]).then_inc(tok_in, 16)
            load(0, 0)
            sp.dma_start(const[:, :], t["const"]).then_inc(const_in, 16)
            for u in range(1, NF):
                load(u, u)
            sp.dma_start(rest_w[:, :], t["rest_w"]).then_inc(rest_in, 16)
            with sp.Fori(1, UNITS // NF) as k:
                for m in range(NF):
                    load(k * NF + m, m)

            def store(i, p):
                sp.wait_ge(out_ready, i + 1)
                for a in range(2):
                    for m in range(2):
                        sp.dma_start(t["out"][2 * i + a, m].rearrange("(k f) c -> k f c", f=2),
                                     out_t[:, p, a].rearrange("p (f m c) -> p f m c", f=2, m=2)[:, :, m]
                                     ).then_inc(stored[p], 16)

            with sp.Fori(0, ITERS // 2) as k:
                for p in range(2):
                    store(2 * k + p, p)
            for p in range(2):
                sp.wait_ge(stored[p], STORE * (ITERS // 2))

        @block.gpsimd
        def _(pool):
            def patch_sums(u, m):
                pool.wait_ge(x_in[m], (u - m) * 8 + 32)
                rows = x[:, m, :, :].rearrange("p b (h s n) -> p (b h) s n", s=S, n=W)
                out = [rows2[:, i, :].rearrange("p (h n) -> p h n", n=W) for i in range(2)]
                pool.wait_ge(patch_summed, u)
                for i in range(2):
                    pool.tensor_tensor(out[i], rows[:, :, 2 * i], rows[:, :, 2 * i + 1], ALU.add).then_inc(row_pairs_added, 1)
                pool.wait_ge(row_pairs_added, 2 * u + 2)
                pool.tensor_tensor(rows2[:, 0, :], rows2[:, 0, :], rows2[:, 1, :], ALU.add).then_inc(rows_added, 1)
                pool.wait_ge(rows_added, u + 1)
                four = rows2[:, 0, :].rearrange("p (n t) -> p n t", t=S)
                two = rows2[:, 1, 0:2 * 2 * PT].rearrange("p (n t) -> p n t", t=2)
                pool.tensor_tensor(two, four[:, :, 0:2], four[:, :, 2:4], ALU.add).then_inc(half_rows_added, 1)
                pool.wait_ge(half_rows_added, u + 1)
                pool.wait_ge(mean_taken, 2 * u)
                pool.tensor_tensor(sum16[:, :], two[:, :, 0], two[:, :, 1], ALU.add).then_inc(patch_summed, 1)

            def softmax(u):
                sc = score[:, :].rearrange("p (h s n) -> p h s n", h=2, s=S)
                wg = wgt[:, :].rearrange("p (h s n) -> p h s n", h=2, s=S)

                def spread(a):
                    return a[:, :].rearrange("p (h n) -> p h n", h=2)[:, :, None, :].to_broadcast([P, 2, S, W])

                pool.wait_ge(scores_scaled, u + 1)
                pool.wait_ge(bias_term_ready, u + 1)
                pool.tensor_tensor(sc, sc, spread(cbias), ALU.add).then_inc(scores_biased, 1)
                pool.wait_ge(score_max_spread, u + 1)
                pool.tensor_tensor(sc, sc, spread(smxs), ALU.subtract).then_inc(scores_shifted, 1)
                pool.wait_ge(scores_exp, u + 1)
                pool.wait_ge(weights_turned, u)
                pool.tensor_tensor(wgt[:, :], score[:, :], rstd[:, :], ALU.mult).then_inc(weights_raw, 1)
                pool.wait_ge(weights_raw, u + 1)
                pool.wait_ge(inverse_sum_ready, u + 1)
                pool.tensor_tensor(wg, wg, spread(srz), ALU.mult).then_inc(weights_ready, 1)

            patch_sums(0, 0)
            patch_sums(1, 1)
            softmax(0)

            def step(n, m):
                if not isinstance(n, int) or n + 2 < UNITS:
                    patch_sums(n + 2, (m + 2) % NF)
                if not isinstance(n, int) or n + 1 < UNITS:
                    softmax(n + 1)

            pipeline(pool, step, UNITS)

            def combine(i):
                for g in range(G):
                    pool.wait_ge(experts_weighted, G * i + g + 1)
                    pool.wait_ge(gated_summed, count(G * i + g - 1))
                    pr = eprod[:, g % 2, :].rearrange("p (m e c) -> p m e c", m=2, e=E)
                    half = esum2[:, g % 2]
                    pool.tensor_tensor(half, pr[:, :, 0:2], pr[:, :, 2:4], ALU.add).then_inc(half_summed, 1)
                    pool.wait_ge(half_summed, G * i + g + 1)
                    if g == 0:
                        pool.wait_ge(sum_ready, i)
                    pool.tensor_tensor(gsum[:, g * P:(g + 1) * P].rearrange("p (m c) -> p m c", m=2),
                                       half[:, :, 0], half[:, :, 1], ALU.add).then_inc(gated_summed, 1)

            def rows(a):
                return a.rearrange("p (n c) -> p n c", c=C)

            def finish(i, p):
                pool.wait_ge(mean_ready, i + 1)
                pool.tensor_tensor(rows(ycen), rows(ysb), y8[:, 1, :][:, :, None].to_broadcast([P, 8, C]),
                                   ALU.subtract).then_inc(out_centred, 1)
                pool.wait_ge(out_rstd_ready, i + 1)
                pool.wait_ge(stored[p], count((i - p) * (STORE // 2)))
                pool.tensor_tensor(out_t[:, p].rearrange("p a (n c) -> p (a n) c", c=C), rows(ycen),
                                   y8[:, 3, :][:, :, None].to_broadcast([P, 8, C]),
                                   ALU.mult).then_inc(out_ready, 1)

            def mstep(i, p):
                if not isinstance(i, int) or i >= 1:
                    finish(i - 1, (p + 1) % 2)
                combine(i)

            mixture(pool, mstep)
            finish(ITERS - 1, (ITERS - 1) % 2)

        @block.scalar
        def _(act):
            act.preload_act_table_set("natural_log_exp_and_others")
            act.wait_ge(setup_mm, 1)
            act.activation(wqkv[:, :, :].rearrange("p a n -> p (a n)"), banks[0][:, 0:3 * P], ACT.Copy).then_inc(weights_centred, 1)

            def take_means(u, m):
                act.wait_ge(patch_summed, u + 1)
                act.activation(means[:, m, 0, :], sum16[:, :], ACT.Copy, scale=1.0 / N_PIX).then_inc(mean_taken, 1)
                act.activation(means[:, m, 1, :], sum16[:, :], ACT.Square, scale=1.0 / N_PIX).then_inc(mean_taken, 1)

            def q_rstd(u):
                act.wait_ge(q_moments_mm, u + 1)
                act.wait_ge(q_log_ready, u)
                act.activation(qstat[:, :], bank_sq[:, 0:2 * PT], ACT.Square).then_inc(q_mean_squared, 1)
                act.wait_ge(q_variance_ready, u + 1)
                act.activation(qstat[:, :], qstat[:, :], ACT.Ln, bias=eps).then_inc(q_log_ready, 1)
                act.wait_ge(q_log_ready, u + 1)
                act.wait_ge(q_scaled, u)
                act.activation(qrstd[:, :], qstat[:, :], ACT.Exp, scale=-0.5).then_inc(q_rstd_ready, 1)

            def query(u, m):
                act.wait_ge(q_scaled, u + 1)
                act.wait_ge(bias_term_mm, count(u - 1))
                act.wait_ge(keys_times_q, count(8 * u - 8))
                act.activation(qbuf[:, m % 2].rearrange("p b n t -> p (b n) t"),
                               qraw[:, :, None].to_broadcast([P, 2 * PT, S]), ACT.Identity,
                               scale=float(C) ** -0.5, bias=bqkv[:, 0:1]).then_inc(q_ready, 1)

            def squares(u, m, b):
                if b == 0:
                    act.wait_ge(x_in[m], (u - m) * 8 + 32)
                    act.wait_ge(pixel_square_mm, u)
                act.activation(xsq[:, b, :], x[:, m, b, :], ACT.Square).then_inc(pixels_squared, 1)

            def pixel_mean(u):
                act.wait_ge(pixel_mean_mm, u + 1)
                act.wait_ge(rstd_ready, u)
                act.activation(vstat[:, :], bank_mu[:, :], ACT.Square).then_inc(mean_squared, 1)

            def score_bias(u):
                act.wait_ge(bias_term_mm, u + 1)
                act.wait_ge(scores_biased, u)
                act.activation(cbias[:, :].rearrange("p (n t) -> p n t", t=S),
                               ring[0][:, 0:32][:, :, None].to_broadcast([P, 32, S]), ACT.Copy).then_inc(bias_term_ready, 1)

            def pixel_rstd(u):
                act.wait_ge(variance_ready, u + 1)
                act.activation(vstat[:, :], vstat[:, :], ACT.Ln, bias=eps).then_inc(log_ready, 1)
                act.wait_ge(log_ready, u + 1)
                act.wait_ge(weights_raw, u)
                act.activation(rstd[:, :], vstat[:, :], ACT.Exp, scale=-0.5).then_inc(rstd_ready, 1)

            def expo(u):
                act.wait_ge(scores_shifted, u + 1)
                act.activation(score[:, :], score[:, :], ACT.Exp).then_inc(scores_exp, 1)

            def copy_w(u, m):
                act.wait_ge(weights_turned, u + 1)
                act.wait_ge(values_weighted, count(8 * u - 8))
                act.activation(wT[:, m % 2, :], bank_t[:, :], ACT.Copy).then_inc(weights_copied, 1)

            def copy_agg(u):
                act.wait_ge(aggregate_mm, 2 * u + 2)
                act.wait_ge(aggregate_turned, u)
                act.activation(aggr_t[:, :], bank_ag[:, 0:2 * PT], ACT.Copy).then_inc(aggregate_copied, 1)

            def copy_turned(u):
                act.wait_ge(aggregate_turned, u + 1)
                act.wait_ge(projected_mm, u)
                act.activation(aggr[:, :], bank_ag[:, 2 * PT:4 * PT], ACT.Copy).then_inc(aggregate_ready, 1)

            act.wait_ge(const_in, 16)
            squares(0, 0, 0)
            squares(0, 0, 1)
            take_means(0, 0)
            q_rstd(0)
            act.wait_ge(biases_ready, 2)
            query(0, 0)
            pixel_mean(0)
            score_bias(0)
            pixel_rstd(0)
            squares(1, 1, 0)
            squares(1, 1, 1)
            take_means(1, 1)
            q_rstd(1)
            query(1, 1)
            expo(0)
            pixel_mean(1)

            def step(n, m):
                nxt = not isinstance(n, int) or n + 1 < UNITS
                nxt2 = not isinstance(n, int) or n + 2 < UNITS
                prev = not isinstance(n, int) or n >= 1
                if nxt:
                    score_bias(n + 1)
                if prev:
                    copy_agg(n - 1)
                    copy_turned(n - 1)
                if nxt:
                    pixel_rstd(n + 1)
                if nxt2:
                    squares(n + 2, (m + 2) % NF, 0)
                copy_w(n, m)
                if nxt2:
                    squares(n + 2, (m + 2) % NF, 1)
                    take_means(n + 2, (m + 2) % NF)
                    q_rstd(n + 2)
                    query(n + 2, m)
                if nxt:
                    expo(n + 1)
                if nxt2:
                    pixel_mean(n + 2)

            pipeline(act, step, UNITS)
            copy_agg(UNITS - 1)
            copy_turned(UNITS - 1)

            def forcing(n, r):
                act.wait_ge(drive_mm, n + 1)
                act.activation(chunk(force, n), banks[r][:, :], ACT.Identity,
                               scale=sv[:, SV_F:SV_F + 1], bias=sv[:, SV_FB:SV_FB + 1]).then_inc(force_ready, 1)

            act.wait_ge(coefs, N_COEFS)
            by_chunk(act, forcing)
            act.preload_act_table(ACT.Gelu)
            def gelu(n, r):
                act.wait_ge(mixed_mm, n + 1)
                act.activation(chunk(force, n), banks[r][:, :], ACT.Gelu,
                               bias=sv[:, SV_CD:SV_CD + 1]).then_inc(gelu_ready, 1)

            by_chunk(act, gelu)
            act.preload_act_table(ACT.Silu)
            for n in range(N_RES):
                act.wait_ge(gelu_ready, (n + 1) * N_CHUNKS // N_RES)
                a = force[:, n * PX // 2:(n + 1) * PX // 2]
                act.activation(a, a, ACT.Silu).then_inc(silu_ready, 1)
            act.preload_act_table_set("natural_log_exp_and_others")

            def norm_sq(i):
                act.wait_ge(centred_mm, i + 1)
                act.wait_ge(norm_variance_mm, i)
                act.activation(sq3, bank_cen[:, :], ACT.Square).then_inc(centred_squared, 1)

            def norm_rstd(i):
                act.wait_ge(norm_variance_mm, i + 1)
                act.wait_ge(normed_ready, i)
                act.activation(ln3, bank_var[:, :], ACT.Ln, bias=eps).then_inc(norm_log_ready, 1)
                act.wait_ge(norm_log_ready, i + 1)
                act.activation(ln3, ln3, ACT.Exp, scale=-0.5).then_inc(norm_rstd_ready, 1)

            def relu(i, k):
                act.wait_ge(hidden_mm, 15 * i + k + 1)
                if k == 0:
                    dst, bias = h1s, ebias[:, 6:7]
                elif k < 9:
                    dst, bias = h1e[:, (k - 1) // E, (k - 1) % E], ebias[:, (k - 1) % E:(k - 1) % E + 1]
                elif k < 11:
                    dst, bias = h2s[:, k - 9], ebias[:, 7:8]
                else:
                    dst, bias = h2e[:, (k - 11) // 2, (k - 11) % 2], ebias[:, 4 + (k - 11) % 2:5 + (k - 11) % 2]
                act.activation(dst, ring[k % 3][:, :], ACT.Relu, bias=bias).then_inc(hidden_ready, 1)

            def out_sq(i):
                act.wait_ge(out_centred, i + 1)
                act.wait_ge(out_square_sum, i)
                act.activation(ysq, ycen, ACT.Square).then_inc(out_squared, 1)

            def out_rstd(i):
                act.wait_ge(out_square_sum, i + 1)
                act.activation(y8[:, 2, :], y8[:, 2, :], ACT.Ln, scale=1.0 / C, bias=eps).then_inc(out_log_ready, 1)
                act.wait_ge(out_log_ready, i + 1)
                act.wait_ge(out_ready, i)
                act.activation(y8[:, 3, :], y8[:, 2, :], ACT.Exp, scale=-0.5).then_inc(out_rstd_ready, 1)

            norm_sq(0)
            norm_rstd(0)

            def mstep(i, p):
                nxt = not isinstance(i, int) or i + 1 < ITERS
                prev = not isinstance(i, int) or i >= 1
                relu(i, 0)
                if nxt:
                    norm_sq(i + 1)
                relu(i, 1)
                act.wait_ge(logits_shifted, i + 1)
                act.activation(lgx, lgx, ACT.Exp).then_inc(logits_exp, 1)
                for k in range(2, 5):
                    relu(i, k)
                act.wait_ge(gates_shifted, i + 1)
                act.activation(pick, pick, ACT.Exp).then_inc(gates_exp, 1)
                for k in range(5, 8):
                    relu(i, k)
                if prev:
                    out_sq(i - 1)
                relu(i, 8)
                if nxt:
                    norm_rstd(i + 1)
                relu(i, 9)
                relu(i, 10)
                if prev:
                    out_rstd(i - 1)
                for k in range(11, 15):
                    relu(i, k)
                act.wait_ge(routing_turned, i + 1)
                act.activation(wmT[0:32, p, :], bank_var[0:32, 0:P], ACT.Copy).then_inc(routing_copied, 1)

            mixture(act, mstep)
            out_sq(ITERS - 1)
            out_rstd(ITERS - 1)

        @block.tensor
        def _(pe):
            pe.wait_ge(const_in, 16)
            pe.wait_ge(weights_scaled, 3)
            pe.matmul(banks[0][:, 0:3 * P], centre, scaled[:, :],
                      start=True, stop=True).then_inc(setup_mm, 1)
            pe.matmul(banks[1][:, 0:1], raw[:, 0 * P:1 * P], vec(V_LNQB), start=True, stop=True)
            pe.matmul(banks[1][:, 1:2], raw[:, 1 * P:2 * P], vec(V_LNKB), start=True, stop=True)
            pe.matmul(banks[1][:, 2:3], raw[:, 2 * P:3 * P], vec(V_LNKB), start=True, stop=True).then_inc(setup_mm, 1)
            pe.wait_ge(weights_scaled, 4)
            pe.matmul(banks[2][:, 0:1], projw[:, :], bqkv[:, 2:3], start=True, stop=True).then_inc(setup_mm, 1)
            pe.wait_ge(weights_centred, 1)

            def query(u, m):
                pe.wait_ge(mean_taken, 2 * u + 2)
                pe.wait_ge(variance_ready, u)
                pe.wait_ge(mean_squared, u)
                pe.matmul(bank_sq[:, :], ones64, means[:, m].rearrange("p a n -> p (a n)"),
                          start=True, stop=True).then_inc(q_moments_mm, 1)
                pe.matmul(bank_mu[:, 0:2 * PT], wqkv[:, 0, :], means[:, m, 0, :],
                          start=True, stop=True).then_inc(q_raw_mm, 1)

            def head_sums(bank, what, b, src):
                for j in range(NJ):
                    mm = pe.matmul(bank[32 * j:32 * j + 32, :], what, src[:, j * CH:(j + 1) * CH],
                                   start=(b == 0), stop=(b == 1))
                return mm

            def pixel_means(u, m):
                pe.wait_ge(x_in[m], (u - m) * 8 + 32)
                pe.wait_ge(q_scaled, u + 1)
                for b in range(2):
                    mm = head_sums(bank_mu, avg(b), b, x[:, m, b, :])
                mm.then_inc(pixel_mean_mm, 1)

            def pixel_squares(u, m):
                pe.wait_ge(pixels_squared, 2 * u + 2)
                pe.wait_ge(q_variance_ready, u + 1)
                for b in range(2):
                    mm = head_sums(bank_sq, avg(b), b, xsq[:, b, :])
                mm.then_inc(pixel_square_mm, 1)

            def ring_free(u, idx):
                first = isinstance(u, int) and u <= 1
                last = isinstance(u, int) and u == UNITS - 1
                if idx <= 2:
                    if first:
                        pe.wait_ge(keys_times_q, 8 * u)
                    else:
                        pe.wait_ge(values_weighted, count(8 * (u - 2) + 6 + idx))
                elif idx == 3:
                    pe.wait_ge(bias_term_ready, u + 1)
                elif idx < RING_P:
                    pe.wait_ge(keys_times_q, count(8 * u + idx - 3))
                elif idx == RING_P:
                    if isinstance(u, int) and u >= UNITS - 2:
                        pe.wait_ge(values_weighted, 8 * u + 8)
                    else:
                        pe.wait_ge(keys_times_q, 8 * (u + 2) + 6)
                elif idx < RING_V + 2:
                    if last:
                        pe.wait_ge(values_weighted, 8 * u)
                    else:
                        pe.wait_ge(keys_times_q, count(8 * (u + 1) + idx - 3))
                elif idx == RING_V + 2:
                    pe.wait_ge(tokens_ready, u)
                else:
                    pe.wait_ge(values_weighted, count(8 * u + idx - RING_V - 2))

            def bias_term(u, m):
                ring_free(u, 0)
                pe.wait_ge(q_ready, u + 1)
                for j in range(NJ):
                    for b in range(2):
                        mm = pe.matmul(ring[0][32 * j:32 * j + 32, 0:32], indbk[:, 32 * b:32 * b + 32],
                                       qbuf[:, m % 2, b, 32 * j:32 * j + 32, 0], start=(b == 0), stop=(b == 1))
                mm.then_inc(bias_term_mm, 1)

            def keys(u, m, c):
                ring_free(u, RING_K + c)
                b, j = c // NJ, c % NJ
                pe.matmul(ring[(RING_K + c) % 3][:, :], wqkv[:, 1, :], x[:, m, b, j * CH:(j + 1) * CH],
                          start=True, stop=True).then_inc(keys_mm, 1)

            def scores(u, b):
                pe.wait_ge(keys_times_q, 8 * u + 4 * b + 4)
                if b == 0:
                    pe.wait_ge(scores_scaled, u)
                head_sums(bank_s, ind(b), b, prodk[:, b, :]).then_inc(scores_mm, 1)

            def turn_weights(u):
                pe.wait_ge(weights_ready, u + 1)
                pe.wait_ge(weights_copied, u)
                for r in range(4):
                    mm = pe.transpose(bank_t[:, r * P:(r + 1) * P], wgt[:, r * P:(r + 1) * P], eye)
                mm.then_inc(weights_turned, 1)

            def values(u, m, c):
                ring_free(u, RING_V + c)
                b, j = c // NJ, c % NJ
                for r in range(4):
                    at = j * CH + r * P
                    mm = pe.matmul(ring[(RING_V + c) % 3][:, r * P:(r + 1) * P], x[:, m, b, at:at + P],
                                   wqkv[:, 2, :], start=True, stop=True)
                mm.then_inc(values_mm, 1)

            def aggregate(u, b):
                pe.wait_ge(values_weighted, 8 * u + 4 * b + 4)
                if b == 0:
                    pe.wait_ge(aggregate_ready, u)
                for r in range(2):
                    for j in range(NJ):
                        rows = prodv[:, NJ * b + j, :].rearrange("p (h r k) -> p r h k", h=2, r=2)
                        mm = pe.matmul(bank_ag[32 * j:32 * j + 32, 0:2 * PT], patch(b), rows[:, r],
                                       start=(b == 0 and r == 0), stop=(b == 1 and r == 1))
                mm.then_inc(aggregate_mm, 1)

            def turn_aggregate(u):
                pe.wait_ge(aggregate_copied, u + 1)
                for h in range(2):
                    mm = pe.transpose(bank_ag[:, (2 + h) * PT:(3 + h) * PT], aggr_t[:, h * P:(h + 1) * P], eye)
                mm.then_inc(aggregate_turned, 1)

            def project(u):
                ring_free(u, RING_P)
                pe.wait_ge(aggregate_ready, u + 1)
                by_pair = aggr[:, :].rearrange("p (h j b w) -> p b j h w", h=2, j=NJ, b=2)
                for b in range(2):
                    mm = pe.matmul(ring[RING_P % 3][:, b * PT:(b + 1) * PT], projw[:, :], by_pair[:, b],
                                   start=True, stop=True)
                mm.then_inc(projected_mm, 1)

            pe.wait_ge(weights_scaled, 5)
            query(0, 0)
            pixel_means(0, 0)
            pixel_squares(0, 0)
            bias_term(0, 0)
            for c in range(8):
                keys(0, 0, c)
            scores(0, 0)
            scores(0, 1)
            query(1, 1)
            pixel_means(1, 1)
            pixel_squares(1, 1)

            def step(n, m):
                prev = not isinstance(n, int) or n >= 1
                nxt = not isinstance(n, int) or n + 1 < UNITS
                nxt2 = not isinstance(n, int) or n + 2 < UNITS
                m1, m2 = (m + 1) % NF, (m + 2) % NF
                if nxt:
                    bias_term(n + 1, m1)
                    keys(n + 1, m1, 0)
                    keys(n + 1, m1, 1)
                if prev:
                    turn_aggregate(n - 1)
                if nxt:
                    for c in range(2, 5):
                        keys(n + 1, m1, c)
                turn_weights(n)
                if nxt:
                    for c in range(5, 8):
                        keys(n + 1, m1, c)
                if prev:
                    project(n - 1)
                if nxt:
                    scores(n + 1, 0)
                for c in range(8):
                    values(n, m, c)
                    if c == 0 and nxt2:
                        query(n + 2, m2)
                    if c == 1 and nxt:
                        scores(n + 1, 1)
                    if c == 4 and nxt2:
                        pixel_means(n + 2, m2)
                    if c == 5:
                        aggregate(n, 0)
                if nxt2:
                    pixel_squares(n + 2, m2)
                aggregate(n, 1)

            pipeline(pe, step, UNITS)
            turn_aggregate(UNITS - 1)
            project(UNITS - 1)

            def drive(n, r):
                pe.wait_ge(force_ready, count(n - 1))
                pe.matmul(banks[r][:, :], wssm[:, 0, :], chunk(hT[:, :], n), start=True, stop=True).then_inc(drive_mm, 1)

            def mixed(n, r):
                pe.wait_ge(gelu_ready, count(n - 1))
                pe.matmul(banks[r][:, :], wssm[:, 1, :], chunk(z, n), start=True, stop=False)
                pe.matmul(banks[r][:, :], wssm[:, 2, :], chunk(hT[:, :], n), start=False, stop=True).then_inc(mixed_mm, 1)

            pe.wait_ge(tokens_ready, UNITS)
            pe.wait_ge(rest_in, 16)
            by_chunk(pe, drive)
            pe.wait_ge(chunk_fixed, 2 * L)
            by_chunk(pe, mixed)

            def centre_rows(i):
                pe.wait_ge(normed_ready, i)
                pe.matmul(bank_cen[:, :], centre, chunk(hT[:, :], i), start=True, stop=True).then_inc(centred_mm, 1)

            def variance(i):
                pe.wait_ge(centred_squared, i + 1)
                pe.wait_ge(logits_biased, i)
                pe.matmul(bank_var[:, :], ones64, sq3, start=True, stop=True).then_inc(norm_variance_mm, 1)

            def logits(i, p):
                pe.wait_ge(normed_ready, i + 1)
                pe.wait_ge(norm_log_ready, i + 1)
                pe.wait_ge(routing_copied, i)
                for g in range(G):
                    mm = pe.matmul(bank_var[:, 8 * g:8 * g + 8], h2[:, p, tokens_of(g)], gw[:, :],
                                   start=True, stop=True)
                mm.then_inc(logits_mm, 1)

            def ring_use(i, k):
                pe.wait_ge(hidden_ready, count(15 * i + k - 2))
                return ring[k % 3]

            def mstep(i, p):
                nxt = not isinstance(i, int) or i + 1 < ITERS
                if nxt:
                    centre_rows(i + 1)
                pe.matmul(ring_use(i, 0)[:, :], sw1[:, :], h2[:, p, :], start=True, stop=True).then_inc(hidden_mm, 1)
                for k in range(1, 9):
                    pe.matmul(ring_use(i, k)[:, :], ew1[:, (k - 1) // E, (k - 1) % E, :], h2[:, p, :],
                              start=True, stop=True).then_inc(hidden_mm, 1)
                if nxt:
                    variance(i + 1)
                for k in range(9, 11):
                    pe.wait_ge(hidden_ready, 15 * i + 1)
                    pe.matmul(ring_use(i, k)[:, :], sw2[:, k - 9, :], h1s,
                              start=True, stop=True).then_inc(hidden_mm, 1)
                for k in range(11, 15):
                    im, q = (k - 11) // 2, (k - 11) % 2
                    bank = ring_use(i, k)
                    pe.wait_ge(hidden_ready, 15 * i + 1 + E * im + 2 * q + 2)
                    for h in range(2):
                        mm = pe.matmul(bank[C * h:C * h + C, :], ew2[:, 2 * q + h, :], h1e[:, im, 2 * q + h],
                                       start=True, stop=True)
                    mm.then_inc(hidden_mm, 1)
                pe.wait_ge(routing_ready, i + 1)
                if nxt:
                    pe.wait_ge(norm_log_ready, i + 2)
                else:
                    pe.wait_ge(logits_biased, i + 1)
                pe.transpose(bank_var[0:32, 0:P], wmoe, eye).then_inc(routing_turned, 1)
                for g in range(G):
                    cols, toks = slice(g * P, (g + 1) * P), tokens_of(g)
                    pe.wait_ge(experts_weighted, count(G * i + g - 1))
                    pe.wait_ge(hidden_ready, 15 * i + 15)
                    for im in range(2):
                        for q in range(2):
                            at = im * 256 + q * P
                            mm = pe.matmul(bank_o[g % 2][:, at:at + P], h2e[:, im, q, toks], ew3[:, q, :],
                                           start=True, stop=True)
                    mm.then_inc(experts_mm, 1)
                    if g == 0:
                        pe.wait_ge(sum_ready, i)
                        pe.wait_ge(routing_copied, i + 1)
                    pe.matmul(bank_base[:, cols], h2[:, p, toks], eye, start=True, stop=False, skip_group_check=True)
                    for im in range(2):
                        pe.matmul(bank_base[:, g * P + C * im:g * P + C * im + C], h2s[:, im, toks], sw3[:, :],
                                  start=False, stop=False, skip_group_check=True)
                    mm = pe.matmul(bank_base[:, cols], wmT[0:33, p, :], b3[0:33, g, :],
                                   start=False, stop=True, skip_group_check=True)
                mm.then_inc(base_done, 1)
                if nxt:
                    logits(i + 1, (p + 1) % 2)

            pe.wait_ge(residual_ready, N_RES)
            pe.wait_ge(ones_row, 1)
            centre_rows(0)
            variance(0)
            logits(0, 0)
            mixture(pe, mstep)

        @block.vector
        def _(dve):
            n_coefs = [0]

            def link(ins):
                n_coefs[0] += 1
                ins.then_inc(coefs, 1)
                dve.wait_ge(coefs, n_coefs[0])

            dve.memset(wmT[32:33, :, :], 1.0).then_inc(ones_row, 1)
            dve.wait_ge(tok_in, 16)
            for n, v in ((0, V_LNQW), (1, V_LNKW), (2, V_LNKW)):
                dve.tensor_scalar(scaled[:, n * P:(n + 1) * P], raw[:, n * P:(n + 1) * P], vec(v), None,
                                  ALU.mult).then_inc(weights_scaled, 1)
            def svc(n):
                return sv[:, n:n + 1]

            link(dve.tensor_scalar(svc(SV_A), vec(V_A), DT * DT, None, ALU.mult))
            link(dve.tensor_scalar(svc(SV_S), svc(SV_A), 1.0, None, ALU.add))
            link(dve.reciprocal(svc(SV_S), svc(SV_S)))
            link(dve.scalar_tensor_tensor(svc(SV_NM), svc(SV_A), -1.0, svc(SV_S), ALU.mult, ALU.mult))
            link(dve.tensor_scalar(svc(SV_F), svc(SV_S), DT * DT, None, ALU.mult))
            link(dve.tensor_tensor(svc(SV_FB), svc(SV_F), vec(V_BB), ALU.mult))
            link(dve.tensor_tensor(svc(SV_CD), vec(V_BC), vec(V_BD), ALU.add))
            for a, n in ((cz, 0), (cz, 1), (cv, 0), (cv, 1)):
                link(dve.memset(a[:, 0, n:n + 1], float((a is cz) == (n == 0))))
            for j in range(L):
                link(dve.tensor_scalar(cacc[:, :], cz[:, j, :], svc(SV_NM), None, ALU.mult))
                link(dve.scalar_tensor_tensor(cv[:, j + 1, :], cv[:, j, :], svc(SV_S), cacc[:, :], ALU.mult, ALU.add))
                link(dve.tensor_tensor(cz[:, j + 1, :], cz[:, j, :], cv[:, j + 1, :], ALU.add))
            assert n_coefs[0] == N_COEFS

            dve.wait_ge(setup_mm, 2)
            dve.tensor_copy(bqkv[:, 1:3], banks[1][:, 1:3]).then_inc(biases_ready, 1)
            dve.tensor_scalar(bqkv[:, 0:1], banks[1][:, 0:1], float(C) ** -0.5, None, ALU.mult).then_inc(biases_ready, 1)
            dve.wait_ge(biases_ready, 2)
            dve.wait_ge(const_in, 16)
            dve.tensor_scalar(indbk[:, :], const[:, K_IND:K_AVG], bqkv[:, 1:2], None, ALU.mult).then_inc(weights_scaled, 1)
            dve.wait_ge(setup_mm, 3)
            dve.tensor_tensor(bqkv[:, 3:4], banks[2][:, 0:1], vec(V_PROJB), ALU.add).then_inc(weights_scaled, 1)

            def query_var(u):
                dve.wait_ge(q_mean_squared, u + 1)
                dve.tensor_tensor(qstat[:, :], bank_sq[:, 2 * PT:4 * PT], qstat[:, :], ALU.subtract).then_inc(q_variance_ready, 1)

            def query_scaled(u):
                dve.wait_ge(q_rstd_ready, u + 1)
                dve.wait_ge(q_raw_mm, u + 1)
                dve.wait_ge(q_ready, u)
                dve.tensor_tensor(qraw[:, :], bank_mu[:, 0:2 * PT], qrstd[:, :], ALU.mult).then_inc(q_scaled, 1)

            def pixel_var(u):
                dve.wait_ge(mean_squared, u + 1)
                dve.wait_ge(pixel_square_mm, u + 1)
                dve.tensor_tensor(vstat[:, :], bank_sq[:, :], vstat[:, :], ALU.subtract).then_inc(variance_ready, 1)

            def key_products(u, m, c):
                b, j = c // NJ, c % NJ
                dve.wait_ge(keys_mm, 8 * u + c + 1)
                if c == 0:
                    dve.wait_ge(q_ready, u + 1)
                if j == 0:
                    dve.wait_ge(scores_mm, count(2 * u - 1 + b))
                shape = "p (h s n) -> p h s n"
                q = qbuf[:, m % 2, b, 32 * j:32 * j + 32, :].rearrange("p (h w) t -> p h (w t)", h=2)
                dve.tensor_tensor(prodk[:, b, j * CH:(j + 1) * CH].rearrange(shape, h=2, s=S),
                                  ring[(RING_K + c) % 3][:, :].rearrange(shape, h=2, s=S),
                                  q[:, :, None, :].to_broadcast([P, 2, S, W]),
                                  ALU.mult).then_inc(keys_times_q, 1)

            def score_scale(u):
                dve.wait_ge(scores_mm, 2 * u + 2)
                dve.wait_ge(rstd_ready, u + 1)
                dve.wait_ge(weights_raw, u)
                dve.tensor_tensor(score[:, :], bank_s[:, :], rstd[:, :], ALU.mult).then_inc(scores_scaled, 1)

            def by_patch(a):
                return a[:, :].rearrange("p (h s w t) -> p h w s t", h=2, s=S, w=16)

            def score_max(u):
                dve.wait_ge(scores_biased, u + 1)
                dve.tensor_reduce(smx[:, :].rearrange("p (h w) -> p h w", h=2), by_patch(score), AX.XY,
                                  ALU.max).then_inc(score_max_ready, 1)
                dve.wait_ge(score_max_ready, u + 1)
                dve.tensor_copy(smxs[:, :].rearrange("p (n t) -> p n t", t=S),
                                smx[:, :, None].to_broadcast([P, 32, S])).then_inc(score_max_spread, 1)

            def score_sum(u):
                dve.wait_ge(scores_exp, u + 1)
                dve.tensor_reduce(ssm[:, :].rearrange("p (h w) -> p h w", h=2), by_patch(score), AX.XY,
                                  ALU.add).then_inc(exp_summed, 1)

            def score_inverse(u):
                dve.wait_ge(exp_summed, u + 1)
                dve.wait_ge(weights_ready, u)
                dve.reciprocal(smx[:, :], ssm[:, :]).then_inc(sum_inverted, 1)
                dve.wait_ge(sum_inverted, u + 1)
                dve.tensor_copy(srz[:, :].rearrange("p (n t) -> p n t", t=S),
                                smx[:, :, None].to_broadcast([P, 32, S])).then_inc(inverse_sum_ready, 1)

            def value_products(u, m, c):
                b, j = c // NJ, c % NJ
                dve.wait_ge(values_mm, 8 * u + c + 1)
                if c == 0:
                    dve.wait_ge(weights_copied, u + 1)
                if j == 0:
                    dve.wait_ge(aggregate_mm, count(2 * u - 1 + b))
                k = wT[:, m % 2, :].rearrange("p (r k) -> p r k", r=4)[:, :, 32 * j + 16 * b:32 * j + 16 * b + 16]
                shape = "p (r k d) -> p r k d"
                dve.tensor_tensor(prodv[:, c, :].rearrange(shape, r=4, d=D),
                                  ring[(RING_V + c) % 3][:, :].rearrange(shape, r=4, d=D),
                                  k[:, :, :, None].to_broadcast([P, 4, 16, D]), ALU.mult).then_inc(values_weighted, 1)

            def tokens(u, m):
                dve.wait_ge(projected_mm, u + 1)
                half = m % 2
                pairs = hT[:, :].rearrange("p (g b n) -> p g b n", b=2, n=HW)
                dst = pairs[:, (u - half) // 2, :, half * PT:(half + 1) * PT]
                dve.scalar_tensor_tensor(dst, ring[RING_P % 3][:, 0:2 * PT].rearrange("p (b n) -> p b n", b=2),
                                         bqkv[:, 3:4], means[:, m, 0, :].rearrange("p (b n) -> p b n", b=2),
                                         ALU.add, ALU.add).then_inc(tokens_ready, 1)

            query_var(0)
            query_scaled(0)
            pixel_var(0)
            for c in range(8):
                key_products(0, 0, c)
            score_scale(0)
            query_var(1)
            score_max(0)
            query_scaled(1)
            score_sum(0)
            score_inverse(0)

            def step(n, m):
                nxt = not isinstance(n, int) or n + 1 < UNITS
                nxt2 = not isinstance(n, int) or n + 2 < UNITS
                m1 = (m + 1) % NF
                if nxt:
                    pixel_var(n + 1)
                if nxt:
                    for c in range(8):
                        key_products(n + 1, m1, c)
                if not isinstance(n, int) or n >= 1:
                    tokens(n - 1, (m - 1) % NF)
                for c in range(8):
                    value_products(n, m, c)
                    if c == 0 and nxt2:
                        query_var(n + 2)
                    if c == 1 and nxt:
                        score_scale(n + 1)
                    if c == 2 and nxt2:
                        query_scaled(n + 2)
                    if c == 4 and nxt:
                        score_max(n + 1)
                if nxt:
                    score_sum(n + 1)
                    score_inverse(n + 1)

            pipeline(dve, step, UNITS)
            tokens(UNITS - 1, (UNITS - 1) % NF)

            def at(a, j):
                return a.rearrange("p (n j) -> p n j", j=L)[:, :, j]

            dve.wait_ge(force_ready, N_CHUNKS)
            dve.tensor_copy(at(z, 0), at(force, 0)).then_inc(scan_step, 1)
            dve.tensor_copy(vel, at(force, 0)).then_inc(scan_step, 1)
            with dve.Fori(0, (L - 1) // 3) as k:
                for r in range(3):
                    j = 3 * k + r + 1
                    done = 9 * k + 3 * r + 2
                    dve.wait_ge(scan_step, done)
                    dve.scalar_tensor_tensor(acc, at(z, j - 1), sv[:, SV_NM:SV_NM + 1], at(force, j),
                                             ALU.mult, ALU.add).then_inc(scan_step, 1)
                    dve.wait_ge(scan_step, done + 1)
                    dve.scalar_tensor_tensor(vel, vel, sv[:, SV_S:SV_S + 1], acc, ALU.mult, ALU.add).then_inc(scan_step, 1)
                    dve.wait_ge(scan_step, done + 2)
                    dve.tensor_tensor(at(z, j), at(z, j - 1), vel, ALU.add).then_inc(scan_step, 1)

            def start(a, c):
                return a.rearrange("p (n c) -> p n c", c=NCK)[:, :, c]

            ends = z.rearrange("p (n c j) -> p n c j", c=NCK, j=L)
            dve.memset(start(zin, 0), 0.0).then_inc(carry_step, 1)
            dve.memset(start(vin, 0), 0.0).then_inc(carry_step, 1)
            dve.wait_ge(scan_step, count(2 + 3 * (L - 1)))
            with dve.Fori(0, (NCK - 1) // 3) as k:
                for r in range(3):
                    c = 3 * k + r
                    done = 12 * k + 4 * r + 2
                    for o, (coef, loc) in enumerate(((cz, ends[:, :, c, L - 1]), (cv, start(vel, c)))):
                        dve.wait_ge(carry_step, done)
                        dve.scalar_tensor_tensor(ctmp[:, o * PAIRS:(o + 1) * PAIRS], start(zin, c), coef[:, L, 0:1], loc,
                                                 ALU.mult, ALU.add).then_inc(carry_step, 1)
                    for o, (coef, dst) in enumerate(((cz, zin), (cv, vin))):
                        dve.wait_ge(carry_step, done + 1 + o)
                        dve.scalar_tensor_tensor(start(dst, c + 1), start(vin, c), coef[:, L, 1:2],
                                                 ctmp[:, o * PAIRS:(o + 1) * PAIRS],
                                                 ALU.mult, ALU.add).then_inc(carry_step, 1)
            dve.wait_ge(carry_step, count(2 + 4 * (NCK - 1)))
            for o, src in enumerate((zin, vin)):
                for j in range(L):
                    dve.wait_ge(chunk_fixed, count(L * o + j + 1 - L))
                    dve.scalar_tensor_tensor(at(z, j), src, cz[:, j + 1, o:o + 1], at(z, j),
                                             ALU.mult, ALU.add).then_inc(chunk_fixed, 1)

            for n in range(N_RES):
                dve.wait_ge(silu_ready, n + 1)
                cols = slice(n * PX // 2, (n + 1) * PX // 2)
                dve.scalar_tensor_tensor(hT[:, cols], hT[:, cols], 2.0, force[:, cols],
                                         ALU.mult, ALU.add).then_inc(residual_ready, 1)

            def normed(i, p):
                dve.wait_ge(norm_rstd_ready, i + 1)
                dve.wait_ge(base_done, count(i - 1))
                dve.tensor_tensor(h2[:, p, :], bank_cen[:, :], ln3, ALU.mult).then_inc(normed_ready, 1)

            def by_row(a):
                return a.rearrange("p (n e) -> p n e", e=E)

            def spread(a):
                return a[:, :, None].to_broadcast([P, 8, E])

            def routing(i):
                mx, sm, rc, m1, tot, inv = (l8[:, n, :] for n in range(6))
                dve.wait_ge(logits_mm, i + 1)
                dve.tensor_tensor(by_row(lg), by_row(bank_var[:, 0:32]), gbias[:, None, :].to_broadcast([P, 8, E]),
                                  ALU.add).then_inc(logits_biased, 1)
                dve.wait_ge(logits_biased, i + 1)
                dve.tensor_reduce(mx, by_row(lg), AX.X, ALU.max).then_inc(logits_max, 1)
                dve.wait_ge(logits_max, i + 1)
                dve.tensor_tensor(by_row(lgx), by_row(lg), spread(mx), ALU.subtract).then_inc(logits_shifted, 1)
                dve.wait_ge(logits_exp, i + 1)
                dve.tensor_reduce(sm, by_row(lgx), AX.X, ALU.add).then_inc(logits_sum, 1)
                dve.wait_ge(logits_sum, i + 1)
                dve.reciprocal(rc, sm).then_inc(logits_inverse, 1)
                dve.wait_ge(logits_inverse, i + 1)
                dve.tensor_tensor(by_row(gat), by_row(lgx), spread(rc), ALU.mult).then_inc(gates_ready, 1)
                dve.wait_ge(gates_ready, i + 1)
                dve.tensor_reduce(m1, by_row(gat), AX.X, ALU.max).then_inc(gate_max, 1)
                dve.wait_ge(gate_max, i + 1)
                dve.tensor_tensor(by_row(pick), by_row(gat), spread(m1), ALU.subtract).then_inc(gates_shifted, 1)
                own = by_row(gat)[:, :, :, None].to_broadcast([P, 8, E, E])
                other = by_row(gat)[:, :, None, :].to_broadcast([P, 8, E, E])
                square = "p (n e f) -> p n e f"
                up = const[:, K_UP:K_EPS].rearrange("p (e f) -> p e f", f=E)[:, None, :, :].to_broadcast([P, 8, E, E])
                bt, ti = beat.rearrange(square, e=E, f=E), tie.rearrange(square, e=E, f=E)
                dve.tensor_tensor(bt, other, own, ALU.is_ge).then_inc(gates_compared, 1)
                dve.tensor_tensor(ti, other, own, ALU.is_equal).then_inc(ties_found, 1)
                dve.wait_ge(ties_found, i + 1)
                dve.tensor_tensor(ti, ti, up, ALU.mult).then_inc(ties_counted, 1)
                dve.wait_ge(ties_counted, i + 1)
                dve.tensor_tensor(beat, beat, tie, ALU.subtract).then_inc(wins_ready, 1)
                dve.wait_ge(wins_ready, i + 1)
                dve.tensor_reduce(by_row(lg), bt, AX.X, ALU.add).then_inc(rank_ready, 1)
                dve.wait_ge(rank_ready, i + 1)
                dve.wait_ge(gates_exp, i + 1)
                dve.scalar_tensor_tensor(pick, lg, 1.5, pick, ALU.is_lt, ALU.mult).then_inc(picked, 1)
                dve.wait_ge(picked, i + 1)
                dve.tensor_reduce(tot, by_row(pick), AX.X, ALU.add).then_inc(picked_sum, 1)
                dve.wait_ge(picked_sum, i + 1)
                dve.reciprocal(inv, tot).then_inc(picked_inverse, 1)
                dve.wait_ge(picked_inverse, i + 1)
                dve.tensor_tensor(by_row(wmoe), by_row(pick), spread(inv), ALU.mult).then_inc(routing_ready, 1)

            def weigh(i, g):
                dve.wait_ge(experts_mm, G * i + g + 1)
                dve.wait_ge(half_summed, count(G * i + g - 1))
                w8 = wmoe[:, 8 * g:8 * g + 8][:, :, None].to_broadcast([P, 8, C])
                dve.tensor_tensor(eprod[:, g % 2, :].rearrange("p (n c) -> p n c", c=C),
                                  bank_o[g % 2][:, :].rearrange("p (n c) -> p n c", c=C), w8,
                                  ALU.mult).then_inc(experts_weighted, 1)

            def rows(a):
                return a.rearrange("p (n c) -> p n c", c=C)

            def total(i):
                dve.wait_ge(base_done, i + 1)
                dve.wait_ge(gated_summed, G * i + G)
                dve.wait_ge(out_centred, i)
                dve.tensor_tensor(ysb, bank_base[:, :], gsum, ALU.add).then_inc(sum_ready, 1)
                dve.wait_ge(sum_ready, i + 1)
                dve.tensor_reduce(y8[:, 0, :], rows(ysb), AX.X, ALU.add).then_inc(sum_added, 1)
                dve.wait_ge(sum_added, i + 1)
                dve.tensor_scalar(y8[:, 1, :], y8[:, 0, :], 1.0 / C, None, ALU.mult).then_inc(mean_ready, 1)

            def square_sum(i):
                dve.wait_ge(out_squared, i + 1)
                dve.wait_ge(out_rstd_ready, i)
                dve.tensor_reduce(y8[:, 2, :], rows(ysq), AX.X, ALU.add).then_inc(out_square_sum, 1)

            normed(0, 0)

            def mstep(i, p):
                prev = not isinstance(i, int) or i >= 1
                if prev:
                    total(i - 1)
                routing(i)
                if prev:
                    square_sum(i - 1)
                if not isinstance(i, int) or i + 1 < ITERS:
                    normed(i + 1, (p + 1) % 2)
                for g in range(G):
                    weigh(i, g)

            mixture(dve, mstep)
            total(ITERS - 1)
            square_sum(ITERS - 1)


_OUT = (B, HW, C)


def _blocks(out, cols, w):
    out[0:C, cols:cols + C] = w
    out[C:P, cols + C:cols + 2 * C] = w


def _tokenizer_pack(a):
    out = np.zeros((P, T_END), np.float32)
    wkv = a["L0_tok_Wkv"]
    for n, w in enumerate((a["L0_tok_Wq"], wkv[0:C], wkv[C:2 * C], a["L0_tok_proj_w"])):
        _blocks(out, T_RAW + n * P, w.T)
    for n, name in enumerate(("tok_ln_q_w", "tok_ln_q_b", "tok_ln_kv_w", "tok_ln_kv_b", "tok_proj_b",
                              "attn_a", "attn_b_B", "attn_b_C", "attn_b_D")):
        for i in range(2):
            out[C * i:C * i + C, T_VEC + n] = a["L0_" + name]
    return out


def _rest_pack(a):
    out = np.zeros((P, R_END), np.float32)
    for n, name in enumerate("BCD"):
        _blocks(out, R_SSM + n * P, a["L0_attn_W_" + name].T)
    _blocks(out, R_SW1, a["L0_ffn_sW1"])
    out[:, R_SW3:R_EW2] = a["L0_ffn_sW3"]
    for i in range(2):
        r = slice(C * i, C * i + C)
        out[r, R_SW2 + i * P:R_SW2 + (i + 1) * P] = a["L0_ffn_sW2"]
        out[r, R_GW + E * i:R_GW + E * i + E] = a["L0_ffn_gW"]
        out[r, R_EB + 6] = a["L0_ffn_sb1"]
        for e in range(E):
            at = R_EW1 + (E * i + e) * P
            out[r, at:at + P] = a["L0_ffn_eW1"][e]
        for q in range(2):
            at = R_EW3 + q * P + C * i
            out[r, at:at + C] = a["L0_ffn_eW3"][2 * q + i]
            out[r, R_EB + 4 + q] = a["L0_ffn_eb2"][2 * q + i]
        for g in range(G):
            at = R_B3 + g * P + C * i
            out[8 * g + E * i:8 * g + E * i + E, at:at + C] = a["L0_ffn_eb3"]
            out[32, at:at + C] = a["L0_ffn_sb3"]
    for e in range(E):
        out[:, R_EW2 + e * C:R_EW2 + (e + 1) * C] = a["L0_ffn_eW2"][e]
        out[:, R_EB + e] = a["L0_ffn_eb1"][e]
    out[:, R_GB:R_EB] = a["L0_ffn_gb"]
    out[:, R_EB + 7] = a["L0_ffn_sb2"]
    return out


def kernel(**inputs):
    import concourse.bacc as _bacc
    from concourse.bass_utils import run_bass_kernel_spmd as _run

    a = {n: np.asarray(v) for n, v in inputs.items()}
    arrays = {
        "x": np.ascontiguousarray(a["x"]).reshape(PAIRS, P, H * W),
        "tok_w": _tokenizer_pack(a),
        "rest_w": _rest_pack(a),
        "const": shape_constants(),
    }
    nc = _bacc.Bacc("TRN2", target_bir_lowering=False, num_devices=1)
    t = {n: nc.dram_tensor(n, v.shape, F32, kind="ExternalInput").ap() for n, v in arrays.items()}
    t["out"] = nc.dram_tensor("out", (PAIRS, 2, HW, C), F32, kind="ExternalOutput").ap()
    build(nc, t)
    r = _run(nc, [arrays], core_ids=[0])
    return np.asarray(r.results[0]["out"]).reshape(_OUT)
```

```python
from contextlib import ExitStack

import numpy as np

import concourse.bass as bass
from concourse import mybir

ALU = mybir.AluOpType
ACT = mybir.ActivationFunctionType
AX = mybir.AxisListType
F32 = mybir.dt.float32
F32R = mybir.dt.float32r

P = 128
B, C, H, W = 64, 64, 64, 64
S = 4
N_PIX = S * S
HEADS = 8
D = C // HEADS
HW = (H // S) * (W // S)
PAIRS = B // 2
UNITS = PAIRS
PX = H * W // 2
PT = HW // 2
CH = 512
NJ = PX // CH
E = 4
NF = 4
DT = 1.0 / HW
L = 16
NCK = HW // L
EPS = 1e-5
ITERS = PAIRS // 2
G = 2 * HW // P

K_ONES, K_CEN, K_EYE, K_IND, K_AVG, K_PATCH, K_UP, K_EPS, K_END = 0, 128, 256, 384, 448, 512, 576, 592, 593
V_LNQW, V_LNQB, V_LNKW, V_LNKB, V_PROJB, V_A, V_BB, V_BC, V_BD, N_VEC = range(10)
T_RAW, T_PROJ, T_VEC, T_END = 0, 384, 512, 512 + N_VEC
R_SSM, R_EW1, R_SW1, R_GW, R_SW2, R_SW3, R_EW2, R_EW3, R_B3, R_GB, R_EB, R_END = (
    0, 384, 896, 1088, 1096, 1352, 1416, 1672, 1928, 2440, 2444, 2452)
W1 = R_GW - R_EW1
W1_S = R_SW1 - R_EW1
SV_A, SV_S, SV_NM, SV_F, SV_FB, SV_CD, SV_NS, SV_G, N_SV = range(9)
N_COEFS = 14 + 3 * L
HP = PAIRS * HW // 2
HS = HP // L
N_PIECE = HP // CH
STORE = 4 * 16
N_RES = 4


def shape_constants():
    k = np.zeros((P, K_END), np.float32)
    blocks = np.kron(np.eye(2), np.ones((C, C))) / C
    k[:, K_ONES:K_CEN] = blocks
    k[:, K_CEN:K_EYE] = np.eye(P) - blocks
    k[:, K_EYE:K_IND] = np.eye(P)
    for b in range(2):
        for p in range(P):
            k[p, K_IND + 32 * b + 16 * b + p // D] = 1.0
            at = K_AVG + 32 * b + 16 * b + HEADS * (p // C)
            k[p, at:at + HEADS] = 1.0 / C
    for p in range(P):
        for b in range(2):
            k[p, K_PATCH + 32 * b + 16 * b + (p % W) // S] = 1.0
    for e in range(E):
        for f in range(E):
            k[:, K_UP + E * e + f] = float(f >= e)
    k[:, K_EPS] = EPS
    return k


def build(nc, t):
    ctx = ExitStack()
    with ctx:
        def sb(name, *shape):
            return ctx.enter_context(nc.sbuf_tensor("sb_" + name, list(shape), F32))

        def sem(name):
            return ctx.enter_context(nc.semaphore(name))

        banks = [ctx.enter_context(nc.psum_tensor(f"bank{i}", [P, CH], F32)) for i in range(8)]

        arena = sb("arena", P, NF * 2 * PX)
        hT = sb("hT", P, PAIRS * HW)
        const = sb("const", P, K_END)
        xsq = sb("xsq", P, 2, PX)
        prodk = sb("prodk", P, 2, PX)
        rows2 = sb("rows2", P, 2, 1024)
        sum16 = sb("sum16", P, 2 * PT)
        means = sb("means", P, NF, 2, 2 * PT)
        qbuf = sb("qbuf", P, 2, 2, PT, S)
        qstat = sb("qstat", P, 2 * PT)
        qrstd = sb("qrstd", P, 2 * PT)
        qraw = sb("qraw", P, 2 * PT)
        vstat = sb("vstat", P, CH)
        rstd = sb("rstd", P, CH)
        score = sb("score", P, CH)
        wgt = sb("wgt", P, CH)
        smx = sb("smx", P, 32)
        smxs = sb("smxs", P, 32 * S)
        ssm = sb("ssm", P, 32)
        srz = sb("srz", P, 32 * S)
        cbias = sb("cbias", P, 32 * S)
        wT = sb("wT", P, 2, CH)
        aggr_t = sb("aggr_t", P, 2 * PT)
        aggr = sb("aggr", P, 2 * PT)
        tok_w = sb("tok_w", P, T_END)
        scaled = prodk[:, 0, 0:3 * P]
        wqkv = sb("wqkv", P, 3, P)
        bqkv = sb("bqkv", P, 4)
        indbk = sb("indbk", P, 64)
        rest_w = sb("rest_w", P, R_END)
        sv = sb("sv", P, N_SV)
        cz = sb("cz", P, L + 1, 2)
        cv = sb("cv", P, L + 1, 2)
        cacc = sb("cacc", P, 2)
        wmT = sb("wmT", P, 2, P)

        with nc.sbuf_tensor("sb_prodv", [P, 8, CH], F32) as prodv:
            pass
        w1_high = ctx.enter_context(nc.sbuf_tensor("sb_w1_high", [P, W1], F32R))
        w1_low = ctx.enter_context(nc.sbuf_tensor("sb_w1_low", [P, W1], F32R))
        parts = ctx.enter_context(nc.sbuf_tensor("sb_parts", [P, 2, CH], F32R))

        raw = tok_w[:, T_RAW:T_PROJ]
        projw = tok_w[:, T_PROJ:T_VEC]
        vecs = tok_w[:, T_VEC:T_END]
        wssm = rest_w[:, R_SSM:R_EW1].rearrange("p (a n) -> p a n", a=3)
        w1 = rest_w[:, R_EW1:R_GW]
        gw = rest_w[:, R_GW:R_SW2]
        sw2 = rest_w[:, R_SW2:R_SW3].rearrange("p (m n) -> p m n", m=2)
        sw3 = rest_w[:, R_SW3:R_EW2]
        ew2 = rest_w[:, R_EW2:R_EW3].rearrange("p (e n) -> p e n", e=E)
        ew3 = rest_w[:, R_EW3:R_B3].rearrange("p (q n) -> p q n", q=2)
        b3 = rest_w[:, R_B3:R_GB].rearrange("p (g n) -> p g n", g=G)
        gbias = rest_w[:, R_GB:R_EB]
        ebias = rest_w[:, R_EB:R_END]

        def vec(n):
            return vecs[:, n:n + 1]

        ones64 = const[:, K_ONES:K_CEN]
        centre = const[:, K_CEN:K_EYE]
        eye = const[:, K_EYE:K_IND]
        eps = const[:, K_EPS:K_EPS + 1]

        def ind(b):
            return const[:, K_IND + 32 * b:K_IND + 32 * b + 32]

        def patch(b):
            return const[:, K_PATCH + 32 * b:K_PATCH + 32 * b + 32]

        def avg(b):
            return const[:, K_AVG + 32 * b:K_AVG + 32 * b + 32]

        x = arena[:, :].rearrange("p (m b n) -> p m b n", m=NF, b=2)

        const_in = sem("const_in")
        tok_in = sem("tok_in")
        rest_in = sem("rest_in")
        coefs = sem("coefs")
        ones_row = sem("ones_row")
        x_in = [sem(f"x_in{m}") for m in range(NF)]
        weights_scaled = sem("weights_scaled")
        setup_mm = sem("setup_mm")
        weights_centred = sem("weights_centred")
        biases_ready = sem("biases_ready")
        row_pairs_added = sem("row_pairs_added")
        rows_added = sem("rows_added")
        half_rows_added = sem("half_rows_added")
        patch_summed = sem("patch_summed")
        mean_taken = sem("mean_taken")
        q_moments_mm = sem("q_moments_mm")
        q_raw_mm = sem("q_raw_mm")
        q_mean_squared = sem("q_mean_squared")
        q_variance_ready = sem("q_variance_ready")
        q_log_ready = sem("q_log_ready")
        q_rstd_ready = sem("q_rstd_ready")
        q_scaled = sem("q_scaled")
        q_ready = sem("q_ready")
        pixels_squared = sem("pixels_squared")
        pixel_mean_mm = sem("pixel_mean_mm")
        pixel_square_mm = sem("pixel_square_mm")
        mean_squared = sem("mean_squared")
        variance_ready = sem("variance_ready")
        log_ready = sem("log_ready")
        rstd_ready = sem("rstd_ready")
        bias_term_mm = sem("bias_term_mm")
        bias_term_ready = sem("bias_term_ready")
        keys_mm = sem("keys_mm")
        keys_times_q = sem("keys_times_q")
        scores_mm = sem("scores_mm")
        scores_scaled = sem("scores_scaled")
        scores_biased = sem("scores_biased")
        score_max_ready = sem("score_max_ready")
        score_max_spread = sem("score_max_spread")
        scores_shifted = sem("scores_shifted")
        scores_exp = sem("scores_exp")
        exp_summed = sem("exp_summed")
        sum_inverted = sem("sum_inverted")
        inverse_sum_ready = sem("inverse_sum_ready")
        weights_raw = sem("weights_raw")
        weights_ready = sem("weights_ready")
        weights_turned = sem("weights_turned")
        weights_copied = sem("weights_copied")
        values_mm = sem("values_mm")
        values_weighted = sem("values_weighted")
        aggregate_mm = sem("aggregate_mm")
        aggregate_copied = sem("aggregate_copied")
        aggregate_turned = sem("aggregate_turned")
        aggregate_ready = sem("aggregate_ready")
        projected_mm = sem("projected_mm")
        tokens_ready = sem("tokens_ready")
        drive_mm = sem("drive_mm")
        force_ready = sem("force_ready")
        scan_step = [sem(f"scan_step{h}") for h in range(2)]
        carry_step = [sem(f"carry_step{h}") for h in range(2)]
        chunk_fixed = [sem(f"chunk_fixed{h}") for h in range(2)]
        mixed_mm = sem("mixed_mm")
        gelu_ready = sem("gelu_ready")
        silu_ready = sem("silu_ready")
        residual_ready = sem("residual_ready")
        centred_mm = sem("centred_mm")
        centred_squared = sem("centred_squared")
        norm_variance_mm = sem("norm_variance_mm")
        norm_log_ready = sem("norm_log_ready")
        norm_rstd_ready = sem("norm_rstd_ready")
        normed_ready = sem("normed_ready")
        logits_mm = sem("logits_mm")
        logits_biased = sem("logits_biased")
        logits_max = sem("logits_max")
        logits_shifted = sem("logits_shifted")
        logits_exp = sem("logits_exp")
        logits_sum = sem("logits_sum")
        logits_inverse = sem("logits_inverse")
        gates_ready = sem("gates_ready")
        gates_compared = sem("gates_compared")
        ties_found = sem("ties_found")
        ties_counted = sem("ties_counted")
        wins_ready = sem("wins_ready")
        rank_ready = sem("rank_ready")
        gate_max = sem("gate_max")
        gates_shifted = sem("gates_shifted")
        gates_exp = sem("gates_exp")
        picked = sem("picked")
        picked_sum = sem("picked_sum")
        picked_inverse = sem("picked_inverse")
        routing_ready = sem("routing_ready")
        routing_turned = sem("routing_turned")
        routing_copied = sem("routing_copied")
        hidden_mm = sem("hidden_mm")
        hidden_ready = [sem(f"hidden_ready{r}") for r in range(5)]
        weights_rounded = sem("weights_rounded")
        weights_split = sem("weights_split")
        high_ready = sem("high_ready")
        low_ready = sem("low_ready")
        experts_mm = sem("experts_mm")
        experts_weighted = sem("experts_weighted")
        half_summed = sem("half_summed")
        gated_summed = sem("gated_summed")
        base_done = sem("base_done")
        sum_ready = sem("sum_ready")
        sum_added = sem("sum_added")
        mean_ready = sem("mean_ready")
        out_centred = sem("out_centred")
        out_squared = sem("out_squared")
        out_square_sum = sem("out_square_sum")
        out_log_ready = sem("out_log_ready")
        out_rstd_ready = sem("out_rstd_ready")
        out_ready = sem("out_ready")
        stored = [sem(f"stored{i}") for i in range(2)]

        def count(value):
            return max(value, 0) if isinstance(value, int) else value

        def pipeline(eng, step, total):
            lead, tail = NF, NF
            for n in range(lead):
                step(n, n % NF)
            with eng.Fori(1, (total - tail) // NF) as k:
                for m in range(NF):
                    step(k * NF + m, m)
            for n in range(total - tail, total):
                step(n, n % NF)

        ring = banks[0:3]
        bank_s, bank_sq, bank_mu, bank_ag, bank_t = banks[3:8]
        RING_K, RING_P, RING_V = 1, 9, 10

        mix = arena[:, :]
        pos = [0]

        def cut(n):
            a = mix[:, pos[0]:pos[0] + n]
            pos[0] += n
            return a

        h2 = cut(2 * CH).rearrange("p (i n) -> p i n", i=2)
        sq3 = cut(CH)
        ln3 = cut(CH)
        h1s = cut(CH)
        h1e = cut(8 * CH).rearrange("p (m e n) -> p m e n", m=2, e=E)
        h2s = cut(2 * CH).rearrange("p (m n) -> p m n", m=2)
        h2e = cut(4 * CH).rearrange("p (m q n) -> p m q n", m=2, q=2)
        eprod = cut(2 * CH).rearrange("p (r n) -> p r n", r=2)
        esum2 = cut(CH).rearrange("p (r m e c) -> p r m e c", r=2, m=2, e=2)
        gsum = cut(CH)
        ysb = cut(CH)
        ycen = cut(CH)
        ysq = cut(CH)
        out_t = cut(2 * CH).rearrange("p (i a n) -> p i a n", i=2, a=2)
        lg = cut(32)
        lgx = cut(32)
        gat = cut(32)
        pick = cut(32)
        wmoe = cut(32)
        l8 = cut(8 * 8).rearrange("p (a n) -> p a n", a=8)
        y8 = cut(8 * 4).rearrange("p (a n) -> p a n", a=4)
        beat = cut(P)
        tie = cut(P)
        assert pos[0] <= NF * 2 * PX
        force = arena[:, 0:2 * HP]
        z = arena[:, 2 * HP:4 * HP]
        vel = xsq[:, 0, 0:CH]
        zin = xsq[:, 0, 2 * CH:3 * CH]
        vin = xsq[:, 0, 3 * CH:4 * CH]
        ctmp = xsq[:, 1, 0:2 * PAIRS]

        def chunk(a, n):
            return a.rearrange("p (n k) -> p n k", k=CH)[:, n, :]

        def at(h, j):
            return slice(h * HP + j * HS, h * HP + (j + 1) * HS)

        def piece(h, n, size=CH):
            return slice(h * HP + n * size, h * HP + (n + 1) * size)

        def tokens_at(h, n, steps):
            return hT[:, h * HP:(h + 1) * HP].rearrange("p (n j) -> p j n", j=L)[:, n * steps:(n + 1) * steps]

        def tokens_of(g):
            return slice((g // 2) * HW + g % 2, (g // 2 + 1) * HW, 2)

        bank_cen, bank_var, bank_base = banks[3], banks[4], banks[5]
        bank_o = banks[6:8]
        hidden_ring = banks[0:3] + bank_o
        RING, RELUS = len(hidden_ring), 15

        def relu(eng, i, k):
            eng.wait_ge(hidden_mm, RELUS * i + k + 1)
            if k == 0:
                dst, bias = h1s, ebias[:, 6:7]
            elif k < 9:
                dst, bias = h1e[:, (k - 1) // E, (k - 1) % E], ebias[:, (k - 1) % E:(k - 1) % E + 1]
            elif k < 11:
                dst, bias = h2s[:, k - 9], ebias[:, 7:8]
            else:
                dst, bias = h2e[:, (k - 11) // 2, (k - 11) % 2], ebias[:, 4 + (k - 11) % 2:5 + (k - 11) % 2]
            bank, done = hidden_ring[k % RING], hidden_ready[k % RING]
            if k % RING == 2:
                eng.tensor_scalar(dst, bank[:, :], bias, 0.0, ALU.add, ALU.max).then_inc(done, 1)
            else:
                eng.activation(dst, bank[:, :], ACT.Relu, bias=bias).then_inc(done, 1)

        def mixture(eng, step):
            for i in range(2):
                step(i, i)
            with eng.Fori(1, ITERS // 2 - 1) as k:
                for p in range(2):
                    step(2 * k + p, p)
            for i in range(ITERS - 2, ITERS):
                step(i, i % 2)

        def fixed(j):
            return min(2 * j + 3, 2 * L)

        block = ctx.enter_context(nc.Block())


        @block.sync
        def _(sp):
            def load(u, m):
                sp.wait_ge(values_mm, count((u - NF) * 8 + 8))
                half = m % 2
                for b in range(2):
                    src = t["x"][(u - half) + b]
                    sp.dma_start(x[:, m, b, :], src[:, half * PX:(half + 1) * PX]).then_inc(x_in[m], 16)

            sp.dma_start(tok_w[:, :], t["tok_w"]).then_inc(tok_in, 16)
            load(0, 0)
            sp.dma_start(const[:, :], t["const"]).then_inc(const_in, 16)
            for u in range(1, NF):
                load(u, u)
            sp.dma_start(rest_w[:, :], t["rest_w"]).then_inc(rest_in, 16)
            with sp.Fori(1, UNITS // NF) as k:
                for m in range(NF):
                    load(k * NF + m, m)

            def store(i, p):
                sp.wait_ge(out_ready, i + 1)
                for a in range(2):
                    for m in range(2):
                        sp.dma_start(t["out"][2 * i + a, m].rearrange("(k f) c -> k f c", f=2),
                                     out_t[:, p, a].rearrange("p (f m c) -> p f m c", f=2, m=2)[:, :, m]
                                     ).then_inc(stored[p], 16)

            with sp.Fori(0, ITERS // 2) as k:
                for p in range(2):
                    store(2 * k + p, p)
            for p in range(2):
                sp.wait_ge(stored[p], STORE * (ITERS // 2))

        @block.gpsimd
        def _(pool):
            def patch_sums(u, m):
                pool.wait_ge(x_in[m], (u - m) * 8 + 32)
                rows = x[:, m, :, :].rearrange("p b (h s n) -> p (b h) s n", s=S, n=W)
                out = [rows2[:, i, :].rearrange("p (h n) -> p h n", n=W) for i in range(2)]
                pool.wait_ge(patch_summed, u)
                for i in range(2):
                    pool.tensor_tensor(out[i], rows[:, :, 2 * i], rows[:, :, 2 * i + 1], ALU.add).then_inc(row_pairs_added, 1)
                pool.wait_ge(row_pairs_added, 2 * u + 2)
                pool.tensor_tensor(rows2[:, 0, :], rows2[:, 0, :], rows2[:, 1, :], ALU.add).then_inc(rows_added, 1)
                pool.wait_ge(rows_added, u + 1)
                four = rows2[:, 0, :].rearrange("p (n t) -> p n t", t=S)
                two = rows2[:, 1, 0:2 * 2 * PT].rearrange("p (n t) -> p n t", t=2)
                pool.tensor_tensor(two, four[:, :, 0:2], four[:, :, 2:4], ALU.add).then_inc(half_rows_added, 1)
                pool.wait_ge(half_rows_added, u + 1)
                pool.wait_ge(mean_taken, 2 * u)
                pool.tensor_tensor(sum16[:, :], two[:, :, 0], two[:, :, 1], ALU.add).then_inc(patch_summed, 1)

            def softmax(u):
                sc = score[:, :].rearrange("p (h s n) -> p h s n", h=2, s=S)
                wg = wgt[:, :].rearrange("p (h s n) -> p h s n", h=2, s=S)

                def spread(a):
                    return a[:, :].rearrange("p (h n) -> p h n", h=2)[:, :, None, :].to_broadcast([P, 2, S, W])

                pool.wait_ge(scores_scaled, u + 1)
                pool.wait_ge(bias_term_ready, u + 1)
                pool.tensor_tensor(sc, sc, spread(cbias), ALU.add).then_inc(scores_biased, 1)
                pool.wait_ge(score_max_spread, u + 1)
                pool.tensor_tensor(sc, sc, spread(smxs), ALU.subtract).then_inc(scores_shifted, 1)
                pool.wait_ge(scores_exp, u + 1)
                pool.wait_ge(weights_turned, u)
                pool.tensor_tensor(wgt[:, :], score[:, :], rstd[:, :], ALU.mult).then_inc(weights_raw, 1)
                pool.wait_ge(weights_raw, u + 1)
                pool.wait_ge(inverse_sum_ready, u + 1)
                pool.tensor_tensor(wg, wg, spread(srz), ALU.mult).then_inc(weights_ready, 1)

            patch_sums(0, 0)
            patch_sums(1, 1)
            softmax(0)

            def step(n, m):
                if not isinstance(n, int) or n + 2 < UNITS:
                    patch_sums(n + 2, (m + 2) % NF)
                if not isinstance(n, int) or n + 1 < UNITS:
                    softmax(n + 1)

            pipeline(pool, step, UNITS)

            pool.wait_ge(rest_in, 16)
            pool.wait_ge(aggregate_mm, 2 * UNITS)
            pool.tensor_copy(w1_high[:, :], w1).then_inc(weights_rounded, 1)
            pool.wait_ge(weights_rounded, 1)
            pool.tensor_tensor(w1_low[:, :], w1, w1_high[:, :].bitcast(F32), ALU.subtract).then_inc(weights_split, 1)

            def combine(i):
                for g in range(G):
                    pool.wait_ge(experts_weighted, G * i + g + 1)
                    pool.wait_ge(gated_summed, count(G * i + g - 1))
                    pr = eprod[:, g % 2, :].rearrange("p (m e c) -> p m e c", m=2, e=E)
                    half = esum2[:, g % 2]
                    pool.tensor_tensor(half, pr[:, :, 0:2], pr[:, :, 2:4], ALU.add).then_inc(half_summed, 1)
                    pool.wait_ge(half_summed, G * i + g + 1)
                    if g == 0:
                        pool.wait_ge(sum_ready, i)
                    pool.tensor_tensor(gsum[:, g * P:(g + 1) * P].rearrange("p (m c) -> p m c", m=2),
                                       half[:, :, 0], half[:, :, 1], ALU.add).then_inc(gated_summed, 1)

            def rows(a):
                return a.rearrange("p (n c) -> p n c", c=C)

            def finish(i, p):
                pool.wait_ge(mean_ready, i + 1)
                pool.tensor_tensor(rows(ycen), rows(ysb), y8[:, 1, :][:, :, None].to_broadcast([P, 8, C]),
                                   ALU.subtract).then_inc(out_centred, 1)
                pool.wait_ge(out_rstd_ready, i + 1)
                pool.wait_ge(stored[p], count((i - p) * (STORE // 2)))
                pool.tensor_tensor(out_t[:, p].rearrange("p a (n c) -> p (a n) c", c=C), rows(ycen),
                                   y8[:, 3, :][:, :, None].to_broadcast([P, 8, C]),
                                   ALU.mult).then_inc(out_ready, 1)

            def mstep(i, p):
                if not isinstance(i, int) or i >= 1:
                    finish(i - 1, (p + 1) % 2)
                combine(i)

            mixture(pool, mstep)
            finish(ITERS - 1, (ITERS - 1) % 2)

        @block.scalar
        def _(act):
            act.preload_act_table_set("natural_log_exp_and_others")
            act.wait_ge(setup_mm, 1)
            act.activation(wqkv[:, :, :].rearrange("p a n -> p (a n)"), banks[0][:, 0:3 * P], ACT.Copy).then_inc(weights_centred, 1)

            def take_means(u, m):
                act.wait_ge(patch_summed, u + 1)
                act.activation(means[:, m, 0, :], sum16[:, :], ACT.Copy, scale=1.0 / N_PIX).then_inc(mean_taken, 1)
                act.activation(means[:, m, 1, :], sum16[:, :], ACT.Square, scale=1.0 / N_PIX).then_inc(mean_taken, 1)

            def q_rstd(u):
                act.wait_ge(q_moments_mm, u + 1)
                act.wait_ge(q_log_ready, u)
                act.activation(qstat[:, :], bank_sq[:, 0:2 * PT], ACT.Square).then_inc(q_mean_squared, 1)
                act.wait_ge(q_variance_ready, u + 1)
                act.activation(qstat[:, :], qstat[:, :], ACT.Ln, bias=eps).then_inc(q_log_ready, 1)
                act.wait_ge(q_log_ready, u + 1)
                act.wait_ge(q_scaled, u)
                act.activation(qrstd[:, :], qstat[:, :], ACT.Exp, scale=-0.5).then_inc(q_rstd_ready, 1)

            def query(u, m):
                act.wait_ge(q_scaled, u + 1)
                act.wait_ge(bias_term_mm, count(u - 1))
                act.wait_ge(keys_times_q, count(8 * u - 8))
                act.activation(qbuf[:, m % 2].rearrange("p b n t -> p (b n) t"),
                               qraw[:, :, None].to_broadcast([P, 2 * PT, S]), ACT.Identity,
                               scale=float(C) ** -0.5, bias=bqkv[:, 0:1]).then_inc(q_ready, 1)

            def squares(u, m, b):
                if b == 0:
                    act.wait_ge(x_in[m], (u - m) * 8 + 32)
                    act.wait_ge(pixel_square_mm, u)
                act.activation(xsq[:, b, :], x[:, m, b, :], ACT.Square).then_inc(pixels_squared, 1)

            def pixel_mean(u):
                act.wait_ge(pixel_mean_mm, u + 1)
                act.wait_ge(rstd_ready, u)
                act.activation(vstat[:, :], bank_mu[:, :], ACT.Square).then_inc(mean_squared, 1)

            def score_bias(u):
                act.wait_ge(bias_term_mm, u + 1)
                act.wait_ge(scores_biased, u)
                act.activation(cbias[:, :].rearrange("p (n t) -> p n t", t=S),
                               ring[0][:, 0:32][:, :, None].to_broadcast([P, 32, S]), ACT.Copy).then_inc(bias_term_ready, 1)

            def pixel_rstd(u):
                act.wait_ge(variance_ready, u + 1)
                act.activation(vstat[:, :], vstat[:, :], ACT.Ln, bias=eps).then_inc(log_ready, 1)
                act.wait_ge(log_ready, u + 1)
                act.wait_ge(weights_raw, u)
                act.activation(rstd[:, :], vstat[:, :], ACT.Exp, scale=-0.5).then_inc(rstd_ready, 1)

            def expo(u):
                act.wait_ge(scores_shifted, u + 1)
                act.activation(score[:, :], score[:, :], ACT.Exp).then_inc(scores_exp, 1)

            def copy_w(u, m):
                act.wait_ge(weights_turned, u + 1)
                act.wait_ge(values_weighted, count(8 * u - 8))
                act.activation(wT[:, m % 2, :], bank_t[:, :], ACT.Copy).then_inc(weights_copied, 1)

            def copy_agg(u):
                act.wait_ge(aggregate_mm, 2 * u + 2)
                act.wait_ge(aggregate_turned, u)
                act.activation(aggr_t[:, :], bank_ag[:, 0:2 * PT], ACT.Copy).then_inc(aggregate_copied, 1)

            def copy_turned(u):
                act.wait_ge(aggregate_turned, u + 1)
                act.wait_ge(projected_mm, u)
                act.activation(aggr[:, :], bank_ag[:, 2 * PT:4 * PT], ACT.Copy).then_inc(aggregate_ready, 1)

            act.wait_ge(const_in, 16)
            squares(0, 0, 0)
            squares(0, 0, 1)
            take_means(0, 0)
            q_rstd(0)
            act.wait_ge(biases_ready, 2)
            query(0, 0)
            pixel_mean(0)
            score_bias(0)
            pixel_rstd(0)
            squares(1, 1, 0)
            squares(1, 1, 1)
            take_means(1, 1)
            q_rstd(1)
            query(1, 1)
            expo(0)
            pixel_mean(1)

            def step(n, m):
                nxt = not isinstance(n, int) or n + 1 < UNITS
                nxt2 = not isinstance(n, int) or n + 2 < UNITS
                prev = not isinstance(n, int) or n >= 1
                if nxt:
                    score_bias(n + 1)
                if prev:
                    copy_agg(n - 1)
                    copy_turned(n - 1)
                if nxt:
                    pixel_rstd(n + 1)
                if nxt2:
                    squares(n + 2, (m + 2) % NF, 0)
                copy_w(n, m)
                if nxt2:
                    squares(n + 2, (m + 2) % NF, 1)
                    take_means(n + 2, (m + 2) % NF)
                    q_rstd(n + 2)
                    query(n + 2, m)
                if nxt:
                    expo(n + 1)
                if nxt2:
                    pixel_mean(n + 2)

            pipeline(act, step, UNITS)
            copy_agg(UNITS - 1)
            copy_turned(UNITS - 1)

            act.wait_ge(coefs, N_COEFS)
            for n in range(2 * N_PIECE):
                act.wait_ge(drive_mm, n + 1)
                act.activation(force[:, piece(0, n)], banks[n % 2][:, :], ACT.Identity,
                               scale=sv[:, SV_F:SV_F + 1], bias=sv[:, SV_FB:SV_FB + 1]).then_inc(force_ready, 1)
            for h in range(2):
                act.preload_act_table(ACT.Gelu)
                for n in range(N_PIECE):
                    act.wait_ge(mixed_mm, N_PIECE * h + n + 1)
                    act.activation(force[:, piece(h, n)], banks[n][:, :], ACT.Gelu,
                                   bias=sv[:, SV_CD:SV_CD + 1]).then_inc(gelu_ready, 1)
                act.preload_act_table(ACT.Silu)
                act.wait_ge(gelu_ready, N_PIECE * (h + 1))
                for n in range(N_RES):
                    a = force[:, piece(h, n, HP // N_RES)]
                    act.activation(a, a, ACT.Silu).then_inc(silu_ready, 1)
            act.preload_act_table_set("natural_log_exp_and_others")

            def norm_sq(i):
                act.wait_ge(centred_mm, i + 1)
                act.wait_ge(norm_variance_mm, i)
                act.activation(sq3, bank_cen[:, :], ACT.Square).then_inc(centred_squared, 1)

            def norm_rstd(i):
                act.wait_ge(norm_variance_mm, i + 1)
                act.wait_ge(normed_ready, i)
                act.activation(ln3, bank_var[:, :], ACT.Ln, bias=eps).then_inc(norm_log_ready, 1)
                act.wait_ge(norm_log_ready, i + 1)
                act.activation(ln3, ln3, ACT.Exp, scale=-0.5).then_inc(norm_rstd_ready, 1)

            def high(i, p):
                act.wait_ge(normed_ready, i + 1)
                for m in range(2):
                    rows = slice(C * m, C * m + C)
                    act.activation(parts[rows, m, :], h2[rows, p], ACT.Copy).then_inc(high_ready, 1)

            def out_sq(i):
                act.wait_ge(out_centred, i + 1)
                act.wait_ge(out_square_sum, i)
                act.activation(ysq, ycen, ACT.Square).then_inc(out_squared, 1)

            def out_rstd(i):
                act.wait_ge(out_square_sum, i + 1)
                act.activation(y8[:, 2, :], y8[:, 2, :], ACT.Ln, scale=1.0 / C, bias=eps).then_inc(out_log_ready, 1)
                act.wait_ge(out_log_ready, i + 1)
                act.wait_ge(out_ready, i)
                act.activation(y8[:, 3, :], y8[:, 2, :], ACT.Exp, scale=-0.5).then_inc(out_rstd_ready, 1)

            norm_sq(0)
            norm_rstd(0)
            high(0, 0)

            def mstep(i, p):
                nxt = not isinstance(i, int) or i + 1 < ITERS
                prev = not isinstance(i, int) or i >= 1
                relu(act, i, 0)
                if nxt:
                    norm_sq(i + 1)
                relu(act, i, 1)
                act.wait_ge(logits_shifted, i + 1)
                act.activation(lgx, lgx, ACT.Exp).then_inc(logits_exp, 1)
                for k in (3, 4, 5, 6):
                    relu(act, i, k)
                act.wait_ge(gates_shifted, i + 1)
                act.activation(pick, pick, ACT.Exp).then_inc(gates_exp, 1)
                relu(act, i, 8)
                if prev:
                    out_sq(i - 1)
                relu(act, i, 9)
                if nxt:
                    norm_rstd(i + 1)
                relu(act, i, 10)
                if prev:
                    out_rstd(i - 1)
                relu(act, i, 11)
                if nxt:
                    high(i + 1, (p + 1) % 2)
                relu(act, i, 13)
                relu(act, i, 14)
                act.wait_ge(routing_turned, i + 1)
                act.activation(wmT[0:32, p, :], bank_var[0:32, 0:P], ACT.Copy).then_inc(routing_copied, 1)

            mixture(act, mstep)
            out_sq(ITERS - 1)
            out_rstd(ITERS - 1)

        @block.tensor
        def _(pe):
            pe.wait_ge(const_in, 16)
            pe.wait_ge(weights_scaled, 3)
            pe.matmul(banks[0][:, 0:3 * P], centre, scaled[:, :],
                      start=True, stop=True).then_inc(setup_mm, 1)
            pe.matmul(banks[1][:, 0:1], raw[:, 0 * P:1 * P], vec(V_LNQB), start=True, stop=True)
            pe.matmul(banks[1][:, 1:2], raw[:, 1 * P:2 * P], vec(V_LNKB), start=True, stop=True)
            pe.matmul(banks[1][:, 2:3], raw[:, 2 * P:3 * P], vec(V_LNKB), start=True, stop=True).then_inc(setup_mm, 1)
            pe.wait_ge(weights_scaled, 4)
            pe.matmul(banks[2][:, 0:1], projw[:, :], bqkv[:, 2:3], start=True, stop=True).then_inc(setup_mm, 1)
            pe.wait_ge(weights_centred, 1)

            def query(u, m):
                pe.wait_ge(mean_taken, 2 * u + 2)
                pe.wait_ge(variance_ready, u)
                pe.wait_ge(mean_squared, u)
                pe.matmul(bank_sq[:, :], ones64, means[:, m].rearrange("p a n -> p (a n)"),
                          start=True, stop=True).then_inc(q_moments_mm, 1)
                pe.matmul(bank_mu[:, 0:2 * PT], wqkv[:, 0, :], means[:, m, 0, :],
                          start=True, stop=True).then_inc(q_raw_mm, 1)

            def head_sums(bank, what, b, src):
                for j in range(NJ):
                    mm = pe.matmul(bank[32 * j:32 * j + 32, :], what, src[:, j * CH:(j + 1) * CH],
                                   start=(b == 0), stop=(b == 1))
                return mm

            def pixel_means(u, m):
                pe.wait_ge(x_in[m], (u - m) * 8 + 32)
                pe.wait_ge(q_scaled, u + 1)
                for b in range(2):
                    mm = head_sums(bank_mu, avg(b), b, x[:, m, b, :])
                mm.then_inc(pixel_mean_mm, 1)

            def pixel_squares(u, m):
                pe.wait_ge(pixels_squared, 2 * u + 2)
                pe.wait_ge(q_variance_ready, u + 1)
                for b in range(2):
                    mm = head_sums(bank_sq, avg(b), b, xsq[:, b, :])
                mm.then_inc(pixel_square_mm, 1)

            def ring_free(u, idx):
                first = isinstance(u, int) and u <= 1
                last = isinstance(u, int) and u == UNITS - 1
                if idx <= 2:
                    if first:
                        pe.wait_ge(keys_times_q, 8 * u)
                    else:
                        pe.wait_ge(values_weighted, count(8 * (u - 2) + 6 + idx))
                elif idx == 3:
                    pe.wait_ge(bias_term_ready, u + 1)
                elif idx < RING_P:
                    pe.wait_ge(keys_times_q, count(8 * u + idx - 3))
                elif idx == RING_P:
                    if isinstance(u, int) and u >= UNITS - 2:
                        pe.wait_ge(values_weighted, 8 * u + 8)
                    else:
                        pe.wait_ge(keys_times_q, 8 * (u + 2) + 6)
                elif idx < RING_V + 2:
                    if last:
                        pe.wait_ge(values_weighted, 8 * u)
                    else:
                        pe.wait_ge(keys_times_q, count(8 * (u + 1) + idx - 3))
                elif idx == RING_V + 2:
                    pe.wait_ge(tokens_ready, u)
                else:
                    pe.wait_ge(values_weighted, count(8 * u + idx - RING_V - 2))

            def bias_term(u, m):
                ring_free(u, 0)
                pe.wait_ge(q_ready, u + 1)
                for j in range(NJ):
                    for b in range(2):
                        mm = pe.matmul(ring[0][32 * j:32 * j + 32, 0:32], indbk[:, 32 * b:32 * b + 32],
                                       qbuf[:, m % 2, b, 32 * j:32 * j + 32, 0], start=(b == 0), stop=(b == 1))
                mm.then_inc(bias_term_mm, 1)

            def keys(u, m, c):
                ring_free(u, RING_K + c)
                b, j = c // NJ, c % NJ
                pe.matmul(ring[(RING_K + c) % 3][:, :], wqkv[:, 1, :], x[:, m, b, j * CH:(j + 1) * CH],
                          start=True, stop=True).then_inc(keys_mm, 1)

            def scores(u, b):
                pe.wait_ge(keys_times_q, 8 * u + 4 * b + 4)
                if b == 0:
                    pe.wait_ge(scores_scaled, u)
                head_sums(bank_s, ind(b), b, prodk[:, b, :]).then_inc(scores_mm, 1)

            def turn_weights(u):
                pe.wait_ge(weights_ready, u + 1)
                pe.wait_ge(weights_copied, u)
                for r in range(4):
                    mm = pe.transpose(bank_t[:, r * P:(r + 1) * P], wgt[:, r * P:(r + 1) * P], eye)
                mm.then_inc(weights_turned, 1)

            def values(u, m, c):
                ring_free(u, RING_V + c)
                b, j = c // NJ, c % NJ
                for r in range(4):
                    at = j * CH + r * P
                    mm = pe.matmul(ring[(RING_V + c) % 3][:, r * P:(r + 1) * P], x[:, m, b, at:at + P],
                                   wqkv[:, 2, :], start=True, stop=True)
                mm.then_inc(values_mm, 1)

            def aggregate(u, b):
                pe.wait_ge(values_weighted, 8 * u + 4 * b + 4)
                if b == 0:
                    pe.wait_ge(aggregate_ready, u)
                for r in range(2):
                    for j in range(NJ):
                        rows = prodv[:, NJ * b + j, :].rearrange("p (h r k) -> p r h k", h=2, r=2)
                        mm = pe.matmul(bank_ag[32 * j:32 * j + 32, 0:2 * PT], patch(b), rows[:, r],
                                       start=(b == 0 and r == 0), stop=(b == 1 and r == 1))
                mm.then_inc(aggregate_mm, 1)

            def turn_aggregate(u):
                pe.wait_ge(aggregate_copied, u + 1)
                for h in range(2):
                    mm = pe.transpose(bank_ag[:, (2 + h) * PT:(3 + h) * PT], aggr_t[:, h * P:(h + 1) * P], eye)
                mm.then_inc(aggregate_turned, 1)

            def project(u):
                ring_free(u, RING_P)
                pe.wait_ge(aggregate_ready, u + 1)
                by_pair = aggr[:, :].rearrange("p (h j b w) -> p b j h w", h=2, j=NJ, b=2)
                for b in range(2):
                    mm = pe.matmul(ring[RING_P % 3][:, b * PT:(b + 1) * PT], projw[:, :], by_pair[:, b],
                                   start=True, stop=True)
                mm.then_inc(projected_mm, 1)

            pe.wait_ge(weights_scaled, 5)
            query(0, 0)
            pixel_means(0, 0)
            pixel_squares(0, 0)
            bias_term(0, 0)
            for c in range(8):
                keys(0, 0, c)
            scores(0, 0)
            scores(0, 1)
            query(1, 1)
            pixel_means(1, 1)
            pixel_squares(1, 1)

            def step(n, m):
                prev = not isinstance(n, int) or n >= 1
                nxt = not isinstance(n, int) or n + 1 < UNITS
                nxt2 = not isinstance(n, int) or n + 2 < UNITS
                m1, m2 = (m + 1) % NF, (m + 2) % NF
                if nxt:
                    bias_term(n + 1, m1)
                    keys(n + 1, m1, 0)
                    keys(n + 1, m1, 1)
                if prev:
                    turn_aggregate(n - 1)
                if nxt:
                    for c in range(2, 5):
                        keys(n + 1, m1, c)
                turn_weights(n)
                if nxt:
                    for c in range(5, 8):
                        keys(n + 1, m1, c)
                if prev:
                    project(n - 1)
                if nxt:
                    scores(n + 1, 0)
                for c in range(8):
                    values(n, m, c)
                    if c == 0 and nxt2:
                        query(n + 2, m2)
                    if c == 1 and nxt:
                        scores(n + 1, 1)
                    if c == 4 and nxt2:
                        pixel_means(n + 2, m2)
                    if c == 5:
                        aggregate(n, 0)
                if nxt2:
                    pixel_squares(n + 2, m2)
                aggregate(n, 1)

            pipeline(pe, step, UNITS)
            turn_aggregate(UNITS - 1)
            project(UNITS - 1)

            pe.wait_ge(tokens_ready, UNITS)
            pe.wait_ge(rest_in, 16)
            for n in range(2 * N_PIECE):
                pe.wait_ge(force_ready, count(n - 1))
                pe.matmul(banks[n % 2][:, :], wssm[:, 0, :], tokens_at(n // N_PIECE, n % N_PIECE, 2),
                          start=True, stop=True).then_inc(drive_mm, 1)

            def direct(h, n):
                if h == 0:
                    pe.wait_ge(force_ready, 2 * N_PIECE)
                else:
                    pe.wait_ge(gelu_ready, n + 1)
                pe.matmul(banks[n][:, :], wssm[:, 2, :], tokens_at(h, n, 2), start=True, stop=False)

            for n in range(N_PIECE):
                direct(0, n)
            for h in range(2):
                for n in range(N_PIECE):
                    pe.wait_ge(chunk_fixed[h], fixed(2 * n + 1))
                    pe.matmul(banks[n][:, :], wssm[:, 1, :], z[:, piece(h, n)],
                              start=False, stop=True).then_inc(mixed_mm, 1)
                    if h == 0 and n > 0:
                        direct(1, n - 1)
                if h == 0:
                    direct(1, N_PIECE - 1)

            def centre_rows(i):
                pe.wait_ge(normed_ready, i)
                if isinstance(i, int) and i == 1:
                    pe.wait_ge(residual_ready, 2 * N_RES)
                pe.matmul(bank_cen[:, :], centre, chunk(hT[:, :], i), start=True, stop=True).then_inc(centred_mm, 1)

            def variance(i):
                pe.wait_ge(centred_squared, i + 1)
                pe.wait_ge(logits_biased, i)
                pe.matmul(bank_var[:, :], ones64, sq3, start=True, stop=True).then_inc(norm_variance_mm, 1)

            def split(w, rows):
                return (w1_high[:, w], rows, True, False), (w1_low[:, w], rows, False, True)

            def logits(i, p):
                pe.wait_ge(normed_ready, i + 1)
                pe.wait_ge(norm_log_ready, i + 1)
                pe.wait_ge(routing_copied, i)
                for g in range(G):
                    mm = pe.matmul(bank_var[:, 8 * g:8 * g + 8], h2[:, p, tokens_of(g)], gw[:, :],
                                   start=True, stop=True)
                mm.then_inc(logits_mm, 1)

            def ring_use(i, k):
                pe.wait_ge(hidden_ready[k % RING], RELUS // RING * i + k // RING)
                if k in (3, 4):
                    pe.wait_ge(experts_weighted, count(G * i + k - 4))
                return hidden_ring[k % RING]

            def hidden(i, k):
                pe.wait_ge(hidden_ready[k % RING], RELUS // RING * i + k // RING + 1)

            def mstep(i, p):
                nxt = not isinstance(i, int) or i + 1 < ITERS
                if nxt:
                    centre_rows(i + 1)
                pe.wait_ge(high_ready, 2 * i + 2)
                pe.wait_ge(low_ready, 2 * i + 2)
                bank = ring_use(i, 0)
                for m in range(2):
                    at = W1_S + C - C * m
                    for w, rows, start, stop in split(slice(at, at + P), parts[:, m, :]):
                        mm = pe.matmul(bank[:, :], w, rows, start=start and m == 0, stop=stop and m == 1)
                mm.then_inc(hidden_mm, 1)
                for k in range(1, 9):
                    m, e = (k - 1) // E, (k - 1) % E
                    bank = ring_use(i, k)
                    for w, rows, start, stop in split(slice(e * P, e * P + P), parts[:, m, :]):
                        mm = pe.matmul(bank[:, :], w, rows, start=start, stop=stop)
                    mm.then_inc(hidden_mm, 1)
                if nxt:
                    variance(i + 1)
                for k in range(9, 11):
                    hidden(i, 0)
                    pe.matmul(ring_use(i, k)[:, :], sw2[:, k - 9, :], h1s,
                              start=True, stop=True).then_inc(hidden_mm, 1)
                for k in range(11, 15):
                    im, q = (k - 11) // 2, (k - 11) % 2
                    bank = ring_use(i, k)
                    for h in range(2):
                        hidden(i, 1 + E * im + 2 * q + h)
                        mm = pe.matmul(bank[C * h:C * h + C, :], ew2[:, 2 * q + h, :], h1e[:, im, 2 * q + h],
                                       start=True, stop=True)
                    mm.then_inc(hidden_mm, 1)
                pe.wait_ge(routing_ready, i + 1)
                if nxt:
                    pe.wait_ge(norm_log_ready, i + 2)
                else:
                    pe.wait_ge(logits_biased, i + 1)
                pe.transpose(bank_var[0:32, 0:P], wmoe, eye).then_inc(routing_turned, 1)
                pe.wait_ge(sum_ready, i)
                hidden(i, 9)
                hidden(i, 10)
                for g in range(G):
                    toks = tokens_of(g)
                    pe.matmul(bank_base[:, g * P:(g + 1) * P], h2[:, p, toks], eye, start=(g == 0), stop=False,
                              skip_group_check=True)
                    for im in range(2):
                        pe.matmul(bank_base[:, g * P + C * im:g * P + C * im + C], h2s[:, im, toks], sw3[:, :],
                                  start=False, stop=False, skip_group_check=True)
                pe.wait_ge(routing_copied, i + 1)
                for k in range(11, 15):
                    hidden(i, k)
                for g in range(G):
                    toks = tokens_of(g)
                    pe.wait_ge(experts_weighted, count(G * i + g - 1))
                    for im in range(2):
                        for q in range(2):
                            at = im * 256 + q * P
                            mm = pe.matmul(bank_o[g % 2][:, at:at + P], h2e[:, im, q, toks], ew3[:, q, :],
                                           start=True, stop=True)
                    mm.then_inc(experts_mm, 1)
                    mm = pe.matmul(bank_base[:, g * P:(g + 1) * P], wmT[0:33, p, :], b3[0:33, g, :],
                                   start=False, stop=True, skip_group_check=True)
                mm.then_inc(base_done, 1)
                if nxt:
                    logits(i + 1, (p + 1) % 2)

            pe.wait_ge(residual_ready, N_RES)
            pe.wait_ge(gelu_ready, 2 * N_PIECE)
            pe.wait_ge(ones_row, 1)
            pe.wait_ge(weights_split, 1)
            centre_rows(0)
            variance(0)
            logits(0, 0)
            mixture(pe, mstep)

        @block.vector
        def _(dve):
            n_coefs = [0]

            def link(ins):
                n_coefs[0] += 1
                ins.then_inc(coefs, 1)
                dve.wait_ge(coefs, n_coefs[0])

            dve.memset(wmT[32:33, :, :], 1.0).then_inc(ones_row, 1)
            dve.wait_ge(tok_in, 16)
            for n, v in ((0, V_LNQW), (1, V_LNKW), (2, V_LNKW)):
                dve.tensor_scalar(scaled[:, n * P:(n + 1) * P], raw[:, n * P:(n + 1) * P], vec(v), None,
                                  ALU.mult).then_inc(weights_scaled, 1)
            def svc(n):
                return sv[:, n:n + 1]

            link(dve.tensor_scalar(svc(SV_A), vec(V_A), DT * DT, None, ALU.mult))
            link(dve.tensor_scalar(svc(SV_S), svc(SV_A), 1.0, None, ALU.add))
            link(dve.reciprocal(svc(SV_S), svc(SV_S)))
            link(dve.scalar_tensor_tensor(svc(SV_NM), svc(SV_A), -1.0, svc(SV_S), ALU.mult, ALU.mult))
            link(dve.tensor_scalar(svc(SV_F), svc(SV_S), DT * DT, None, ALU.mult))
            link(dve.tensor_tensor(svc(SV_FB), svc(SV_F), vec(V_BB), ALU.mult))
            link(dve.tensor_tensor(svc(SV_CD), vec(V_BC), vec(V_BD), ALU.add))
            link(dve.tensor_scalar(svc(SV_NS), svc(SV_S), -1.0, None, ALU.mult))
            link(dve.tensor_scalar(svc(SV_G), svc(SV_S), 1.0, None, ALU.add))
            link(dve.tensor_tensor(svc(SV_G), svc(SV_G), svc(SV_NM), ALU.add))
            for a, n in ((cz, 0), (cz, 1), (cv, 0), (cv, 1)):
                link(dve.memset(a[:, 0, n:n + 1], float((a is cz) == (n == 0))))
            for j in range(L):
                link(dve.tensor_scalar(cacc[:, :], cz[:, j, :], svc(SV_NM), None, ALU.mult))
                link(dve.scalar_tensor_tensor(cv[:, j + 1, :], cv[:, j, :], svc(SV_S), cacc[:, :], ALU.mult, ALU.add))
                link(dve.tensor_tensor(cz[:, j + 1, :], cz[:, j, :], cv[:, j + 1, :], ALU.add))
            assert n_coefs[0] == N_COEFS

            dve.wait_ge(setup_mm, 2)
            dve.tensor_copy(bqkv[:, 1:3], banks[1][:, 1:3]).then_inc(biases_ready, 1)
            dve.tensor_scalar(bqkv[:, 0:1], banks[1][:, 0:1], float(C) ** -0.5, None, ALU.mult).then_inc(biases_ready, 1)
            dve.wait_ge(biases_ready, 2)
            dve.wait_ge(const_in, 16)
            dve.tensor_scalar(indbk[:, :], const[:, K_IND:K_AVG], bqkv[:, 1:2], None, ALU.mult).then_inc(weights_scaled, 1)
            dve.wait_ge(setup_mm, 3)
            dve.tensor_tensor(bqkv[:, 3:4], banks[2][:, 0:1], vec(V_PROJB), ALU.add).then_inc(weights_scaled, 1)

            def query_var(u):
                dve.wait_ge(q_mean_squared, u + 1)
                dve.tensor_tensor(qstat[:, :], bank_sq[:, 2 * PT:4 * PT], qstat[:, :], ALU.subtract).then_inc(q_variance_ready, 1)

            def query_scaled(u):
                dve.wait_ge(q_rstd_ready, u + 1)
                dve.wait_ge(q_raw_mm, u + 1)
                dve.wait_ge(q_ready, u)
                dve.tensor_tensor(qraw[:, :], bank_mu[:, 0:2 * PT], qrstd[:, :], ALU.mult).then_inc(q_scaled, 1)

            def pixel_var(u):
                dve.wait_ge(mean_squared, u + 1)
                dve.wait_ge(pixel_square_mm, u + 1)
                dve.tensor_tensor(vstat[:, :], bank_sq[:, :], vstat[:, :], ALU.subtract).then_inc(variance_ready, 1)

            def key_products(u, m, c):
                b, j = c // NJ, c % NJ
                dve.wait_ge(keys_mm, 8 * u + c + 1)
                if c == 0:
                    dve.wait_ge(q_ready, u + 1)
                if j == 0:
                    dve.wait_ge(scores_mm, count(2 * u - 1 + b))
                shape = "p (h s n) -> p h s n"
                q = qbuf[:, m % 2, b, 32 * j:32 * j + 32, :].rearrange("p (h w) t -> p h (w t)", h=2)
                dve.tensor_tensor(prodk[:, b, j * CH:(j + 1) * CH].rearrange(shape, h=2, s=S),
                                  ring[(RING_K + c) % 3][:, :].rearrange(shape, h=2, s=S),
                                  q[:, :, None, :].to_broadcast([P, 2, S, W]),
                                  ALU.mult).then_inc(keys_times_q, 1)

            def score_scale(u):
                dve.wait_ge(scores_mm, 2 * u + 2)
                dve.wait_ge(rstd_ready, u + 1)
                dve.wait_ge(weights_raw, u)
                dve.tensor_tensor(score[:, :], bank_s[:, :], rstd[:, :], ALU.mult).then_inc(scores_scaled, 1)

            def by_patch(a):
                return a[:, :].rearrange("p (h s w t) -> p h w s t", h=2, s=S, w=16)

            def score_max(u):
                dve.wait_ge(scores_biased, u + 1)
                dve.tensor_reduce(smx[:, :].rearrange("p (h w) -> p h w", h=2), by_patch(score), AX.XY,
                                  ALU.max).then_inc(score_max_ready, 1)
                dve.wait_ge(score_max_ready, u + 1)
                dve.tensor_copy(smxs[:, :].rearrange("p (n t) -> p n t", t=S),
                                smx[:, :, None].to_broadcast([P, 32, S])).then_inc(score_max_spread, 1)

            def score_sum(u):
                dve.wait_ge(scores_exp, u + 1)
                dve.tensor_reduce(ssm[:, :].rearrange("p (h w) -> p h w", h=2), by_patch(score), AX.XY,
                                  ALU.add).then_inc(exp_summed, 1)

            def score_inverse(u):
                dve.wait_ge(exp_summed, u + 1)
                dve.wait_ge(weights_ready, u)
                dve.reciprocal(smx[:, :], ssm[:, :]).then_inc(sum_inverted, 1)
                dve.wait_ge(sum_inverted, u + 1)
                dve.tensor_copy(srz[:, :].rearrange("p (n t) -> p n t", t=S),
                                smx[:, :, None].to_broadcast([P, 32, S])).then_inc(inverse_sum_ready, 1)

            def value_products(u, m, c):
                b, j = c // NJ, c % NJ
                dve.wait_ge(values_mm, 8 * u + c + 1)
                if c == 0:
                    dve.wait_ge(weights_copied, u + 1)
                if j == 0:
                    dve.wait_ge(aggregate_mm, count(2 * u - 1 + b))
                k = wT[:, m % 2, :].rearrange("p (r k) -> p r k", r=4)[:, :, 32 * j + 16 * b:32 * j + 16 * b + 16]
                shape = "p (r k d) -> p r k d"
                dve.tensor_tensor(prodv[:, c, :].rearrange(shape, r=4, d=D),
                                  ring[(RING_V + c) % 3][:, :].rearrange(shape, r=4, d=D),
                                  k[:, :, :, None].to_broadcast([P, 4, 16, D]), ALU.mult).then_inc(values_weighted, 1)

            def tokens(u, m):
                dve.wait_ge(projected_mm, u + 1)
                half = m % 2
                pairs = hT[:, :].rearrange("p (g b n) -> p g b n", b=2, n=HW)
                dst = pairs[:, (u - half) // 2, :, half * PT:(half + 1) * PT]
                dve.scalar_tensor_tensor(dst, ring[RING_P % 3][:, 0:2 * PT].rearrange("p (b n) -> p b n", b=2),
                                         bqkv[:, 3:4], means[:, m, 0, :].rearrange("p (b n) -> p b n", b=2),
                                         ALU.add, ALU.add).then_inc(tokens_ready, 1)

            query_var(0)
            query_scaled(0)
            pixel_var(0)
            for c in range(8):
                key_products(0, 0, c)
            score_scale(0)
            query_var(1)
            score_max(0)
            query_scaled(1)
            score_sum(0)
            score_inverse(0)

            def step(n, m):
                nxt = not isinstance(n, int) or n + 1 < UNITS
                nxt2 = not isinstance(n, int) or n + 2 < UNITS
                m1 = (m + 1) % NF
                if nxt:
                    pixel_var(n + 1)
                if nxt:
                    for c in range(8):
                        key_products(n + 1, m1, c)
                if not isinstance(n, int) or n >= 1:
                    tokens(n - 1, (m - 1) % NF)
                for c in range(8):
                    value_products(n, m, c)
                    if c == 0 and nxt2:
                        query_var(n + 2)
                    if c == 1 and nxt:
                        score_scale(n + 1)
                    if c == 2 and nxt2:
                        query_scaled(n + 2)
                    if c == 4 and nxt:
                        score_max(n + 1)
                if nxt:
                    score_sum(n + 1)
                    score_inverse(n + 1)

            pipeline(dve, step, UNITS)
            tokens(UNITS - 1, (UNITS - 1) % NF)

            def scan_first(h):
                dve.wait_ge(force_ready, N_PIECE * h + 1)
                dve.tensor_copy(z[:, at(h, 0)], force[:, at(h, 0)]).then_inc(scan_step[h], 1)

            def scan_ahead(h, j):
                dve.wait_ge(scan_step[h], 2 * j - 1)
                if j + 1 < L:
                    dve.wait_ge(force_ready, N_PIECE * h + (j + 1) // 2 + 1)
                    dve.scalar_tensor_tensor(force[:, at(h, j + 1)], z[:, at(h, j - 1)], sv[:, SV_NS:SV_NS + 1],
                                             force[:, at(h, j + 1)], ALU.mult, ALU.add).then_inc(scan_step[h], 1)

            def scan_on(h, j):
                dve.wait_ge(scan_step[h], 2 * j - 1)
                dve.scalar_tensor_tensor(z[:, at(h, j)], z[:, at(h, j - 1)], sv[:, SV_G:SV_G + 1], force[:, at(h, j)],
                                         ALU.mult, ALU.add).then_inc(scan_step[h], 1)

            def seqs(a, h):
                return a[:, h * HS:(h + 1) * HS]

            def start(a, c):
                return a.rearrange("p (n c) -> p n c", c=NCK)[:, :, c]

            def scan_last(h):
                dve.wait_ge(scan_step[h], 2 * L - 2)
                dve.tensor_tensor(seqs(vel, h), z[:, at(h, L - 1)], z[:, at(h, L - 2)],
                                  ALU.subtract).then_inc(scan_step[h], 1)
                dve.memset(start(seqs(zin, h), 0), 0.0).then_inc(carry_step[h], 1)
                dve.memset(start(seqs(vin, h), 0), 0.0).then_inc(carry_step[h], 1)

            def tmp(h, o):
                return ctmp[:, (2 * h + o) * (PAIRS // 2):(2 * h + o + 1) * (PAIRS // 2)]

            def carry_from(h, c):
                dve.wait_ge(scan_step[h], 2 * L - 1)
                dve.wait_ge(carry_step[h], 4 * c + 2)
                for o, (coef, loc) in enumerate(((cz, z[:, at(h, L - 1)]), (cv, seqs(vel, h)))):
                    dve.scalar_tensor_tensor(tmp(h, o), start(seqs(zin, h), c), coef[:, L, 0:1], start(loc, c),
                                             ALU.mult, ALU.add).then_inc(carry_step[h], 1)

            def carry_to(h, c):
                for o, (coef, dst) in enumerate(((cz, zin), (cv, vin))):
                    dve.wait_ge(carry_step[h], 4 * c + 4)
                    dve.scalar_tensor_tensor(start(seqs(dst, h), c + 1), start(seqs(vin, h), c), coef[:, L, 1:2], tmp(h, o),
                                             ALU.mult, ALU.add).then_inc(carry_step[h], 1)

            def fix_z(h, j):
                dve.wait_ge(carry_step[h], 4 * NCK - 2)
                dve.scalar_tensor_tensor(z[:, at(h, j)], seqs(zin, h), cz[:, j + 1, 0:1], z[:, at(h, j)],
                                         ALU.mult, ALU.add).then_inc(chunk_fixed[h], 1)

            def fix_v(h, j):
                dve.wait_ge(chunk_fixed[h], max(2 * j, 1))
                dve.scalar_tensor_tensor(z[:, at(h, j)], seqs(vin, h), cz[:, j + 1, 1:2], z[:, at(h, j)],
                                         ALU.mult, ALU.add).then_inc(chunk_fixed[h], 1)

            def residual(h):
                for n in range(N_RES):
                    dve.wait_ge(silu_ready, N_RES * h + n + 1)
                    dst = tokens_at(h, n, L // N_RES)
                    out = force[:, piece(h, n, HP // N_RES)].rearrange("p (j n) -> p j n", n=HS)
                    dve.scalar_tensor_tensor(dst, dst, 2.0, out, ALU.mult, ALU.add).then_inc(residual_ready, 1)

            scan_first(0)
            for j in range(1, L):
                scan_ahead(0, j)
                scan_on(0, j)
            scan_last(0)
            scan_first(1)
            for j in range(1, L):
                carry_from(0, j - 1)
                scan_ahead(1, j)
                carry_to(0, j - 1)
                scan_on(1, j)
            scan_last(1)
            for j in range(L):
                if j < NCK - 1:
                    carry_from(1, j)
                fix_z(0, j)
                if j < NCK - 1:
                    carry_to(1, j)
                if j > 0:
                    fix_v(0, j - 1)
            fix_v(0, L - 1)
            for j in range(L):
                fix_z(1, j)
                if j > 0:
                    fix_v(1, j - 1)
            fix_v(1, L - 1)
            residual(0)
            residual(1)

            def normed(i, p):
                dve.wait_ge(norm_rstd_ready, i + 1)
                dve.wait_ge(base_done, count(i - 1))
                dve.tensor_tensor(h2[:, p, :], bank_cen[:, :], ln3, ALU.mult).then_inc(normed_ready, 1)

            def low(i, p):
                dve.wait_ge(high_ready, 2 * i + 2)
                for m in range(2):
                    rows, other = slice(C * m, C * m + C), slice(C - C * m, P - C * m)
                    dve.tensor_tensor(parts[other, m, :], h2[rows, p], parts[rows, m, :].bitcast(F32),
                                      ALU.subtract).then_inc(low_ready, 1)

            def by_row(a):
                return a.rearrange("p (n e) -> p n e", e=E)

            def spread(a):
                return a[:, :, None].to_broadcast([P, 8, E])

            def routing(i):
                mx = l8[:, 0, :]
                dve.wait_ge(logits_mm, i + 1)
                dve.tensor_tensor(by_row(lg), by_row(bank_var[:, 0:32]), gbias[:, None, :].to_broadcast([P, 8, E]),
                                  ALU.add).then_inc(logits_biased, 1)
                dve.wait_ge(logits_biased, i + 1)
                dve.tensor_reduce(mx, by_row(lg), AX.X, ALU.max).then_inc(logits_max, 1)
                dve.wait_ge(logits_max, i + 1)
                dve.tensor_tensor(by_row(lgx), by_row(lg), spread(mx), ALU.subtract).then_inc(logits_shifted, 1)

            def gates(i):
                mx, sm, rc, m1 = (l8[:, n, :] for n in range(4))
                dve.wait_ge(logits_exp, i + 1)
                dve.tensor_reduce(sm, by_row(lgx), AX.X, ALU.add).then_inc(logits_sum, 1)
                dve.wait_ge(logits_sum, i + 1)
                dve.reciprocal(rc, sm).then_inc(logits_inverse, 1)
                dve.wait_ge(logits_inverse, i + 1)
                dve.tensor_tensor(by_row(gat), by_row(lgx), spread(rc), ALU.mult).then_inc(gates_ready, 1)
                dve.wait_ge(gates_ready, i + 1)
                dve.tensor_reduce(m1, by_row(gat), AX.X, ALU.max).then_inc(gate_max, 1)
                dve.wait_ge(gate_max, i + 1)
                dve.tensor_tensor(by_row(pick), by_row(gat), spread(m1), ALU.subtract).then_inc(gates_shifted, 1)
                own = by_row(gat)[:, :, :, None].to_broadcast([P, 8, E, E])
                other = by_row(gat)[:, :, None, :].to_broadcast([P, 8, E, E])
                square = "p (n e f) -> p n e f"
                up = const[:, K_UP:K_EPS].rearrange("p (e f) -> p e f", f=E)[:, None, :, :].to_broadcast([P, 8, E, E])
                bt, ti = beat.rearrange(square, e=E, f=E), tie.rearrange(square, e=E, f=E)
                dve.tensor_tensor(bt, other, own, ALU.is_ge).then_inc(gates_compared, 1)
                dve.tensor_tensor(ti, other, own, ALU.is_equal).then_inc(ties_found, 1)
                dve.wait_ge(ties_found, i + 1)
                dve.tensor_tensor(ti, ti, up, ALU.mult).then_inc(ties_counted, 1)
                dve.wait_ge(ties_counted, i + 1)
                dve.tensor_tensor(beat, beat, tie, ALU.subtract).then_inc(wins_ready, 1)
                dve.wait_ge(wins_ready, i + 1)
                dve.tensor_reduce(by_row(lg), bt, AX.X, ALU.add).then_inc(rank_ready, 1)

            def chosen(i):
                tot, inv = l8[:, 4, :], l8[:, 5, :]
                dve.wait_ge(rank_ready, i + 1)
                dve.wait_ge(gates_exp, i + 1)
                dve.scalar_tensor_tensor(pick, lg, 1.5, pick, ALU.is_lt, ALU.mult).then_inc(picked, 1)
                dve.wait_ge(picked, i + 1)
                dve.tensor_reduce(tot, by_row(pick), AX.X, ALU.add).then_inc(picked_sum, 1)
                dve.wait_ge(picked_sum, i + 1)
                dve.reciprocal(inv, tot).then_inc(picked_inverse, 1)
                dve.wait_ge(picked_inverse, i + 1)
                dve.tensor_tensor(by_row(wmoe), by_row(pick), spread(inv), ALU.mult).then_inc(routing_ready, 1)

            def weigh(i, g):
                dve.wait_ge(experts_mm, G * i + g + 1)
                dve.wait_ge(half_summed, count(G * i + g - 1))
                w8 = wmoe[:, 8 * g:8 * g + 8][:, :, None].to_broadcast([P, 8, C])
                dve.tensor_tensor(eprod[:, g % 2, :].rearrange("p (n c) -> p n c", c=C),
                                  bank_o[g % 2][:, :].rearrange("p (n c) -> p n c", c=C), w8,
                                  ALU.mult).then_inc(experts_weighted, 1)

            def rows(a):
                return a.rearrange("p (n c) -> p n c", c=C)

            def total(i):
                dve.wait_ge(base_done, i + 1)
                dve.wait_ge(gated_summed, G * i + G)
                dve.wait_ge(out_centred, i)
                dve.tensor_tensor(ysb, bank_base[:, :], gsum, ALU.add).then_inc(sum_ready, 1)
                dve.wait_ge(sum_ready, i + 1)
                dve.tensor_reduce(y8[:, 0, :], rows(ysb), AX.X, ALU.add).then_inc(sum_added, 1)
                dve.wait_ge(sum_added, i + 1)
                dve.tensor_scalar(y8[:, 1, :], y8[:, 0, :], 1.0 / C, None, ALU.mult).then_inc(mean_ready, 1)

            def square_sum(i):
                dve.wait_ge(out_squared, i + 1)
                dve.wait_ge(out_rstd_ready, i)
                dve.tensor_reduce(y8[:, 2, :], rows(ysq), AX.X, ALU.add).then_inc(out_square_sum, 1)

            normed(0, 0)
            low(0, 0)

            def mstep(i, p):
                prev = not isinstance(i, int) or i >= 1
                routing(i)
                relu(dve, i, 2)
                if prev:
                    total(i - 1)
                gates(i)
                relu(dve, i, 7)
                chosen(i)
                if prev:
                    square_sum(i - 1)
                if not isinstance(i, int) or i + 1 < ITERS:
                    normed(i + 1, (p + 1) % 2)
                relu(dve, i, 12)
                if not isinstance(i, int) or i + 1 < ITERS:
                    low(i + 1, (p + 1) % 2)
                for g in range(G):
                    weigh(i, g)

            mixture(dve, mstep)
            total(ITERS - 1)
            square_sum(ITERS - 1)


_OUT = (B, HW, C)


def _blocks(out, cols, w):
    out[0:C, cols:cols + C] = w
    out[C:P, cols + C:cols + 2 * C] = w


def _tokenizer_pack(a):
    out = np.zeros((P, T_END), np.float32)
    wkv = a["L0_tok_Wkv"]
    for n, w in enumerate((a["L0_tok_Wq"], wkv[0:C], wkv[C:2 * C], a["L0_tok_proj_w"])):
        _blocks(out, T_RAW + n * P, w.T)
    for n, name in enumerate(("tok_ln_q_w", "tok_ln_q_b", "tok_ln_kv_w", "tok_ln_kv_b", "tok_proj_b",
                              "attn_a", "attn_b_B", "attn_b_C", "attn_b_D")):
        for i in range(2):
            out[C * i:C * i + C, T_VEC + n] = a["L0_" + name]
    return out


def _rest_pack(a):
    out = np.zeros((P, R_END), np.float32)
    for n, name in enumerate("BCD"):
        _blocks(out, R_SSM + n * P, a["L0_attn_W_" + name].T)
    out[:, R_SW3:R_EW2] = a["L0_ffn_sW3"]
    for i in range(2):
        r = slice(C * i, C * i + C)
        out[r, R_SW2 + i * P:R_SW2 + (i + 1) * P] = a["L0_ffn_sW2"]
        out[r, R_GW + E * i:R_GW + E * i + E] = a["L0_ffn_gW"]
        out[r, R_SW1 + C:R_SW1 + 2 * C] = a["L0_ffn_sW1"]
        out[r, R_EB + 6] = a["L0_ffn_sb1"]
        for e in range(E):
            at = R_EW1 + e * P
            out[r, at:at + P] = a["L0_ffn_eW1"][e]
        for q in range(2):
            at = R_EW3 + q * P + C * i
            out[r, at:at + C] = a["L0_ffn_eW3"][2 * q + i]
            out[r, R_EB + 4 + q] = a["L0_ffn_eb2"][2 * q + i]
        for g in range(G):
            at = R_B3 + g * P + C * i
            out[8 * g + E * i:8 * g + E * i + E, at:at + C] = a["L0_ffn_eb3"]
            out[32, at:at + C] = a["L0_ffn_sb3"]
    for e in range(E):
        out[:, R_EW2 + e * C:R_EW2 + (e + 1) * C] = a["L0_ffn_eW2"][e]
        out[:, R_EB + e] = a["L0_ffn_eb1"][e]
    out[:, R_GB:R_EB] = a["L0_ffn_gb"]
    out[:, R_EB + 7] = a["L0_ffn_sb2"]
    return out


def kernel(**inputs):
    import concourse.bacc as _bacc
    from concourse.bass_utils import run_bass_kernel_spmd as _run

    a = {n: np.asarray(v) for n, v in inputs.items()}
    arrays = {
        "x": np.ascontiguousarray(a["x"]).reshape(PAIRS, P, H * W),
        "tok_w": _tokenizer_pack(a),
        "rest_w": _rest_pack(a),
        "const": shape_constants(),
    }
    nc = _bacc.Bacc("TRN2", target_bir_lowering=False, num_devices=1)
    t = {n: nc.dram_tensor(n, v.shape, F32, kind="ExternalInput").ap() for n, v in arrays.items()}
    t["out"] = nc.dram_tensor("out", (PAIRS, 2, HW, C), F32, kind="ExternalOutput").ap()
    build(nc, t)
    r = _run(nc, [arrays], core_ids=[0])
    return np.asarray(r.results[0]["out"]).reshape(_OUT)
```

```python
from contextlib import ExitStack

import numpy as np

import concourse.bass as bass
from concourse import mybir

ALU = mybir.AluOpType
ACT = mybir.ActivationFunctionType
AX = mybir.AxisListType
F32 = mybir.dt.float32
F32R = mybir.dt.float32r

P = 128
B, C, H, W = 64, 64, 64, 64
S = 4
N_PIX = S * S
HEADS = 8
D = C // HEADS
HW = (H // S) * (W // S)
PAIRS = B // 2
UNITS = PAIRS
PX = H * W // 2
PT = HW // 2
CH = 512
NJ = PX // CH
E = 4
NF = 4
DT = 1.0 / HW
L = 16
NCK = HW // L
EPS = 1e-5
ITERS = PAIRS // 2
G = 2 * HW // P

K_ONES, K_CEN, K_EYE, K_IND, K_AVG, K_PATCH, K_UP, K_EPS, K_SEL, K_END = 0, 128, 256, 384, 448, 512, 576, 592, 593, 1105
V_LNQW, V_LNQB, V_LNKW, V_LNKB, V_PROJB, V_A, V_BB, V_BC, V_BD, N_VEC = range(10)
T_RAW, T_PROJ, T_VEC, T_END = 0, 384, 512, 512 + N_VEC
R_SSM, R_EW1, R_SW1, R_B3, R_SW2, R_GW, R_SW3, R_EW2, R_EW3, R_GB, R_EB, R_END = (
    0, 384, 896, 1088, 1216, 1344, 1376, 1440, 1696, 1824, 1828, 1837)
W1 = R_GW - R_EW1
W1_S, W1_B, W1_S2 = R_SW1 - R_EW1, R_B3 - R_EW1, R_SW2 - R_EW1
LOW = 32
N_ROUTE = LOW + 2 * E
SV_A, SV_S, SV_NM, SV_F, SV_FB, SV_CD, SV_NS, SV_G, N_SV = range(9)
N_COEFS = 14 + 3 * L
HP = PAIRS * HW // 2
HS = HP // L
N_PIECE = HP // CH
STORE = 4 * 16
N_RES = 4


def shape_constants():
    k = np.zeros((P, K_END), np.float32)
    blocks = np.kron(np.eye(2), np.ones((C, C))) / C
    k[:, K_ONES:K_CEN] = blocks
    k[:, K_CEN:K_EYE] = np.eye(P) - blocks
    k[:, K_EYE:K_IND] = np.eye(P)
    for b in range(2):
        for p in range(P):
            k[p, K_IND + 32 * b + 16 * b + p // D] = 1.0
            at = K_AVG + 32 * b + 16 * b + HEADS * (p // C)
            k[p, at:at + HEADS] = 1.0 / C
    for p in range(P):
        for b in range(2):
            k[p, K_PATCH + 32 * b + 16 * b + (p % W) // S] = 1.0
    for e in range(E):
        for f in range(E):
            k[:, K_UP + E * e + f] = float(f >= e)
    k[:, K_EPS] = EPS
    for m in range(2):
        for q in range(2):
            for h in range(2):
                for at in (0, LOW):
                    cols = K_SEL + (2 * q + m) * P + C * h
                    k[at + E * m + 2 * q + h, cols:cols + C] = 1.0
    return k


def build(nc, t):
    ctx = ExitStack()
    with ctx:
        def sb(name, *shape):
            return ctx.enter_context(nc.sbuf_tensor("sb_" + name, list(shape), F32))

        def sem(name):
            return ctx.enter_context(nc.semaphore(name))

        banks = [ctx.enter_context(nc.psum_tensor(f"bank{i}", [P, CH], F32)) for i in range(8)]

        arena = sb("arena", P, NF * 2 * PX)
        hT = sb("hT", P, PAIRS * HW)
        const = sb("const", P, K_END)
        xsq = sb("xsq", P, 2, PX)
        prodk = sb("prodk", P, 2, PX)
        sum16 = sb("sum16", P, 2 * PT)
        means = sb("means", P, NF, 2, 2 * PT)
        qbuf = sb("qbuf", P, 2, 2, PT, S)
        qstat = sb("qstat", P, 2 * PT)
        qrstd = sb("qrstd", P, 2 * PT)
        qraw = sb("qraw", P, 2 * PT)
        vstat = sb("vstat", P, CH)
        rstd = sb("rstd", P, CH)
        score = sb("score", P, CH)
        wgt = sb("wgt", P, CH)
        smx = sb("smx", P, 32)
        smxs = sb("smxs", P, 32 * S)
        ssm = sb("ssm", P, 32)
        srz = sb("srz", P, 32 * S)
        cbias = sb("cbias", P, 32 * S)
        aggr_t = sb("aggr_t", P, 2 * PT)
        aggr = sb("aggr", P, 2 * PT)
        tok_w = sb("tok_w", P, T_END)
        scaled = prodk[:, 0, 0:3 * P]
        wqkv = sb("wqkv", P, 3, P)
        bqkv = sb("bqkv", P, 4)
        indbk = sb("indbk", P, 64)
        rest_w = sb("rest_w", P, R_END)
        sv = sb("sv", P, N_SV)
        cz = sb("cz", P, L + 1, 2)
        cv = sb("cv", P, L + 1, 2)
        cacc = sb("cacc", P, 2)

        with (nc.sbuf_tensor("sb_prodv", [P, 8, CH], F32) as prodv,
              nc.sbuf_tensor("sb_wT", [P, 2, CH], F32) as wT,
              nc.sbuf_tensor("sb_rows2", [P, 2, 1024], F32) as rows2):
            pass
        w1_high = ctx.enter_context(nc.sbuf_tensor("sb_w1_high", [P, W1 + 5 * P], F32R))
        w1_low = ctx.enter_context(nc.sbuf_tensor("sb_w1_low", [P, W1], F32R))
        parts = ctx.enter_context(nc.sbuf_tensor("sb_parts", [P, 2, CH], F32R))
        route = ctx.enter_context(nc.sbuf_tensor("sb_route", [P, CH], F32R))

        parts_q = ctx.enter_context(nc.sbuf_tensor("sb_parts_q", [P, 2, CH], F32R))
        parts_s = ctx.enter_context(nc.sbuf_tensor("sb_parts_s", [P, 2, CH], F32R))

        raw = tok_w[:, T_RAW:T_PROJ]
        projw = tok_w[:, T_PROJ:T_VEC]
        vecs = tok_w[:, T_VEC:T_END]
        wssm = rest_w[:, R_SSM:R_EW1].rearrange("p (a n) -> p a n", a=3)
        w1 = rest_w[:, R_EW1:R_GW]
        gw = rest_w[:, R_GW:R_SW3]
        sw3 = rest_w[:, R_SW3:R_EW2]
        ew2 = rest_w[:, R_EW2:R_EW3].rearrange("p (e n) -> p e n", e=E)
        ew3 = rest_w[:, R_EW3:R_GB].rearrange("p (q n) -> p q n", q=2)
        gbias = rest_w[:, R_GB:R_EB]
        ebias = rest_w[:, R_EB:R_END]

        def vec(n):
            return vecs[:, n:n + 1]

        ones64 = const[:, K_ONES:K_CEN]
        centre = const[:, K_CEN:K_EYE]
        eye = const[:, K_EYE:K_IND]
        eps = const[:, K_EPS:K_EPS + 1]
        one = const[:, K_UP + E - 1:K_UP + E]

        def ind(b):
            return const[:, K_IND + 32 * b:K_IND + 32 * b + 32]

        def patch(b):
            return const[:, K_PATCH + 32 * b:K_PATCH + 32 * b + 32]

        def avg(b):
            return const[:, K_AVG + 32 * b:K_AVG + 32 * b + 32]

        x = arena[:, :].rearrange("p (m b n) -> p m b n", m=NF, b=2)

        const_in = sem("const_in")
        tok_in = sem("tok_in")
        rest_in = sem("rest_in")
        coefs = sem("coefs")
        x_in = [sem(f"x_in{m}") for m in range(NF)]
        weights_scaled = sem("weights_scaled")
        setup_mm = sem("setup_mm")
        weights_centred = sem("weights_centred")
        biases_ready = sem("biases_ready")
        row_pairs_added = sem("row_pairs_added")
        rows_added = sem("rows_added")
        half_rows_added = sem("half_rows_added")
        patch_summed = sem("patch_summed")
        mean_taken = sem("mean_taken")
        q_moments_mm = sem("q_moments_mm")
        q_raw_mm = sem("q_raw_mm")
        q_mean_squared = sem("q_mean_squared")
        q_variance_ready = sem("q_variance_ready")
        q_log_ready = sem("q_log_ready")
        q_rstd_ready = sem("q_rstd_ready")
        q_scaled = sem("q_scaled")
        q_ready = sem("q_ready")
        pixels_squared = sem("pixels_squared")
        pixel_mean_mm = sem("pixel_mean_mm")
        pixel_square_mm = sem("pixel_square_mm")
        mean_squared = sem("mean_squared")
        variance_ready = sem("variance_ready")
        log_ready = sem("log_ready")
        rstd_ready = sem("rstd_ready")
        bias_term_mm = sem("bias_term_mm")
        bias_term_ready = sem("bias_term_ready")
        keys_mm = sem("keys_mm")
        keys_times_q = sem("keys_times_q")
        scores_mm = sem("scores_mm")
        scores_scaled = sem("scores_scaled")
        scores_biased = sem("scores_biased")
        score_max_ready = sem("score_max_ready")
        score_max_spread = sem("score_max_spread")
        scores_shifted = sem("scores_shifted")
        scores_exp = sem("scores_exp")
        exp_summed = sem("exp_summed")
        sum_inverted = sem("sum_inverted")
        inverse_sum_ready = sem("inverse_sum_ready")
        weights_raw = sem("weights_raw")
        weights_ready = sem("weights_ready")
        weights_turned = sem("weights_turned")
        weights_copied = sem("weights_copied")
        values_mm = sem("values_mm")
        values_weighted = sem("values_weighted")
        aggregate_mm = sem("aggregate_mm")
        aggregate_copied = sem("aggregate_copied")
        aggregate_turned = sem("aggregate_turned")
        aggregate_ready = sem("aggregate_ready")
        projected_mm = sem("projected_mm")
        tokens_ready = sem("tokens_ready")
        drive_mm = sem("drive_mm")
        force_ready = sem("force_ready")
        scan_step = [sem(f"scan_step{h}") for h in range(2)]
        carry_step = [sem(f"carry_step{h}") for h in range(2)]
        v_share_ready = sem("v_share_ready")
        chunk_fixed = [sem(f"chunk_fixed{h}") for h in range(2)]
        mixed_mm = sem("mixed_mm")
        gelu_ready = sem("gelu_ready")
        silu_ready = sem("silu_ready")
        residual_ready = sem("residual_ready")
        centred_mm = sem("centred_mm")
        centred_squared = sem("centred_squared")
        norm_variance_mm = sem("norm_variance_mm")
        norm_log_ready = sem("norm_log_ready")
        norm_rstd_ready = sem("norm_rstd_ready")
        normed_ready = sem("normed_ready")
        logits_mm = sem("logits_mm")
        logits_copied = sem("logits_copied")
        logits_turned = sem("logits_turned")
        logits_biased = sem("logits_biased")
        logits_max = sem("logits_max")
        logits_shifted = sem("logits_shifted")
        logits_exp = sem("logits_exp")
        logits_sum = sem("logits_sum")
        logits_inverse = sem("logits_inverse")
        gates_ready = sem("gates_ready")
        gates_compared = sem("gates_compared")
        ties_found = sem("ties_found")
        ties_counted = sem("ties_counted")
        wins_ready = sem("wins_ready")
        rank_ready = sem("rank_ready")
        gate_max = sem("gate_max")
        gates_shifted = sem("gates_shifted")
        gates_exp = sem("gates_exp")
        picked = sem("picked")
        picked_sum = sem("picked_sum")
        picked_inverse = sem("picked_inverse")
        routing_ready = sem("routing_ready")
        routing_turned = sem("routing_turned")
        ring_mm = sem("ring_mm")
        taken = [sem(f"taken{r}") for r in range(5)]
        weights_rounded = sem("weights_rounded")
        weights_split = sem("weights_split")
        high_ready = sem("high_ready")
        low_ready = sem("low_ready")
        shared_high = sem("shared_high")
        squares_high = sem("squares_high")
        squares_split = sem("squares_split")
        shared_split = sem("shared_split")
        routing_high = sem("routing_high")
        routing_low = sem("routing_low")
        route_cleared = sem("route_cleared")
        out_rows_mm = sem("out_rows_mm")
        out_squared = sem("out_squared")
        out_square_sum = sem("out_square_sum")
        out_log_ready = sem("out_log_ready")
        out_rstd_ready = sem("out_rstd_ready")
        out_ready = sem("out_ready")
        stored = [sem(f"stored{i}") for i in range(2)]

        def count(value):
            return max(value, 0) if isinstance(value, int) else value

        def pipeline(eng, step, total):
            lead, tail = NF, NF
            for n in range(lead):
                step(n, n % NF)
            with eng.Fori(1, (total - tail) // NF) as k:
                for m in range(NF):
                    step(k * NF + m, m)
            for n in range(total - tail, total):
                step(n, n % NF)

        ring = banks[0:3]
        bank_s, bank_sq, bank_mu, bank_ag, bank_t = banks[3:8]
        drive_banks = (bank_sq, bank_mu)
        RING_K, RING_P, RING_V = 1, 9, 10

        mix = arena[:, :]
        pos = [0]

        def cut(n):
            a = mix[:, pos[0]:pos[0] + n]
            pos[0] += n
            return a

        h2 = cut(2 * CH).rearrange("p (i n) -> p i n", i=2)
        sq3 = cut(CH)
        ln3 = cut(CH)
        h1s = cut(CH)
        h1e = cut(8 * CH).rearrange("p (m e n) -> p m e n", m=2, e=E)
        h2s = cut(2 * CH).rearrange("p (m n) -> p m n", m=2)
        h2e = cut(4 * CH).rearrange("p (m q n) -> p m q n", m=2, q=2)
        h2w = cut(4 * CH).rearrange("p (m q n) -> p m q n", m=2, q=2)
        ysum = cut(CH)
        ysq = cut(CH)
        out_t = cut(2 * CH).rearrange("p (i a n) -> p i a n", i=2, a=2)
        lg_rows = cut(P)
        lg = cut(32)
        lgx = cut(32)
        gat = cut(32)
        pick = cut(32)
        wmoe = cut(32)
        l8 = cut(8 * 8).rearrange("p (a n) -> p a n", a=8)
        y8 = cut(8 * 2).rearrange("p (a n) -> p a n", a=2)
        beat = cut(P)
        tie = cut(P)
        assert pos[0] <= NF * 2 * PX
        force = arena[:, 0:2 * HP]
        z = arena[:, 2 * HP:4 * HP]
        v_share = prodk[:, :, :].rearrange("p b n -> p (b n)")
        vel = xsq[:, 0, 0:CH]
        zin = xsq[:, 0, 2 * CH:3 * CH]
        vin = xsq[:, 0, 3 * CH:4 * CH]
        ctmp = xsq[:, 1, 0:2 * PAIRS]

        def chunk(a, n):
            return a.rearrange("p (n k) -> p n k", k=CH)[:, n, :]

        def at(h, j):
            return slice(h * HP + j * HS, h * HP + (j + 1) * HS)

        def piece(h, n, size=CH):
            return slice(h * HP + n * size, h * HP + (n + 1) * size)

        def tokens_at(h, n, steps):
            return hT[:, h * HP:(h + 1) * HP].rearrange("p (n j) -> p j n", j=L)[:, n * steps:(n + 1) * steps]

        def tokens_of(g):
            return slice((g // 2) * HW + g % 2, (g // 2 + 1) * HW, 2)

        bank_cen, bank_var, bank_base = banks[3], banks[4], banks[5]
        mix_ring = banks[0:3] + banks[6:8]
        RING = len(mix_ring)
        K_SHARED, K_SPREAD, K_SUM, USES = 13, 15, 19, 20

        def relu(eng, i, k):
            eng.wait_ge(ring_mm, USES * i + k + 1)
            if k == 0:
                dst, bias = h1s, ebias[:, 6:7]
                eng.wait_ge(shared_split, 2 * i)
            elif k < 9:
                dst, bias = h1e[:, (k - 1) // E, (k - 1) % E], ebias[:, (k - 1) % E:(k - 1) % E + 1]
            elif k < K_SHARED:
                dst, bias = h2e[:, (k - 9) // 2, (k - 9) % 2], ebias[:, 4 + (k - 9) % 2:5 + (k - 9) % 2]
            else:
                dst, bias = h2s[:, k - K_SHARED], ebias[:, 7:8]
            bank, done = mix_ring[k % RING], taken[k % RING]
            if k % RING == 2:
                eng.tensor_scalar(dst, bank[:, :], bias, 0.0, ALU.add, ALU.max).then_inc(done, 1)
            else:
                eng.activation(dst, bank[:, :], ACT.Relu, bias=bias).then_inc(done, 1)

        def patch_sums(eng, u, m):
            eng.wait_ge(x_in[m], (u - m) * 8 + 32)
            rows = x[:, m, :, :].rearrange("p b (h s n) -> p (b h) s n", s=S, n=W)
            out = [rows2[:, i, :].rearrange("p (h n) -> p h n", n=W) for i in range(2)]
            eng.wait_ge(patch_summed, u)
            for i in range(2):
                eng.tensor_tensor(out[i], rows[:, :, 2 * i], rows[:, :, 2 * i + 1], ALU.add).then_inc(row_pairs_added, 1)
            eng.wait_ge(row_pairs_added, 2 * u + 2)
            eng.tensor_tensor(rows2[:, 0, :], rows2[:, 0, :], rows2[:, 1, :], ALU.add).then_inc(rows_added, 1)
            eng.wait_ge(rows_added, u + 1)
            four = rows2[:, 0, :].rearrange("p (n t) -> p n t", t=S)
            two = rows2[:, 1, 0:2 * 2 * PT].rearrange("p (n t) -> p n t", t=2)
            eng.tensor_tensor(two, four[:, :, 0:2], four[:, :, 2:4], ALU.add).then_inc(half_rows_added, 1)
            eng.wait_ge(half_rows_added, u + 1)
            eng.wait_ge(mean_taken, 2 * u)
            eng.tensor_tensor(sum16[:, :], two[:, :, 0], two[:, :, 1], ALU.add).then_inc(patch_summed, 1)

        def low(eng, i, p, m):
            eng.wait_ge(high_ready, 2 * i + m + 1)
            rows, other = slice(C * m, C * m + C), slice(C - C * m, P - C * m)
            eng.tensor_tensor(parts[other, m, :], h2[rows, p], parts[rows, m, :].bitcast(F32),
                              ALU.subtract).then_inc(low_ready, 1)

        def by_group(a):
            return a.rearrange("p (a f k) -> p a f k", a=2, f=2)

        def in_order(a):
            return a.rearrange("p (a k f) -> p a f k", a=2, f=2)

        def mixture(eng, step):
            for i in range(2):
                step(i, i)
            with eng.Fori(1, ITERS // 2 - 1) as k:
                for p in range(2):
                    step(2 * k + p, p)
            for i in range(ITERS - 2, ITERS):
                step(i, i % 2)

        def fixed(h, j):
            return j + 1 if h == 0 else min(2 * j + 3, 2 * L)

        block = ctx.enter_context(nc.Block())


        @block.sync
        def _(sp):
            def load(u, m):
                sp.wait_ge(values_mm, count((u - NF) * 8 + 8))
                half = m % 2
                for b in range(2):
                    src = t["x"][(u - half) + b]
                    sp.dma_start(x[:, m, b, :], src[:, half * PX:(half + 1) * PX]).then_inc(x_in[m], 16)

            sp.dma_start(tok_w[:, :], t["tok_w"]).then_inc(tok_in, 16)
            load(0, 0)
            sp.dma_start(const[:, :], t["const"]).then_inc(const_in, 16)
            for u in range(1, NF):
                load(u, u)
            sp.dma_start(rest_w[:, :], t["rest_w"]).then_inc(rest_in, 16)
            with sp.Fori(1, UNITS // NF) as k:
                for m in range(NF):
                    load(k * NF + m, m)

            def store(i, p):
                sp.wait_ge(out_ready, i + 1)
                for a in range(2):
                    for m in range(2):
                        sp.dma_start(t["out"][2 * i + a, m].rearrange("(k f) c -> k f c", f=2),
                                     out_t[:, p, a].rearrange("p (f m c) -> p f m c", f=2, m=2)[:, :, m]
                                     ).then_inc(stored[p], 16)

            with sp.Fori(0, ITERS // 2) as k:
                for p in range(2):
                    store(2 * k + p, p)
            for p in range(2):
                sp.wait_ge(stored[p], STORE * (ITERS // 2))

        @block.gpsimd
        def _(pool):
            def softmax(u):
                sc = score[:, :].rearrange("p (h s n) -> p h s n", h=2, s=S)
                wg = wgt[:, :].rearrange("p (h s n) -> p h s n", h=2, s=S)

                def spread(a):
                    return a[:, :].rearrange("p (h n) -> p h n", h=2)[:, :, None, :].to_broadcast([P, 2, S, W])

                pool.wait_ge(scores_scaled, u + 1)
                pool.wait_ge(bias_term_ready, u + 1)
                pool.tensor_tensor(sc, sc, spread(cbias), ALU.add).then_inc(scores_biased, 1)
                pool.wait_ge(score_max_spread, u + 1)
                pool.tensor_tensor(sc, sc, spread(smxs), ALU.subtract).then_inc(scores_shifted, 1)
                pool.wait_ge(scores_exp, u + 1)
                pool.wait_ge(weights_turned, u)
                pool.tensor_tensor(wgt[:, :], score[:, :], rstd[:, :], ALU.mult).then_inc(weights_raw, 1)
                pool.wait_ge(weights_raw, u + 1)
                pool.wait_ge(inverse_sum_ready, u + 1)
                pool.tensor_tensor(wg, wg, spread(srz), ALU.mult).then_inc(weights_ready, 1)

            patch_sums(pool, 1, 1)
            softmax(0)

            def step(n, m):
                if not isinstance(n, int) or n + 2 < UNITS:
                    patch_sums(pool, n + 2, (m + 2) % NF)
                if not isinstance(n, int) or n + 1 < UNITS:
                    softmax(n + 1)

            pipeline(pool, step, UNITS)

            pool.wait_ge(rest_in, 16)
            pool.wait_ge(aggregate_mm, 2 * UNITS)
            pool.tensor_copy(w1_high[:, 0:W1], w1).then_inc(weights_rounded, 1)
            pool.tensor_copy(w1_high[:, W1:W1 + 4 * P], const[:, K_SEL:K_END]).then_inc(weights_rounded, 1)
            pool.tensor_copy(w1_high[:, W1 + 4 * P:W1 + 5 * P], const[:, K_ONES:K_CEN]).then_inc(weights_rounded, 1)
            pool.memset(route[:, :].bitcast(F32), 0.0).then_inc(route_cleared, 1)
            pool.wait_ge(weights_rounded, 3)
            pool.tensor_tensor(w1_low[:, :], w1, w1_high[:, 0:W1].bitcast(F32), ALU.subtract).then_inc(weights_split, 1)

            def split_shared(i):
                pool.wait_ge(taken[0], USES // RING * i + 1)
                pool.wait_ge(ring_mm, count(USES * i - USES + K_SPREAD))
                for m in range(2):
                    rows = slice(C * m, C * m + C)
                    pool.tensor_tensor(parts_s[rows, m, :], h1s[rows], one[rows].to_broadcast([C, CH]),
                                       ALU.mult).then_inc(shared_high, 1)
                for m in range(2):
                    rows, other = slice(C * m, C * m + C), slice(C - C * m, P - C * m)
                    pool.wait_ge(shared_high, 2 * i + m + 1)
                    pool.tensor_tensor(parts_s[other, m, :], h1s[rows], parts_s[rows, m, :].bitcast(F32),
                                       ALU.subtract).then_inc(shared_split, 1)

            def split_squares(i):
                pool.wait_ge(centred_squared, i + 1)
                pool.wait_ge(norm_variance_mm, i)
                pool.wait_ge(low_ready, 2 * i)
                pool.tensor_tensor(parts_q[:, 0, :], sq3, one.to_broadcast([P, CH]), ALU.mult).then_inc(squares_high, 1)
                pool.wait_ge(squares_high, i)
                pool.tensor_tensor(parts_q[:, 1, :], sq3, parts_q[:, 0, :].bitcast(F32), ALU.subtract).then_inc(squares_split, 1)

            def mstep(i, p):
                if not isinstance(i, int) or i + 1 < ITERS:
                    split_squares(i + 1)
                    pool.wait_ge(squares_split, i + 1)
                split_shared(i)
                if not isinstance(i, int) or i + 1 < ITERS:
                    for m in range(2):
                        low(pool, i + 1, (p + 1) % 2, m)

            low(pool, 0, 0, 1)
            mixture(pool, mstep)

        @block.scalar
        def _(act):
            act.preload_act_table_set("natural_log_exp_and_others")
            def take_means(u, m):
                act.wait_ge(patch_summed, u + 1)
                act.activation(means[:, m, 0, :], sum16[:, :], ACT.Copy, scale=1.0 / N_PIX).then_inc(mean_taken, 1)
                act.activation(means[:, m, 1, :], sum16[:, :], ACT.Square, scale=1.0 / N_PIX).then_inc(mean_taken, 1)

            def q_rstd(u):
                act.wait_ge(q_moments_mm, u + 1)
                act.wait_ge(q_log_ready, u)
                act.activation(qstat[:, :], bank_sq[:, 0:2 * PT], ACT.Square).then_inc(q_mean_squared, 1)
                act.wait_ge(q_variance_ready, u + 1)
                act.activation(qstat[:, :], qstat[:, :], ACT.Ln, bias=eps).then_inc(q_log_ready, 1)
                act.wait_ge(q_log_ready, u + 1)
                act.wait_ge(q_scaled, u)
                act.activation(qrstd[:, :], qstat[:, :], ACT.Exp, scale=-0.5).then_inc(q_rstd_ready, 1)

            def query(u, m):
                act.wait_ge(q_scaled, u + 1)
                act.wait_ge(bias_term_mm, count(u - 1))
                act.wait_ge(keys_times_q, count(8 * u - 8))
                act.activation(qbuf[:, m % 2].rearrange("p b n t -> p (b n) t"),
                               qraw[:, :, None].to_broadcast([P, 2 * PT, S]), ACT.Identity,
                               scale=float(C) ** -0.5, bias=bqkv[:, 0:1]).then_inc(q_ready, 1)

            def squares(u, m, b):
                if b == 0:
                    act.wait_ge(x_in[m], (u - m) * 8 + 32)
                    act.wait_ge(pixel_square_mm, u)
                act.activation(xsq[:, b, :], x[:, m, b, :], ACT.Square).then_inc(pixels_squared, 1)

            def pixel_mean(u):
                act.wait_ge(pixel_mean_mm, u + 1)
                act.wait_ge(rstd_ready, u)
                act.activation(vstat[:, :], bank_mu[:, :], ACT.Square).then_inc(mean_squared, 1)

            def score_bias(u):
                act.wait_ge(bias_term_mm, u + 1)
                act.wait_ge(scores_biased, u)
                act.activation(cbias[:, :].rearrange("p (n t) -> p n t", t=S),
                               ring[0][:, 0:32][:, :, None].to_broadcast([P, 32, S]), ACT.Copy).then_inc(bias_term_ready, 1)

            def pixel_rstd(u):
                act.wait_ge(variance_ready, u + 1)
                act.activation(vstat[:, :], vstat[:, :], ACT.Ln, bias=eps).then_inc(log_ready, 1)
                act.wait_ge(log_ready, u + 1)
                act.wait_ge(weights_raw, u)
                act.activation(rstd[:, :], vstat[:, :], ACT.Exp, scale=-0.5).then_inc(rstd_ready, 1)

            def expo(u):
                act.wait_ge(scores_shifted, u + 1)
                act.activation(score[:, :], score[:, :], ACT.Exp).then_inc(scores_exp, 1)

            def copy_w(u, m):
                act.wait_ge(weights_turned, u + 1)
                act.wait_ge(values_weighted, count(8 * u - 8))
                act.activation(wT[:, m % 2, :], bank_t[:, :], ACT.Copy).then_inc(weights_copied, 1)

            def copy_agg(u):
                act.wait_ge(aggregate_mm, 2 * u + 2)
                act.wait_ge(aggregate_turned, u)
                act.activation(aggr_t[:, :], bank_ag[:, 0:2 * PT], ACT.Copy).then_inc(aggregate_copied, 1)

            def copy_turned(u):
                act.wait_ge(aggregate_turned, u + 1)
                act.wait_ge(projected_mm, u)
                act.activation(aggr[:, :], bank_ag[:, 2 * PT:4 * PT], ACT.Copy).then_inc(aggregate_ready, 1)

            squares(0, 0, 0)
            act.wait_ge(setup_mm, 1)
            act.activation(wqkv[:, :, :].rearrange("p a n -> p (a n)"), banks[0][:, 0:3 * P], ACT.Copy).then_inc(weights_centred, 1)
            take_means(0, 0)
            act.wait_ge(const_in, 16)
            squares(0, 0, 1)
            q_rstd(0)
            act.wait_ge(biases_ready, 2)
            query(0, 0)
            pixel_mean(0)
            score_bias(0)
            pixel_rstd(0)
            squares(1, 1, 0)
            squares(1, 1, 1)
            take_means(1, 1)
            q_rstd(1)
            query(1, 1)
            expo(0)
            pixel_mean(1)

            def forcing(h, pieces=range(N_PIECE)):
                act.wait_ge(coefs, N_COEFS)
                for n in pieces:
                    act.wait_ge(drive_mm, N_PIECE * h + n + 1)
                    act.activation(force[:, piece(h, n)], drive_banks[n % 2][:, :], ACT.Identity,
                                   scale=sv[:, SV_F:SV_F + 1], bias=sv[:, SV_FB:SV_FB + 1]).then_inc(force_ready, 1)

            def step(n, m):
                nxt = not isinstance(n, int) or n + 1 < UNITS
                nxt2 = not isinstance(n, int) or n + 2 < UNITS
                prev = not isinstance(n, int) or n >= 1
                if nxt:
                    score_bias(n + 1)
                if prev:
                    copy_agg(n - 1)
                    if not nxt:
                        forcing(0, (0, 1))
                    copy_turned(n - 1)
                    if not nxt:
                        forcing(0, (2, 3))
                if nxt:
                    pixel_rstd(n + 1)
                if nxt2:
                    squares(n + 2, (m + 2) % NF, 0)
                copy_w(n, m)
                if nxt2:
                    squares(n + 2, (m + 2) % NF, 1)
                    take_means(n + 2, (m + 2) % NF)
                    q_rstd(n + 2)
                    query(n + 2, m)
                if nxt:
                    expo(n + 1)
                if nxt2:
                    pixel_mean(n + 2)

            pipeline(act, step, UNITS)
            forcing(0, (4, 5))
            copy_agg(UNITS - 1)
            forcing(0, (6,))
            copy_turned(UNITS - 1)
            forcing(0, (7,))

            forcing(1)
            def norm_sq(i):
                act.wait_ge(centred_mm, i + 1)
                act.wait_ge(norm_variance_mm, i)
                act.wait_ge(squares_split, count(i - 1))
                act.activation(sq3, bank_cen[:, :], ACT.Square).then_inc(centred_squared, 1)

            act.wait_ge(carry_step[0], 4 * NCK - 2)
            for j in range(L):
                act.activation(v_share[:, at(0, j)], vin[:, 0:HS], ACT.Copy, scale=cz[:, j + 1, 1:2]).then_inc(v_share_ready, 1)
            for h in range(2):
                act.preload_act_table(ACT.Gelu)
                for n in range(N_PIECE):
                    act.wait_ge(mixed_mm, N_PIECE * h + n + 1)
                    act.activation(force[:, piece(h, n)], banks[n][:, :], ACT.Gelu,
                                   bias=sv[:, SV_CD:SV_CD + 1]).then_inc(gelu_ready, 1)
                act.preload_act_table(ACT.Silu)
                act.wait_ge(gelu_ready, N_PIECE * (h + 1))
                for n in range(N_RES):
                    if h == 1 and n == N_RES - 2:
                        norm_sq(0)
                    a = force[:, piece(h, n, HP // N_RES)]
                    act.activation(a, a, ACT.Silu).then_inc(silu_ready, 1)
            act.preload_act_table_set("natural_log_exp_and_others")

            def norm_rstd(i):
                act.wait_ge(norm_variance_mm, i + 1)
                act.wait_ge(normed_ready, i)
                act.activation(ln3, bank_var[:, :], ACT.Ln, bias=eps).then_inc(norm_log_ready, 1)
                act.wait_ge(norm_log_ready, i + 1)
                act.activation(ln3, ln3, ACT.Exp, scale=-0.5).then_inc(norm_rstd_ready, 1)

            def high(i, p):
                act.wait_ge(normed_ready, i + 1)
                for m in range(2):
                    rows = slice(C * m, C * m + C)
                    act.activation(parts[rows, m, :], h2[rows, p], ACT.Copy).then_inc(high_ready, 1)

            def out_sq(i):
                act.wait_ge(out_rows_mm, i + 1)
                act.wait_ge(out_square_sum, i)
                act.activation(ysq, bank_base[:, :], ACT.Square).then_inc(out_squared, 1)

            def out_rstd(i):
                act.wait_ge(out_square_sum, i + 1)
                act.activation(y8[:, 0, :], y8[:, 0, :], ACT.Ln, scale=1.0 / C, bias=eps).then_inc(out_log_ready, 1)
                act.wait_ge(out_log_ready, i + 1)
                act.wait_ge(out_ready, i)
                act.activation(y8[:, 1, :], y8[:, 0, :], ACT.Exp, scale=-0.5).then_inc(out_rstd_ready, 1)

            norm_rstd(0)
            high(0, 0)

            def mstep(i, p):
                nxt = not isinstance(i, int) or i + 1 < ITERS
                prev = not isinstance(i, int) or i >= 1
                act.wait_ge(logits_mm, i + 1)
                act.wait_ge(logits_turned, i)
                act.activation(lg_rows, bank_var[:, 0:P], ACT.Copy).then_inc(logits_copied, 1)
                relu(act, i, 0)
                if nxt:
                    norm_sq(i + 1)
                relu(act, i, 1)
                act.wait_ge(logits_shifted, i + 1)
                act.activation(lgx, lgx, ACT.Exp).then_inc(logits_exp, 1)
                for k in (3, 4, 5, 6):
                    relu(act, i, k)
                act.wait_ge(gates_shifted, i + 1)
                act.activation(pick, pick, ACT.Exp).then_inc(gates_exp, 1)
                relu(act, i, 8)
                if prev:
                    out_sq(i - 1)
                relu(act, i, 9)
                if nxt:
                    norm_rstd(i + 1)
                relu(act, i, 10)
                if prev:
                    out_rstd(i - 1)
                relu(act, i, 11)
                act.wait_ge(routing_turned, i + 1)
                act.activation(in_order(route[0:2 * E, :]), by_group(bank_var[0:2 * E, :]), ACT.Copy).then_inc(routing_high, 1)
                relu(act, i, 13)
                relu(act, i, 14)
                if nxt:
                    high(i + 1, (p + 1) % 2)

            mixture(act, mstep)
            out_sq(ITERS - 1)
            out_rstd(ITERS - 1)

        @block.tensor
        def _(pe):
            pe.wait_ge(const_in, 16)
            pe.wait_ge(weights_scaled, 3)
            pe.matmul(banks[0][:, 0:3 * P], centre, scaled[:, :],
                      start=True, stop=True).then_inc(setup_mm, 1)
            pe.matmul(banks[1][:, 0:1], raw[:, 0 * P:1 * P], vec(V_LNQB), start=True, stop=True)
            pe.matmul(banks[1][:, 1:2], raw[:, 1 * P:2 * P], vec(V_LNKB), start=True, stop=True)
            pe.matmul(banks[1][:, 2:3], raw[:, 2 * P:3 * P], vec(V_LNKB), start=True, stop=True).then_inc(setup_mm, 1)
            pe.wait_ge(weights_scaled, 4)
            pe.matmul(banks[2][:, 0:1], projw[:, :], bqkv[:, 2:3], start=True, stop=True).then_inc(setup_mm, 1)
            pe.wait_ge(weights_centred, 1)

            def query(u, m):
                pe.wait_ge(mean_taken, 2 * u + 2)
                pe.wait_ge(variance_ready, u)
                pe.wait_ge(mean_squared, u)
                pe.matmul(bank_sq[:, :], ones64, means[:, m].rearrange("p a n -> p (a n)"),
                          start=True, stop=True).then_inc(q_moments_mm, 1)
                pe.matmul(bank_mu[:, 0:2 * PT], wqkv[:, 0, :], means[:, m, 0, :],
                          start=True, stop=True).then_inc(q_raw_mm, 1)

            def head_sums(bank, what, b, src):
                for j in range(NJ):
                    mm = pe.matmul(bank[32 * j:32 * j + 32, :], what, src[:, j * CH:(j + 1) * CH],
                                   start=(b == 0), stop=(b == 1))
                return mm

            def pixel_means(u, m):
                pe.wait_ge(x_in[m], (u - m) * 8 + 32)
                pe.wait_ge(q_scaled, u + 1)
                for b in range(2):
                    mm = head_sums(bank_mu, avg(b), b, x[:, m, b, :])
                mm.then_inc(pixel_mean_mm, 1)

            def pixel_squares(u, m):
                pe.wait_ge(pixels_squared, 2 * u + 2)
                pe.wait_ge(q_variance_ready, u + 1)
                for b in range(2):
                    mm = head_sums(bank_sq, avg(b), b, xsq[:, b, :])
                mm.then_inc(pixel_square_mm, 1)

            def ring_free(u, idx):
                first = isinstance(u, int) and u <= 1
                last = isinstance(u, int) and u == UNITS - 1
                if idx <= 2:
                    if first:
                        pe.wait_ge(keys_times_q, 8 * u)
                    else:
                        pe.wait_ge(values_weighted, count(8 * (u - 2) + 6 + idx))
                elif idx == 3:
                    pe.wait_ge(bias_term_ready, u + 1)
                elif idx < RING_P:
                    pe.wait_ge(keys_times_q, count(8 * u + idx - 3))
                elif idx == RING_P:
                    if isinstance(u, int) and u >= UNITS - 2:
                        pe.wait_ge(values_weighted, 8 * u + 8)
                    else:
                        pe.wait_ge(keys_times_q, 8 * (u + 2) + 6)
                elif idx < RING_V + 2:
                    if last:
                        pe.wait_ge(values_weighted, 8 * u)
                    else:
                        pe.wait_ge(keys_times_q, count(8 * (u + 1) + idx - 3))
                elif idx == RING_V + 2:
                    pe.wait_ge(tokens_ready, u)
                else:
                    pe.wait_ge(values_weighted, count(8 * u + idx - RING_V - 2))

            def bias_term(u, m):
                ring_free(u, 0)
                pe.wait_ge(q_ready, u + 1)
                for j in range(NJ):
                    for b in range(2):
                        mm = pe.matmul(ring[0][32 * j:32 * j + 32, 0:32], indbk[:, 32 * b:32 * b + 32],
                                       qbuf[:, m % 2, b, 32 * j:32 * j + 32, 0], start=(b == 0), stop=(b == 1))
                mm.then_inc(bias_term_mm, 1)

            def keys(u, m, c):
                ring_free(u, RING_K + c)
                b, j = c // NJ, c % NJ
                pe.matmul(ring[(RING_K + c) % 3][:, :], wqkv[:, 1, :], x[:, m, b, j * CH:(j + 1) * CH],
                          start=True, stop=True).then_inc(keys_mm, 1)

            def scores(u, b):
                pe.wait_ge(keys_times_q, 8 * u + 4 * b + 4)
                if b == 0:
                    pe.wait_ge(scores_scaled, u)
                head_sums(bank_s, ind(b), b, prodk[:, b, :]).then_inc(scores_mm, 1)

            def turn_weights(u):
                pe.wait_ge(weights_ready, u + 1)
                pe.wait_ge(weights_copied, u)
                for r in range(4):
                    mm = pe.transpose(bank_t[:, r * P:(r + 1) * P], wgt[:, r * P:(r + 1) * P], eye)
                mm.then_inc(weights_turned, 1)

            def values(u, m, c):
                ring_free(u, RING_V + c)
                b, j = c // NJ, c % NJ
                for r in range(4):
                    at = j * CH + r * P
                    mm = pe.matmul(ring[(RING_V + c) % 3][:, r * P:(r + 1) * P], x[:, m, b, at:at + P],
                                   wqkv[:, 2, :], start=True, stop=True)
                mm.then_inc(values_mm, 1)

            def aggregate(u, b):
                pe.wait_ge(values_weighted, 8 * u + 4 * b + 4)
                if b == 0:
                    pe.wait_ge(aggregate_ready, u)
                for r in range(2):
                    for j in range(NJ):
                        rows = prodv[:, NJ * b + j, :].rearrange("p (h r k) -> p r h k", h=2, r=2)
                        mm = pe.matmul(bank_ag[32 * j:32 * j + 32, 0:2 * PT], patch(b), rows[:, r],
                                       start=(b == 0 and r == 0), stop=(b == 1 and r == 1))
                mm.then_inc(aggregate_mm, 1)

            def turn_aggregate(u):
                pe.wait_ge(aggregate_copied, u + 1)
                for h in range(2):
                    mm = pe.transpose(bank_ag[:, (2 + h) * PT:(3 + h) * PT], aggr_t[:, h * P:(h + 1) * P], eye)
                mm.then_inc(aggregate_turned, 1)

            def project(u):
                ring_free(u, RING_P)
                pe.wait_ge(aggregate_ready, u + 1)
                by_pair = aggr[:, :].rearrange("p (h j b w) -> p b j h w", h=2, j=NJ, b=2)
                for b in range(2):
                    mm = pe.matmul(ring[RING_P % 3][:, b * PT:(b + 1) * PT], projw[:, :], by_pair[:, b],
                                   start=True, stop=True)
                mm.then_inc(projected_mm, 1)

            def drive(h, pieces=range(N_PIECE)):
                for n in pieces:
                    pe.wait_ge(force_ready, count(N_PIECE * h + n - 1))
                    pe.matmul(drive_banks[n % 2][:, :], wssm[:, 0, :], tokens_at(h, n, 2),
                              start=True, stop=True).then_inc(drive_mm, 1)

            pe.wait_ge(weights_scaled, 5)
            query(0, 0)
            pixel_means(0, 0)
            pixel_squares(0, 0)
            bias_term(0, 0)
            for c in range(8):
                keys(0, 0, c)
            scores(0, 0)
            scores(0, 1)
            query(1, 1)
            pixel_means(1, 1)
            pixel_squares(1, 1)

            def step(n, m):
                prev = not isinstance(n, int) or n >= 1
                nxt = not isinstance(n, int) or n + 1 < UNITS
                nxt2 = not isinstance(n, int) or n + 2 < UNITS
                m1, m2 = (m + 1) % NF, (m + 2) % NF
                if nxt:
                    bias_term(n + 1, m1)
                    keys(n + 1, m1, 0)
                    keys(n + 1, m1, 1)
                elif isinstance(n, int):
                    pe.wait_ge(rest_in, 16)
                    pe.wait_ge(variance_ready, UNITS)
                    pe.wait_ge(mean_squared, UNITS)
                    pe.wait_ge(tokens_ready, UNITS // 2)
                    drive(0, (0, 1))
                if prev:
                    turn_aggregate(n - 1)
                if nxt:
                    for c in range(2, 5):
                        keys(n + 1, m1, c)
                else:
                    drive(0, (2,))
                turn_weights(n)
                if nxt:
                    for c in range(5, 8):
                        keys(n + 1, m1, c)
                else:
                    drive(0, (3,))
                if prev:
                    project(n - 1)
                if nxt:
                    scores(n + 1, 0)
                for c in range(8):
                    values(n, m, c)
                    if c == 1 and nxt:
                        scores(n + 1, 1)
                    if c == 1 and nxt2:
                        query(n + 2, m2)
                    if c == 5 and nxt2:
                        pixel_means(n + 2, m2)
                    if c == 5:
                        if not nxt:
                            drive(0, (4,))
                        aggregate(n, 0)
                if nxt2:
                    pixel_squares(n + 2, m2)
                if not nxt:
                    drive(0, (5,))
                aggregate(n, 1)

            pipeline(pe, step, UNITS)
            drive(0, (6,))
            turn_aggregate(UNITS - 1)
            drive(0, (7,))
            project(UNITS - 1)

            pe.wait_ge(tokens_ready, UNITS)
            drive(1)

            def direct(h, n):
                if h == 0:
                    pe.wait_ge(force_ready, 2 * N_PIECE)
                else:
                    pe.wait_ge(gelu_ready, n + 1)
                pe.matmul(banks[n][:, :], wssm[:, 2, :], tokens_at(h, n, 2), start=True, stop=False)

            for n in range(N_PIECE):
                direct(0, n)
            for h in range(2):
                for n in range(N_PIECE):
                    if h == 0:
                        pe.wait_ge(v_share_ready, 2 * n + 2)
                        pe.matmul(banks[n][:, :], wssm[:, 1, :], v_share[:, piece(0, n)], start=False, stop=False)
                    pe.wait_ge(chunk_fixed[h], fixed(h, 2 * n + 1))
                    pe.matmul(banks[n][:, :], wssm[:, 1, :], z[:, piece(h, n)],
                              start=False, stop=True).then_inc(mixed_mm, 1)
                if h == 0:
                    for n in range(N_PIECE):
                        direct(1, n)

            def centre_rows(i):
                pe.wait_ge(normed_ready, i)
                if isinstance(i, int) and i == 3:
                    pe.wait_ge(residual_ready, 2 * N_RES)
                pe.matmul(bank_cen[:, :], centre, chunk(hT[:, :], i), start=True, stop=True).then_inc(centred_mm, 1)

            def variance(i):
                pe.wait_ge(logits_biased, i)
                if isinstance(i, int) and i < 1:
                    pe.wait_ge(centred_squared, i + 1)
                    pe.matmul(bank_var[:, :], ones64, sq3, start=True, stop=True).then_inc(norm_variance_mm, 1)
                else:
                    pe.wait_ge(squares_split, i)
                    by = w1_high[:, W1 + 4 * P:W1 + 5 * P]
                    pe.matmul(bank_var[:, :], by, parts_q[:, 0, :], start=True, stop=False)
                    pe.matmul(bank_var[:, :], by, parts_q[:, 1, :], start=False, stop=True).then_inc(norm_variance_mm, 1)

            def split(w, rows):
                return (w1_high[:, w], rows, True, False), (w1_low[:, w], rows, False, True)

            def logits(i, p):
                pe.wait_ge(normed_ready, i + 1)
                pe.wait_ge(norm_log_ready, i + 1)
                pe.wait_ge(routing_low, i)
                for g in range(G):
                    mm = pe.matmul(bank_var[32 * g:32 * g + 32, 0:P], gw[:, :], h2[:, p, tokens_of(g)],
                                   start=True, stop=True)
                mm.then_inc(logits_mm, 1)

            def turn_logits(i):
                pe.wait_ge(logits_copied, i + 1)
                pe.transpose(bank_var[:, P:2 * P], lg_rows, eye).then_inc(logits_turned, 1)

            def ring_use(i, k):
                pe.wait_ge(taken[k % RING], USES // RING * i + k // RING)
                return mix_ring[k % RING]

            def out_rows(i):
                pe.wait_ge(taken[K_SUM % RING], USES // RING * i + K_SUM // RING + 1)
                pe.wait_ge(out_ready, i)
                for g in range(G):
                    mm = pe.matmul(bank_base[:, g * P:(g + 1) * P], ysum[:, tokens_of(g)], centre, start=True, stop=True)
                mm.then_inc(out_rows_mm, 1)

            def turn_routing(i, nxt):
                pe.wait_ge(routing_ready, i + 1)
                if nxt:
                    pe.wait_ge(norm_log_ready, i + 2)
                for g in range(G):
                    mm = pe.transpose(bank_var[0:2 * E, g * P:(g + 1) * P], wmoe[:, 2 * E * g:2 * E * (g + 1)], eye)
                mm.then_inc(routing_turned, 1)

            def mstep(i, p):
                nxt = not isinstance(i, int) or i + 1 < ITERS
                prev = not isinstance(i, int) or i >= 1
                pe.wait_ge(high_ready, 2 * i + 2)
                pe.wait_ge(low_ready, 2 * i + 2)
                bank = ring_use(i, 0)
                for m in range(2):
                    at = W1_S + C - C * m
                    for w, rows, start, stop in split(slice(at, at + P), parts[:, m, :]):
                        mm = pe.matmul(bank[:, :], w, rows, start=start and m == 0, stop=stop and m == 1)
                mm.then_inc(ring_mm, 1)
                turn_logits(i)
                for k in range(1, 9):
                    m, e = (k - 1) // E, (k - 1) % E
                    bank = ring_use(i, k)
                    for w, rows, start, stop in split(slice(e * P, e * P + P), parts[:, m, :]):
                        mm = pe.matmul(bank[:, :], w, rows, start=start, stop=stop)
                    mm.then_inc(ring_mm, 1)
                    if k == 2 and prev:
                        out_rows(i - 1)
                if nxt:
                    variance(i + 1)
                for k in range(9, K_SHARED):
                    im, q = (k - 9) // 2, (k - 9) % 2
                    bank = ring_use(i, k)
                    for h in range(2):
                        k1 = 1 + E * im + 2 * q + h
                        pe.wait_ge(taken[k1 % RING], USES // RING * i + k1 // RING + 1)
                        mm = pe.matmul(bank[C * h:C * h + C, :], ew2[:, 2 * q + h, :], h1e[:, im, 2 * q + h],
                                       start=True, stop=True)
                    mm.then_inc(ring_mm, 1)
                    if k == 11:
                        turn_routing(i, nxt)
                pe.wait_ge(shared_split, 2 * i + 2)
                for m in range(2):
                    bank = ring_use(i, K_SHARED + m)
                    for w, rows, start, stop in split(slice(W1_S2, W1_S2 + P), parts_s[:, m, :]):
                        mm = pe.matmul(bank[:, :], w, rows, start=start, stop=stop)
                    mm.then_inc(ring_mm, 1)
                if not isinstance(i, int) or i + 2 < ITERS:
                    centre_rows(i + 2)
                pe.wait_ge(routing_low, i + 1)
                for n in range(4):
                    pe.matmul(ring_use(i, K_SPREAD + n)[:, :], w1_high[0:N_ROUTE, W1 + n * P:W1 + (n + 1) * P],
                              route[0:N_ROUTE, :], start=True, stop=True).then_inc(ring_mm, 1)
                bank = ring_use(i, K_SUM)
                for k in (K_SHARED, K_SHARED + 1):
                    pe.wait_ge(taken[k % RING], USES // RING * i + k // RING + 1)
                for im in range(2):
                    pe.matmul(bank[C * im:C * im + C, :], sw3[:, :], h2s[:, im], start=True, stop=False,
                              skip_group_check=True)
                for w in (w1_high, w1_low):
                    pe.matmul(bank[:, :], w[0:N_ROUTE, W1_B:W1_B + P], route[0:N_ROUTE, :], start=False, stop=False,
                              skip_group_check=True)
                for q in range(2):
                    for im in range(2):
                        k = K_SPREAD + 2 * q + im
                        pe.wait_ge(taken[k % RING], USES // RING * i + k // RING + 1)
                        mm = pe.matmul(bank[C * im:C * im + C, :], ew3[:, q, :], h2w[:, im, q], start=False, stop=(q == 1),
                                       skip_group_check=True)
                mm.then_inc(ring_mm, 1)
                if nxt:
                    logits(i + 1, (p + 1) % 2)

            pe.wait_ge(residual_ready, N_RES)
            pe.wait_ge(gelu_ready, 2 * N_PIECE)
            pe.wait_ge(route_cleared, 1)
            pe.wait_ge(weights_split, 1)
            centre_rows(0)
            variance(0)
            logits(0, 0)
            centre_rows(1)
            mixture(pe, mstep)
            out_rows(ITERS - 1)

        @block.vector
        def _(dve):
            n_coefs = [0]

            def link(ins):
                n_coefs[0] += 1
                ins.then_inc(coefs, 1)
                dve.wait_ge(coefs, n_coefs[0])

            dve.wait_ge(tok_in, 16)
            for n, v in ((0, V_LNQW), (1, V_LNKW), (2, V_LNKW)):
                dve.tensor_scalar(scaled[:, n * P:(n + 1) * P], raw[:, n * P:(n + 1) * P], vec(v), None,
                                  ALU.mult).then_inc(weights_scaled, 1)
            def svc(n):
                return sv[:, n:n + 1]

            link(dve.tensor_scalar(svc(SV_A), vec(V_A), DT * DT, None, ALU.mult))
            link(dve.tensor_scalar(svc(SV_S), svc(SV_A), 1.0, None, ALU.add))
            link(dve.reciprocal(svc(SV_S), svc(SV_S)))
            link(dve.scalar_tensor_tensor(svc(SV_NM), svc(SV_A), -1.0, svc(SV_S), ALU.mult, ALU.mult))
            link(dve.tensor_scalar(svc(SV_F), svc(SV_S), DT * DT, None, ALU.mult))
            link(dve.tensor_tensor(svc(SV_FB), svc(SV_F), vec(V_BB), ALU.mult))
            link(dve.tensor_tensor(svc(SV_CD), vec(V_BC), vec(V_BD), ALU.add))
            link(dve.tensor_scalar(svc(SV_NS), svc(SV_S), -1.0, None, ALU.mult))
            link(dve.tensor_scalar(svc(SV_G), svc(SV_S), 1.0, None, ALU.add))
            link(dve.tensor_tensor(svc(SV_G), svc(SV_G), svc(SV_NM), ALU.add))
            for a, n in ((cz, 0), (cz, 1), (cv, 0), (cv, 1)):
                link(dve.memset(a[:, 0, n:n + 1], float((a is cz) == (n == 0))))
            def free_steps(first, last):
                for j in range(first, last):
                    link(dve.tensor_scalar(cacc[:, :], cz[:, j, :], svc(SV_NM), None, ALU.mult))
                    link(dve.scalar_tensor_tensor(cv[:, j + 1, :], cv[:, j, :], svc(SV_S), cacc[:, :], ALU.mult, ALU.add))
                    link(dve.tensor_tensor(cz[:, j + 1, :], cz[:, j, :], cv[:, j + 1, :], ALU.add))

            free_steps(0, 4)
            patch_sums(dve, 0, 0)

            dve.wait_ge(setup_mm, 2)
            dve.tensor_copy(bqkv[:, 1:3], banks[1][:, 1:3]).then_inc(biases_ready, 1)
            dve.tensor_scalar(bqkv[:, 0:1], banks[1][:, 0:1], float(C) ** -0.5, None, ALU.mult).then_inc(biases_ready, 1)
            dve.wait_ge(biases_ready, 2)
            dve.wait_ge(const_in, 16)
            dve.tensor_scalar(indbk[:, :], const[:, K_IND:K_AVG], bqkv[:, 1:2], None, ALU.mult).then_inc(weights_scaled, 1)
            dve.wait_ge(setup_mm, 3)
            dve.tensor_tensor(bqkv[:, 3:4], banks[2][:, 0:1], vec(V_PROJB), ALU.add).then_inc(weights_scaled, 1)

            def query_var(u):
                dve.wait_ge(q_mean_squared, u + 1)
                dve.tensor_tensor(qstat[:, :], bank_sq[:, 2 * PT:4 * PT], qstat[:, :], ALU.subtract).then_inc(q_variance_ready, 1)

            def query_scaled(u):
                dve.wait_ge(q_rstd_ready, u + 1)
                dve.wait_ge(q_raw_mm, u + 1)
                dve.wait_ge(q_ready, u)
                dve.tensor_tensor(qraw[:, :], bank_mu[:, 0:2 * PT], qrstd[:, :], ALU.mult).then_inc(q_scaled, 1)

            def pixel_var(u):
                dve.wait_ge(mean_squared, u + 1)
                dve.wait_ge(pixel_square_mm, u + 1)
                dve.tensor_tensor(vstat[:, :], bank_sq[:, :], vstat[:, :], ALU.subtract).then_inc(variance_ready, 1)

            def key_products(u, m, c):
                b, j = c // NJ, c % NJ
                dve.wait_ge(keys_mm, 8 * u + c + 1)
                if c == 0:
                    dve.wait_ge(q_ready, u + 1)
                if j == 0:
                    dve.wait_ge(scores_mm, count(2 * u - 1 + b))
                shape = "p (h s n) -> p h s n"
                q = qbuf[:, m % 2, b, 32 * j:32 * j + 32, :].rearrange("p (h w) t -> p h (w t)", h=2)
                dve.tensor_tensor(prodk[:, b, j * CH:(j + 1) * CH].rearrange(shape, h=2, s=S),
                                  ring[(RING_K + c) % 3][:, :].rearrange(shape, h=2, s=S),
                                  q[:, :, None, :].to_broadcast([P, 2, S, W]),
                                  ALU.mult).then_inc(keys_times_q, 1)

            def score_scale(u):
                dve.wait_ge(scores_mm, 2 * u + 2)
                dve.wait_ge(rstd_ready, u + 1)
                dve.wait_ge(weights_raw, u)
                dve.tensor_tensor(score[:, :], bank_s[:, :], rstd[:, :], ALU.mult).then_inc(scores_scaled, 1)

            def by_patch(a):
                return a[:, :].rearrange("p (h s w t) -> p h w s t", h=2, s=S, w=16)

            def score_max(u):
                dve.wait_ge(scores_biased, u + 1)
                dve.tensor_reduce(smx[:, :].rearrange("p (h w) -> p h w", h=2), by_patch(score), AX.XY,
                                  ALU.max).then_inc(score_max_ready, 1)
                dve.wait_ge(score_max_ready, u + 1)
                dve.tensor_copy(smxs[:, :].rearrange("p (n t) -> p n t", t=S),
                                smx[:, :, None].to_broadcast([P, 32, S])).then_inc(score_max_spread, 1)

            def score_sum(u):
                dve.wait_ge(scores_exp, u + 1)
                dve.tensor_reduce(ssm[:, :].rearrange("p (h w) -> p h w", h=2), by_patch(score), AX.XY,
                                  ALU.add).then_inc(exp_summed, 1)

            def score_inverse(u):
                dve.wait_ge(exp_summed, u + 1)
                dve.wait_ge(weights_ready, u)
                dve.reciprocal(smx[:, :], ssm[:, :]).then_inc(sum_inverted, 1)
                dve.wait_ge(sum_inverted, u + 1)
                dve.tensor_copy(srz[:, :].rearrange("p (n t) -> p n t", t=S),
                                smx[:, :, None].to_broadcast([P, 32, S])).then_inc(inverse_sum_ready, 1)

            def value_products(u, m, c):
                b, j = c // NJ, c % NJ
                dve.wait_ge(values_mm, 8 * u + c + 1)
                if c == 0:
                    dve.wait_ge(weights_copied, u + 1)
                if j == 0:
                    dve.wait_ge(aggregate_mm, count(2 * u - 1 + b))
                k = wT[:, m % 2, :].rearrange("p (r k) -> p r k", r=4)[:, :, 32 * j + 16 * b:32 * j + 16 * b + 16]
                shape = "p (r k d) -> p r k d"
                dve.tensor_tensor(prodv[:, c, :].rearrange(shape, r=4, d=D),
                                  ring[(RING_V + c) % 3][:, :].rearrange(shape, r=4, d=D),
                                  k[:, :, :, None].to_broadcast([P, 4, 16, D]), ALU.mult).then_inc(values_weighted, 1)

            def tokens(u, m):
                dve.wait_ge(projected_mm, u + 1)
                half = m % 2
                pairs = hT[:, :].rearrange("p (g b n) -> p g b n", b=2, n=HW)
                dst = pairs[:, (u - half) // 2, :, half * PT:(half + 1) * PT]
                dve.scalar_tensor_tensor(dst, ring[RING_P % 3][:, 0:2 * PT].rearrange("p (b n) -> p b n", b=2),
                                         bqkv[:, 3:4], means[:, m, 0, :].rearrange("p (b n) -> p b n", b=2),
                                         ALU.add, ALU.add).then_inc(tokens_ready, 1)

            def scan_first(h):
                dve.wait_ge(force_ready, N_PIECE * h + 1)
                dve.tensor_copy(z[:, at(h, 0)], force[:, at(h, 0)]).then_inc(scan_step[h], 1)

            def scan_ahead(h, j):
                dve.wait_ge(scan_step[h], 2 * j - 1)
                if j + 1 < L:
                    dve.wait_ge(force_ready, N_PIECE * h + (j + 1) // 2 + 1)
                    dve.scalar_tensor_tensor(force[:, at(h, j + 1)], z[:, at(h, j - 1)], sv[:, SV_NS:SV_NS + 1],
                                             force[:, at(h, j + 1)], ALU.mult, ALU.add).then_inc(scan_step[h], 1)

            def scan_on(h, j):
                dve.wait_ge(scan_step[h], 2 * j - 1)
                dve.scalar_tensor_tensor(z[:, at(h, j)], z[:, at(h, j - 1)], sv[:, SV_G:SV_G + 1], force[:, at(h, j)],
                                         ALU.mult, ALU.add).then_inc(scan_step[h], 1)

            def seqs(a, h):
                return a[:, h * HS:(h + 1) * HS]

            def start(a, c):
                return a.rearrange("p (n c) -> p n c", c=NCK)[:, :, c]

            def scan_last(h):
                dve.wait_ge(scan_step[h], 2 * L - 2)
                dve.tensor_tensor(seqs(vel, h), z[:, at(h, L - 1)], z[:, at(h, L - 2)],
                                  ALU.subtract).then_inc(scan_step[h], 1)
                dve.memset(start(seqs(zin, h), 0), 0.0).then_inc(carry_step[h], 1)
                dve.memset(start(seqs(vin, h), 0), 0.0).then_inc(carry_step[h], 1)

            def tmp(h, o):
                return ctmp[:, (2 * h + o) * (PAIRS // 2):(2 * h + o + 1) * (PAIRS // 2)]

            def carry_from(h, c):
                dve.wait_ge(scan_step[h], 2 * L - 1)
                dve.wait_ge(carry_step[h], 4 * c + 2)
                for o, (coef, loc) in enumerate(((cz, z[:, at(h, L - 1)]), (cv, seqs(vel, h)))):
                    dve.scalar_tensor_tensor(tmp(h, o), start(seqs(zin, h), c), coef[:, L, 0:1], start(loc, c),
                                             ALU.mult, ALU.add).then_inc(carry_step[h], 1)

            def carry_to(h, c):
                for o, (coef, dst) in enumerate(((cz, zin), (cv, vin))):
                    dve.wait_ge(carry_step[h], 4 * c + 4)
                    dve.scalar_tensor_tensor(start(seqs(dst, h), c + 1), start(seqs(vin, h), c), coef[:, L, 1:2], tmp(h, o),
                                             ALU.mult, ALU.add).then_inc(carry_step[h], 1)

            EARLY, BEFORE_TOKENS = 6, 12

            query_var(0)
            query_scaled(0)
            free_steps(4, 13)
            pixel_var(0)
            for c in range(8):
                key_products(0, 0, c)
            score_scale(0)
            query_var(1)
            score_max(0)
            query_scaled(1)
            free_steps(13, L)
            assert n_coefs[0] == N_COEFS
            score_sum(0)
            score_inverse(0)
            def step(n, m):
                nxt = not isinstance(n, int) or n + 1 < UNITS
                nxt2 = not isinstance(n, int) or n + 2 < UNITS
                m1 = (m + 1) % NF
                if nxt:
                    pixel_var(n + 1)
                if nxt:
                    for c in range(8):
                        key_products(n + 1, m1, c)
                if not nxt:
                    scan_first(0)
                    for j in range(1, EARLY):
                        scan_ahead(0, j)
                        scan_on(0, j)
                if not isinstance(n, int) or n >= 1:
                    tokens(n - 1, (m - 1) % NF)
                for c in range(8):
                    value_products(n, m, c)
                    if c == 1 and nxt:
                        score_scale(n + 1)
                    if c == 1 and nxt2:
                        query_var(n + 2)
                    if c == 3 and nxt2:
                        query_scaled(n + 2)
                    if c == 4 and nxt:
                        score_max(n + 1)
                if nxt:
                    score_sum(n + 1)
                    score_inverse(n + 1)
                else:
                    for j in range(EARLY, BEFORE_TOKENS):
                        scan_ahead(0, j)
                        scan_on(0, j)

            pipeline(dve, step, UNITS)
            tokens(UNITS - 1, (UNITS - 1) % NF)

            def fix_z(h, j):
                dve.wait_ge(carry_step[h], 4 * NCK - 2)
                dve.scalar_tensor_tensor(z[:, at(h, j)], seqs(zin, h), cz[:, j + 1, 0:1], z[:, at(h, j)],
                                         ALU.mult, ALU.add).then_inc(chunk_fixed[h], 1)

            def fix_v(h, j):
                dve.wait_ge(chunk_fixed[h], max(2 * j, 1))
                dve.scalar_tensor_tensor(z[:, at(h, j)], seqs(vin, h), cz[:, j + 1, 1:2], z[:, at(h, j)],
                                         ALU.mult, ALU.add).then_inc(chunk_fixed[h], 1)

            def residual(h):
                for n in range(N_RES):
                    dve.wait_ge(silu_ready, N_RES * h + n + 1)
                    dst = tokens_at(h, n, L // N_RES)
                    out = force[:, piece(h, n, HP // N_RES)].rearrange("p (j n) -> p j n", n=HS)
                    dve.scalar_tensor_tensor(dst, dst, 2.0, out, ALU.mult, ALU.add).then_inc(residual_ready, 1)

            for j in range(BEFORE_TOKENS, L):
                scan_ahead(0, j)
                scan_on(0, j)
            scan_last(0)
            scan_first(1)
            for j in range(1, L):
                carry_from(0, j - 1)
                scan_ahead(1, j)
                carry_to(0, j - 1)
                scan_on(1, j)
            scan_last(1)
            for j in range(L):
                if j < NCK - 1:
                    carry_from(1, j)
                fix_z(0, j)
                if j < NCK - 1:
                    carry_to(1, j)
            for j in range(L):
                fix_z(1, j)
                if j > 0:
                    fix_v(1, j - 1)
            fix_v(1, L - 1)
            residual(0)
            residual(1)

            def normed(i, p):
                dve.wait_ge(norm_rstd_ready, i + 1)
                dve.wait_ge(low_ready, count(2 * i - 2))
                dve.wait_ge(taken[K_SUM % RING], count(USES // RING * (i - 1)))
                dve.tensor_tensor(h2[:, p, :], bank_cen[:, :], ln3, ALU.mult).then_inc(normed_ready, 1)

            def by_row(a):
                return a.rearrange("p (n e) -> p n e", e=E)

            def spread(a):
                return a[:, :, None].to_broadcast([P, 8, E])

            def routing(i):
                mx = l8[:, 0, :]
                dve.wait_ge(logits_turned, i + 1)
                turned = bank_var[:, P:2 * P].rearrange("p (g t m e) -> p g t m e", g=G, t=4, m=2)[:, :, 0]
                dve.tensor_tensor(lg.rearrange("p (g m e) -> p g m e", g=G, m=2), turned,
                                  gbias[:, None, None, :].to_broadcast([P, G, 2, E]), ALU.add).then_inc(logits_biased, 1)
                dve.wait_ge(logits_biased, i + 1)
                dve.tensor_reduce(mx, by_row(lg), AX.X, ALU.max).then_inc(logits_max, 1)
                dve.wait_ge(logits_max, i + 1)
                dve.tensor_tensor(by_row(lgx), by_row(lg), spread(mx), ALU.subtract).then_inc(logits_shifted, 1)

            def gates(i):
                mx, sm, rc, m1 = (l8[:, n, :] for n in range(4))
                dve.wait_ge(logits_exp, i + 1)
                dve.tensor_reduce(sm, by_row(lgx), AX.X, ALU.add).then_inc(logits_sum, 1)
                dve.wait_ge(logits_sum, i + 1)
                dve.reciprocal(rc, sm).then_inc(logits_inverse, 1)
                dve.wait_ge(logits_inverse, i + 1)
                dve.tensor_tensor(by_row(gat), by_row(lgx), spread(rc), ALU.mult).then_inc(gates_ready, 1)
                dve.wait_ge(gates_ready, i + 1)
                dve.tensor_reduce(m1, by_row(gat), AX.X, ALU.max).then_inc(gate_max, 1)
                dve.wait_ge(gate_max, i + 1)
                dve.tensor_tensor(by_row(pick), by_row(gat), spread(m1), ALU.subtract).then_inc(gates_shifted, 1)
                own = by_row(gat)[:, :, :, None].to_broadcast([P, 8, E, E])
                other = by_row(gat)[:, :, None, :].to_broadcast([P, 8, E, E])
                square = "p (n e f) -> p n e f"
                up = const[:, K_UP:K_EPS].rearrange("p (e f) -> p e f", f=E)[:, None, :, :].to_broadcast([P, 8, E, E])
                bt, ti = beat.rearrange(square, e=E, f=E), tie.rearrange(square, e=E, f=E)
                dve.tensor_tensor(bt, other, own, ALU.is_ge).then_inc(gates_compared, 1)
                dve.tensor_tensor(ti, other, own, ALU.is_equal).then_inc(ties_found, 1)
                dve.wait_ge(ties_found, i + 1)
                dve.tensor_tensor(ti, ti, up, ALU.mult).then_inc(ties_counted, 1)
                dve.wait_ge(ties_counted, i + 1)
                dve.tensor_tensor(beat, beat, tie, ALU.subtract).then_inc(wins_ready, 1)
                dve.wait_ge(wins_ready, i + 1)
                dve.tensor_reduce(by_row(lg), bt, AX.X, ALU.add).then_inc(rank_ready, 1)

            def chosen(i):
                tot, inv = l8[:, 4, :], l8[:, 5, :]
                dve.wait_ge(rank_ready, i + 1)
                dve.wait_ge(gates_exp, i + 1)
                dve.scalar_tensor_tensor(pick, lg, 1.5, pick, ALU.is_lt, ALU.mult).then_inc(picked, 1)
                dve.wait_ge(picked, i + 1)
                dve.tensor_reduce(tot, by_row(pick), AX.X, ALU.add).then_inc(picked_sum, 1)
                dve.wait_ge(picked_sum, i + 1)
                dve.reciprocal(inv, tot).then_inc(picked_inverse, 1)
                dve.wait_ge(picked_inverse, i + 1)
                dve.tensor_tensor(by_row(wmoe), by_row(pick), spread(inv), ALU.mult).then_inc(routing_ready, 1)

            def route_low(i):
                dve.wait_ge(routing_high, i + 1)
                high = route[0:2 * E, :].bitcast(F32)
                dve.tensor_tensor(in_order(route[LOW:LOW + 2 * E, :]), by_group(bank_var[0:2 * E, :]), in_order(high),
                                  ALU.subtract).then_inc(routing_low, 1)

            def weigh(i, n):
                k = K_SPREAD + n
                dve.wait_ge(ring_mm, USES * i + k + 1)
                q, m = n // 2, n % 2
                kr = 9 + 2 * m + q
                dve.wait_ge(taken[kr % RING], USES // RING * i + kr // RING + 1)
                dve.tensor_tensor(h2w[:, m, q], mix_ring[k % RING][:, :], h2e[:, m, q],
                                  ALU.mult).then_inc(taken[k % RING], 1)

            def total(i, p):
                dve.wait_ge(ring_mm, USES * i + K_SUM + 1)
                dve.wait_ge(out_rows_mm, i)
                dve.scalar_tensor_tensor(ysum, mix_ring[K_SUM % RING][:, :], ebias[:, 8:9], h2[:, p, :],
                                         ALU.add, ALU.add).then_inc(taken[K_SUM % RING], 1)

            def rows(a):
                return a.rearrange("p (n c) -> p n c", c=C)

            def square_sum(i):
                dve.wait_ge(out_squared, i + 1)
                dve.wait_ge(out_rstd_ready, i)
                dve.tensor_reduce(y8[:, 0, :], rows(ysq), AX.X, ALU.add).then_inc(out_square_sum, 1)

            def finish(i, p):
                dve.wait_ge(out_rstd_ready, i + 1)
                dve.wait_ge(stored[p], count((i - p) * (STORE // 2)))
                dve.tensor_tensor(out_t[:, p].rearrange("p a (n c) -> p (a n) c", c=C), rows(bank_base[:, :]),
                                  y8[:, 1, :][:, :, None].to_broadcast([P, 8, C]),
                                  ALU.mult).then_inc(out_ready, 1)

            normed(0, 0)
            low(dve, 0, 0, 0)

            def mstep(i, p):
                prev = not isinstance(i, int) or i >= 1
                routing(i)
                relu(dve, i, 2)
                gates(i)
                relu(dve, i, 7)
                chosen(i)
                if prev:
                    square_sum(i - 1)
                if not isinstance(i, int) or i + 1 < ITERS:
                    normed(i + 1, (p + 1) % 2)
                relu(dve, i, 12)
                route_low(i)
                if prev:
                    finish(i - 1, (p + 1) % 2)
                for n in range(4):
                    weigh(i, n)
                total(i, p)

            mixture(dve, mstep)
            square_sum(ITERS - 1)
            finish(ITERS - 1, (ITERS - 1) % 2)


_OUT = (B, HW, C)


def _blocks(out, cols, w):
    out[0:C, cols:cols + C] = w
    out[C:P, cols + C:cols + 2 * C] = w


def _tokenizer_pack(a):
    out = np.zeros((P, T_END), np.float32)
    wkv = a["L0_tok_Wkv"]
    for n, w in enumerate((a["L0_tok_Wq"], wkv[0:C], wkv[C:2 * C], a["L0_tok_proj_w"])):
        _blocks(out, T_RAW + n * P, w.T)
    for n, name in enumerate(("tok_ln_q_w", "tok_ln_q_b", "tok_ln_kv_w", "tok_ln_kv_b", "tok_proj_b",
                              "attn_a", "attn_b_B", "attn_b_C", "attn_b_D")):
        for i in range(2):
            out[C * i:C * i + C, T_VEC + n] = a["L0_" + name]
    return out


def _rest_pack(a):
    out = np.zeros((P, R_END), np.float32)
    for n, name in enumerate("BCD"):
        _blocks(out, R_SSM + n * P, a["L0_attn_W_" + name].T)
    out[:, R_SW3:R_EW2] = a["L0_ffn_sW3"]
    for i in range(2):
        r = slice(C * i, C * i + C)
        out[r, R_SW2:R_SW2 + P] = a["L0_ffn_sW2"]
        out[r, R_GW + E * i:R_GW + E * i + E] = a["L0_ffn_gW"]
        out[r, R_SW1 + C:R_SW1 + 2 * C] = a["L0_ffn_sW1"]
        out[r, R_EB + 6] = a["L0_ffn_sb1"]
        for e in range(E):
            at = R_EW1 + e * P
            out[r, at:at + P] = a["L0_ffn_eW1"][e]
        for q in range(2):
            out[r, R_EW3 + q * C:R_EW3 + (q + 1) * C] = a["L0_ffn_eW3"][2 * q + i]
            out[r, R_EB + 4 + q] = a["L0_ffn_eb2"][2 * q + i]
        for at in (0, LOW):
            out[at + E * i:at + E * i + E, R_B3 + C * i:R_B3 + C * i + C] = a["L0_ffn_eb3"]
        out[r, R_EB + 8] = a["L0_ffn_sb3"]
    for e in range(E):
        out[:, R_EW2 + e * C:R_EW2 + (e + 1) * C] = a["L0_ffn_eW2"][e]
        out[:, R_EB + e] = a["L0_ffn_eb1"][e]
    out[:, R_GB:R_EB] = a["L0_ffn_gb"]
    out[:, R_EB + 7] = a["L0_ffn_sb2"]
    return out


def kernel(**inputs):
    import concourse.bacc as _bacc
    from concourse.bass_utils import run_bass_kernel_spmd as _run

    a = {n: np.asarray(v) for n, v in inputs.items()}
    arrays = {
        "x": np.ascontiguousarray(a["x"]).reshape(PAIRS, P, H * W),
        "tok_w": _tokenizer_pack(a),
        "rest_w": _rest_pack(a),
        "const": shape_constants(),
    }
    nc = _bacc.Bacc("TRN2", target_bir_lowering=False, num_devices=1)
    t = {n: nc.dram_tensor(n, v.shape, F32, kind="ExternalInput").ap() for n, v in arrays.items()}
    t["out"] = nc.dram_tensor("out", (PAIRS, 2, HW, C), F32, kind="ExternalOutput").ap()
    build(nc, t)
    r = _run(nc, [arrays], core_ids=[0])
    return np.asarray(r.results[0]["out"]).reshape(_OUT)
```
